# Optimizing a Trainium2 kernel written in Bass

```python
import numpy as np
import jax
import jax.numpy as jnp

def _softmax(x, axis=-1):
    return jax.nn.softmax(x, axis=axis)

def _gelu(x):
    return jax.nn.gelu(x, approximate=True)

def _silu(x):
    return jax.nn.silu(x)

def _sigmoid(x):
    return jax.nn.sigmoid(x)

def _layernorm(x, axis=-1, eps=1e-05):
    m = jnp.mean(x, axis=axis, keepdims=True)
    v = jnp.var(x, axis=axis, keepdims=True)
    return (x - m) / jnp.sqrt(v + eps)

def _scatter_add(tgt, idx, src, axis=0):
    return tgt.at[idx].add(src)

def _segment_sum(src, seg, n):
    return jax.ops.segment_sum(src, seg, n)
kernel_name = 'mk_gnn_resnorm_d2_gnn_r8_48a194'

def setup_inputs(seed: int=0):
    np.random.seed(seed)
    _w = jnp.asarray

    def _rec_inputs():
        import jax
        import jax.numpy as jnp
        _gk = jax.random.key(seed)
        x = -0.000202 + 1 * jax.random.normal(jax.random.fold_in(_gk, 1), (6250, 128), jnp.float32)
        src = jax.random.randint(jax.random.fold_in(_gk, 2), (200000,), 0, 6250, jnp.int32)
        dst = jax.random.randint(jax.random.fold_in(_gk, 3), (200000,), 0, 6250, jnp.int32)
        _o = jnp.argsort(dst, stable=True)
        src = src[_o]
        dst = dst[_o]
        edge_attr_128 = 0.000133148 + 1.00009 * jax.random.normal(jax.random.fold_in(_gk, 12), (200000, 128), jnp.float32)
        return (x, src, dst, edge_attr_128)
    x, src, dst, edge_attr_128 = _rec_inputs()

    def _L0_gnn_setup():
        import jax, jax.numpy as jnp
        import numpy as np
        N_NODES = 6250
        N_EDGES = 100000
        D_FEAT = 128
        EMBED = 128
        key = jax.random.key(seed)
        ks = jax.random.split(key, 6)
        node_features = jax.random.normal(ks[0], (N_NODES, D_FEAT), dtype=jnp.float32)
        senders = jax.random.randint(ks[1], (N_EDGES,), 0, N_NODES, dtype=jnp.int32)
        receivers = jax.random.randint(ks[2], (N_EDGES,), 0, N_NODES, dtype=jnp.int32)
        edge_features = jax.random.normal(ks[3], (N_EDGES, D_FEAT), dtype=jnp.float32)
        W = jax.random.normal(ks[4], (D_FEAT, 2 * EMBED), dtype=jnp.float32) * (2.0 / (D_FEAT + 2 * EMBED)) ** 0.5
        W_e = jax.random.normal(ks[5], (D_FEAT, EMBED), dtype=jnp.float32) * (2.0 / (D_FEAT + EMBED)) ** 0.5
        b_W = jnp.zeros((2 * EMBED,), dtype=jnp.float32)
        b_We = jnp.zeros((EMBED,), dtype=jnp.float32)
        return dict(node_features=node_features, senders=senders, receivers=receivers, edge_features=edge_features, W=W, b_W=b_W, W_e=W_e, b_We=b_We)
    _L0_gnn_all = _L0_gnn_setup()
    _L0_gnn_in = {k: v for k, v in _L0_gnn_all.items() if k in ('W', 'b_W', 'W_e', 'b_We')}
    del _L0_gnn_all

    def _L1_gnn_setup():
        import jax, jax.numpy as jnp
        import numpy as np
        ALPHA = 0.01
        BN_EPS = 1e-05
        key = jax.random.key(seed)
        k1, k2, k3, k4 = jax.random.split(key, 4)
        N, E, F_in, F_out = (25000, 62500, 128, 128)
        x = jax.random.normal(k1, (N, F_in), dtype=jnp.float32)
        edge_idx = jax.random.randint(k2, (2, E), 0, N, dtype=jnp.int64)
        W = jax.random.normal(k3, (F_in, F_out), dtype=jnp.float32) / np.sqrt(F_in)
        b = jnp.zeros((F_out,), dtype=jnp.float32)
        gamma = jnp.ones((F_out,), dtype=jnp.float32)
        beta = jnp.zeros((F_out,), dtype=jnp.float32)
        return {'x': x, 'edge_idx': edge_idx, 'W': W, 'b': b, 'gamma': gamma, 'beta': beta}
    _L1_gnn_all = _L1_gnn_setup()
    _L1_gnn_in = {k: v for k, v in _L1_gnn_all.items() if k in ('W', 'b', 'gamma', 'beta')}
    del _L1_gnn_all
    return {'x': x, 'src': src, 'dst': dst, 'edge_attr_128': edge_attr_128, 'L0_gnn_W': _L0_gnn_in['W'], 'L0_gnn_b_W': _L0_gnn_in['b_W'], 'L0_gnn_W_e': _L0_gnn_in['W_e'], 'L0_gnn_b_We': _L0_gnn_in['b_We'], 'L1_gnn_W': _L1_gnn_in['W'], 'L1_gnn_b': _L1_gnn_in['b'], 'L1_gnn_gamma': _L1_gnn_in['gamma'], 'L1_gnn_beta': _L1_gnn_in['beta']}

def reference(x, src, dst, edge_attr_128, L0_gnn_W, L0_gnn_b_W, L0_gnn_W_e, L0_gnn_b_We, L1_gnn_W, L1_gnn_b, L1_gnn_gamma, L1_gnn_beta):
    import jax
    import jax.numpy as jnp

    def _L0_gnn_ref(node_features, senders, receivers, edge_features, W, b_W, W_e, b_We):
        import jax, jax.numpy as jnp
        import numpy as np
        N_NODES = 6250
        N_EDGES = 100000
        D_FEAT = 128
        EMBED = 128
        num_nodes = node_features.shape[-2]
        h = node_features @ W + b_W
        xi, xj = jnp.split(h, 2, axis=-1)
        xji = xj[senders]
        xji = xji + (edge_features @ W_e + b_We)
        in_degree = jax.ops.segment_sum(jnp.ones_like(receivers, dtype=xji.dtype), receivers, num_segments=num_nodes)
        xji = xji / (in_degree[receivers][..., None] + 1e-06)
        nodes = xi + jax.ops.segment_sum(xji, receivers, num_segments=num_nodes)
        return nodes

    def _L1_gnn_ref(x, edge_idx, W, b, gamma, beta):
        import jax, jax.numpy as jnp
        import numpy as np
        ALPHA = 0.01
        BN_EPS = 1e-05
        N = x.shape[0]
        h = x @ W
        self_loops = jnp.arange(N, dtype=edge_idx.dtype)
        src = jnp.concatenate([edge_idx[0], self_loops])
        dst = jnpp = jnp.concatenate([edge_idx[1], self_loops])
        ones = jnp.ones(src.shape[0], dtype=h.dtype)
        deg = jax.ops.segment_sum(ones, dst, num_segments=N)
        dinv = jnp.where(deg > 0, jax.lax.rsqrt(deg), 0.0)
        norm = dinv[src] * dinv[dst]
        out = jax.ops.segment_sum(h[src] * norm[:, None], dst, num_segments=N) + b
        mean = out.mean(axis=0)
        var = out.var(axis=0)
        y = (out - mean) * jax.lax.rsqrt(var + BN_EPS) * gamma + beta
        return jnp.where(y >= 0, y, ALPHA * y)
    edge_index = jnp.stack([src, dst])
    x = _layernorm(x + _L0_gnn_ref(x, src, dst, edge_attr_128, L0_gnn_W, L0_gnn_b_W, L0_gnn_W_e, L0_gnn_b_We), axis=-1)
    x = _layernorm(x + _L1_gnn_ref(x, edge_index, L1_gnn_W, L1_gnn_b, L1_gnn_gamma, L1_gnn_beta), axis=-1)
    return x

_drawn_inputs = setup_inputs


def setup_inputs(seed=0):
    import zlib

    import numpy as np

    out = dict(_drawn_inputs(seed))
    spreads = {'L0_gnn_b_W': (0.0, 0.1),
     'L0_gnn_b_We': (0.0, 0.1),
     'L1_gnn_b': (0.0, 0.1),
     'L1_gnn_gamma': (1.0, 0.2),
     'L1_gnn_beta': (0.0, 0.1)}
    factors = {}
    for name, (base, spread) in spreads.items():
        noise = np.random.default_rng([zlib.crc32(name.encode()), seed]).standard_normal(out[name].shape)
        drawn = base * np.exp(spread * noise) if base else spread * noise
        out[name] = jnp.asarray(drawn.astype(out[name].dtype))
    for name, factor in factors.items():
        out[name] = (out[name] * factor).astype(out[name].dtype)
    return out
```

```python
import concourse.bass as bass
from concourse import mybir
from contextlib import ExitStack

F32 = mybir.dt.float32
BF16 = mybir.dt.bfloat16
I32 = mybir.dt.int32
ALU = mybir.AluOpType
ACT = mybir.ActivationFunctionType
AX = mybir.AxisListType

P = 128
F = 128
WN = 5
TILES = 2
WE = TILES * P
BN = 250
BW = BN // WN
PAIRS = BW // 2
GW = 125
EW = 63
EK = 4
EJ = 18
EE = EJ * P
RING = 5
HR = 500
GE = 125
GN = 512


class Dims:
    def __init__(self, n, e):
        self.N, self.E = n, e
        self.HI = -(-n // P)
        self.NP = self.HI * P
        self.REM = n - (self.HI - 1) * P
        self.NB = n // BN
        self.NW = n // WN
        self.G = self.NW // GW
        self.R = e // HR
        self.CH = max(c for c in range(1, 8) if self.HI % c == 0)
        self.NC = self.HI // self.CH
        assert n % BN == 0 and self.NW % GW == 0 and e % HR == 0 and e % GE == 0
        assert self.NB % 2 == 1 and self.NB * EK <= P and self.R <= 512 and WN * self.HI * 2 <= 512


class Steps:

    def __init__(self, engine, sem):
        self.engine, self.sem, self.n = engine, sem, 0

    def __call__(self, ins):
        self.n += 1
        ins.then_inc(self.sem, 1)
        self.engine.wait_ge(self.sem, self.n)


def reach(engine, sem, value):
    if not isinstance(value, int) or value > 0:
        engine.wait_ge(sem, value)


def wait_alone(engine, sem, value, passed):
    if not isinstance(value, int) or value > 0:
        engine.wait_ge(sem, value)
        engine.sem_inc(passed, 1)


def all_blocks(engine, nb, step):
    step(0, 0, -1)
    step(1, 1, 0)
    step(2, 0, 0)
    if nb > 3:
        with engine.Fori(1, (nb - 1) // 2) as i:
            step(i * 2 + 1, 1, i)
            step(i * 2 + 2, 0, i)


def all_turns(engine, n, step):
    step(0)
    if n > 1:
        with engine.Fori(1, n) as i:
            step(i)


def prepare(nc, d, x, src, dst, keep, scratch):
    xrows, xsplit, ident, flag, iota, key_t, lo_t, ekey_t, startrow, iota_e = (
        keep[k] for k in ("xrows", "xsplit", "ident", "flag", "iota", "key_t", "lo_t", "ekey_t",
                          "startrow", "iota_e"))
    N, E, HI, G, R, NB = d.N, d.E, d.HI, d.G, d.R, d.NB
    NE = NB * EK
    with ExitStack() as ctx:
        sb = lambda name, shape, dt: ctx.enter_context(nc.sbuf_tensor(name, shape, dt))
        sem = lambda name: ctx.enter_context(nc.semaphore(name))
        heads_i, heads = sb("heads_i", [1, R], I32), sb("heads", [1, R], F32)
        ones = sb("ones", [P, P], F32)
        iota_i, iota_ei = sb("iota_i", [P, 256], I32), sb("iota_ei", [P, EW], I32)
        th_i, th = sb("th_i", [P, G + 1], I32), sb("th", [P, G + 1], F32)
        e_b, e_k, e_w = sb("e_b", [P, 1], I32), sb("e_k", [P, 1], I32), sb("e_w", [P, 1], F32)
        cnt1, cnt2 = sb("cnt1", [P, G + 1], F32), sb("cnt2", [P, G + 1], F32)
        row_f, row_i = sb("row_f", [P, G + 1], F32), sb("row_i", [P, G + 1], I32)
        start_i = sb("start_i", [P, G + 1], I32)
        rows = sb("rows", [P, G + 1, HR], I32)
        junk = sb("junk", [P, max(G * WE, EE)], F32)
        gdst, gsrc = sb("gdst", [P, G, WE], I32), sb("gsrc", [P, G, WE], I32)
        edst = sb("edst", [P, EE], I32)
        edl = edst[:, :].bitcast(F32)
        dl, key = sb("dl", [P, G, WE], F32), sb("key", [P, G, WE], F32)
        spare = rows[:, :, :].rearrange("p g e -> p (g e)")
        hi_i, lo_i = (spare[:, k * G * WE:(k + 1) * G * WE].rearrange("p (g e) -> p g e", g=G) for k in range(2))
        lo = gdst[:, :, :].bitcast(F32)
        deg = sb("deg", [P, G, WN], F32)
        below, total = sb("below", [P, 2], F32), sb("total", [P, 2], F32)
        ok, ok1 = sb("ok", [1, 2], F32), sb("ok1", [1, 1], F32)
        zpad = sb("zpad", [1, P], F32)
        part = sb("part", [P, HI, F], F32)
        heads_ps = ctx.enter_context(nc.psum_tensor("heads_ps", [P, 512], F32))
        total_ps = ctx.enter_context(nc.psum_tensor("total_ps", [P, 2], F32))
        tps = [ctx.enter_context(nc.psum_tensor(f"tps{i}", [P, 4, P], F32)) for i in range(4)]

        heads_in, x_cleared, x_in = sem("heads_in"), sem("x_cleared"), sem("x_in")
        consts, vstep, pstep = sem("consts"), sem("prep_vector_step"), sem("prep_pool_step")
        heads_f, heads_out = sem("heads_float"), sem("heads_broadcast")
        rows_known, starts_known = sem("rows_known"), sem("starts_known")
        row_in = [sem(f"row_in{g}") for g in range(G + 1)]
        dst_in, src_in, edst_in = sem("window_dst_in"), sem("window_src_in"), sem("edge_window_dst_in")
        keys_ready, lo_ready, ekeys_ready = sem("keys_ready"), sem("lo_ready"), sem("edge_keys_ready")
        lo_int = sem("lo_int")
        turned, tabled = sem("transposed"), sem("tabled")
        deg_ready, totals_ready, totals_out = sem("deg_ready"), sem("totals_ready"), sem("totals_out")
        start_out, start_back, deg_out = sem("start_out"), sem("start_back"), sem("deg_out")
        hi_cast, mid_cast, rest1 = sem("x_hi"), sem("x_mid"), sem("x_rest")
        block = ctx.enter_context(nc.Block())
        EBANKS = -(-EJ // 4)

        @block.sync
        def _(sp):
            sp.dma_start(heads_i[:, :], dst.rearrange("(r c) -> c r", c=HR)[0:1, :],
                         allow_slow_non_contiguous=True).then_inc(heads_in, 16)
            sp.dma_start(xrows[:, 0:HI - 1, :],
                         x[0:(HI - 1) * P, :].rearrange("(h p) f -> p h f", p=P)).then_inc(x_in, 16)
            sp.wait_ge(x_cleared, 1)
            sp.dma_start(xrows[0:d.REM, HI - 1, :], x[(HI - 1) * P:N, :]).then_inc(x_in, 16)
            sp.wait_ge(starts_known, 1)
            sp.dma_start(scratch["starts"], start_i[0:NE, G:G + 1]).then_inc(start_out, 16)
            sp.wait_ge(start_out, 16)
            sp.dma_start(startrow[:, :], scratch["starts"].rearrange("n o -> o n")).then_inc(start_back, 16)
            sp.wait_ge(deg_ready, 1)
            sp.dma_start(scratch["deg"][0:N].rearrange("(g p k) -> p g k", p=GW, k=WN),
                         deg[0:GW, :, :]).then_inc(deg_out, 16)
            sp.dma_start(scratch["deg"][N:d.NP].rearrange("(o n) -> o n", o=1),
                         zpad[:, 0:d.NP - N]).then_inc(deg_out, 16)
            sp.wait_ge(start_back, 16)
            sp.wait_ge(deg_out, 32)

        @block.gpsimd
        def _(pool):
            step = Steps(pool, pstep)
            nc.gpsimd.memset(xrows[:, HI - 1, :], 0.0).then_inc(x_cleared, 1)
            step(nc.gpsimd.memset(ident[:, :], 0.0))
            nc.gpsimd.affine_select(out=ident[:, :], in_=ident[:, :], compare_op=ALU.not_equal, fill=1.0,
                                    base=0, pattern=[[-1, P]], channel_multiplier=1).then_inc(consts, 1)
            nc.gpsimd.memset(ones[:, :], 1.0).then_inc(consts, 1)
            nc.gpsimd.iota(th_i[:, 0:G], pattern=[[WN * GW, G]], base=0, channel_multiplier=WN).then_inc(consts, 1)
            nc.gpsimd.iota(th_i[:, G:G + 1], pattern=[[0, 1]], base=0, channel_multiplier=1).then_inc(consts, 1)
            nc.gpsimd.iota(iota_i[:, :], pattern=[[1, 256]], base=0, channel_multiplier=0).then_inc(consts, 1)
            nc.gpsimd.iota(iota_ei[:, :], pattern=[[1, EW]], base=0, channel_multiplier=0).then_inc(consts, 1)
            nc.gpsimd.memset(zpad[:, :], 0.0).then_inc(consts, 1)
            pool.wait_ge(rows_known, 1)
            flat_dst, flat_src = dst.rearrange("(n o) -> n o", o=1), src.rearrange("(n o) -> n o", o=1)

            def gather(out, table, at, done):
                nc.gpsimd.indirect_dma_start(
                    out=out, out_offset=None, in_=table,
                    in_offset=bass.IndirectOffsetOnAxis(ap=at, axis=0)).then_inc(done, 16)

            for g in range(G):
                gather(rows[0:GW, g, :], flat_dst, row_i[0:GW, g:g + 1], row_in[g])
            gather(rows[0:NE, G, :], flat_dst, row_i[0:NE, G:G + 1], row_in[G])
            pool.wait_ge(starts_known, 1)
            for g in range(G):
                gather(gdst[0:GW, g, :], flat_dst, start_i[0:GW, g:g + 1], dst_in)
            for g in range(G):
                gather(gsrc[0:GW, g, :], flat_src, start_i[0:GW, g:g + 1], src_in)
            gather(edst[0:NE, :], flat_dst, start_i[0:NE, G:G + 1], edst_in)

        @block.vector
        def _(dve):
            step = Steps(dve, vstep)
            v = nc.vector
            dve.wait_ge(heads_in, 16)
            v.tensor_copy(heads[:, :], heads_i[:, :]).then_inc(heads_f, 1)
            dve.wait_ge(consts, 7)
            v.tensor_copy(iota[:, :], iota_i[:, :])
            v.tensor_copy(iota_e[:, :], iota_ei[:, :])
            v.tensor_copy(th[:, 0:G], th_i[:, 0:G])
            v.memset(total[:, :], 0.0)
            v.tensor_scalar(e_b[:, :], th_i[:, G:G + 1], 2, None, ALU.logical_shift_right)
            v.tensor_scalar(e_k[:, :], th_i[:, G:G + 1], 3, None, ALU.bitwise_and)
            step(v.tensor_scalar(th[:, G:G + 1], th_i[:, G:G + 1], float(EW), None, ALU.mult))
            step(v.scalar_tensor_tensor(out=th[:, G:G + 1], in0=e_b[:, :], scalar=float(BN - EK * EW),
                                        in1=th[:, G:G + 1], op0=ALU.mult, op1=ALU.add))
            step(v.tensor_scalar(e_w[:, :], e_k[:, :], float(EK - 1), float(BN - EK * EW), ALU.is_equal, ALU.mult))
            step(v.tensor_scalar(e_w[:, :], e_w[:, :], float(EW), None, ALU.add))
            dve.wait_ge(heads_out, 1)
            for g in range(G + 1):
                n = GW if g < G else NE
                step(v.tensor_scalar(junk[0:n, 0:R], heads_ps[0:n, 0:R], th[0:n, g:g + 1], 0.0, ALU.is_lt,
                                     ALU.add, accum_out=cnt1[0:n, g:g + 1]))

            def each(f):
                f(slice(0, GW), slice(0, G))
                f(slice(0, NE), slice(G, G + 1))
                step(v.memset(junk[0:1, 0:1], 0.0))

            each(lambda p, c: v.tensor_scalar(row_f[p, c], cnt1[p, c], -1.0, 0.0, ALU.add, ALU.max))
            each(lambda p, c: v.tensor_scalar(row_f[p, c], row_f[p, c], float(HR), None, ALU.mult))
            each(lambda p, c: v.tensor_copy(row_i[p, c], row_f[p, c]))
            dve.sem_inc(rows_known, 1)
            for g in range(G + 1):
                n = GW if g < G else NE
                dve.wait_ge(row_in[g], 16)
                step(v.tensor_scalar(junk[0:n, 0:HR], rows[0:n, g, :], th[0:n, g:g + 1], 0.0, ALU.is_lt,
                                     ALU.add, accum_out=cnt2[0:n, g:g + 1]))
            each(lambda p, c: v.tensor_tensor(row_f[p, c], row_f[p, c], cnt2[p, c], ALU.add))
            step(v.tensor_scalar(start_i[0:GW, 0:G], row_f[0:GW, 0:G], float(E - WE), None, ALU.min))
            step(v.tensor_scalar(start_i[0:NE, G:G + 1], row_f[0:NE, G:G + 1], float(E - EE), None, ALU.min))
            dve.sem_inc(starts_known, 1)
            dve.wait_ge(x_in, 32)
            dve.wait_ge(hi_cast, 1)
            v.tensor_tensor(part[:, :, :], xrows[:, :, :], xsplit[:, :, 0, :], ALU.subtract).then_inc(rest1, 1)
            dve.wait_ge(dst_in, 16 * G)
            thb = th[0:GW, 0:G].unsqueeze(2).to_broadcast([GW, G, WE])
            step(v.tensor_tensor(dl[0:GW, :, :], gdst[0:GW, :, :], thb, ALU.subtract))
            dve.wait_ge(src_in, 16 * G)
            v.tensor_scalar(lo_i[0:GW, :, :], gsrc[0:GW, :, :], P - 1, None, ALU.bitwise_and).then_inc(lo_int, 1)
            step(v.tensor_scalar(hi_i[0:GW, :, :], gsrc[0:GW, :, :], 7, None, ALU.logical_shift_right))
            v.scalar_tensor_tensor(out=key[0:GW, :, :], in0=dl[0:GW, :, :], scalar=float(HI),
                                   in1=hi_i[0:GW, :, :], op0=ALU.mult, op1=ALU.add).then_inc(keys_ready, 1)
            dve.wait_ge(edst_in, 16)
            v.tensor_scalar(edl[0:NE, :], edst[0:NE, :], th[0:NE, G:G + 1], None, ALU.subtract)\
             .then_inc(ekeys_ready, 1)
            jw = junk[0:GW, 0:G * WE].rearrange("p (g e) -> p g e", g=G)
            for k in range(WN):
                step(v.tensor_scalar(jw, dl[0:GW, :, :], float(k), None, ALU.is_equal))
                step(v.tensor_reduce(out=deg[0:GW, :, k], in_=jw, axis=AX.X, op=ALU.add))
            dve.sem_inc(deg_ready, 1)
            dve.wait_ge(ekeys_ready, 1)
            step(v.tensor_scalar(junk[0:NE, 0:EE], edl[0:NE, :], 0.0, 0.0, ALU.is_lt, ALU.add,
                                 accum_out=below[0:NE, 0:1]))
            step(v.tensor_scalar(junk[0:NE, 0:EE], edl[0:NE, :], e_w[0:NE, 0:1], 0.0, ALU.is_lt, ALU.add,
                                 accum_out=below[0:NE, 1:2]))
            step(v.tensor_tensor(total[0:NE, 1:2], below[0:NE, 1:2], below[0:NE, 0:1], ALU.subtract))
            step(v.tensor_reduce(out=total[0:GW, 0:1], in_=deg[0:GW, :, :], axis=AX.XY, op=ALU.add))
            dve.sem_inc(totals_ready, 1)
            dve.wait_ge(hi_cast, 2)
            v.tensor_tensor(xsplit[:, :, 2, :], part[:, :, :], xsplit[:, :, 1, :], ALU.subtract)
            dve.wait_ge(totals_out, 1)
            step(v.tensor_scalar(ok[:, :], total_ps[0:1, 0:2], float(E), None, ALU.is_equal))
            step(v.tensor_tensor(ok1[:, :], ok[:, 0:1], ok[:, 1:2], ALU.mult))
            step(v.tensor_copy(flag[:, :], ok1[:, :]))

        @block.scalar
        def _(act):
            act.wait_ge(x_in, 32)
            nc.scalar.copy(xsplit[:, :, 0, :], xrows[:, :, :]).then_inc(hi_cast, 1)
            act.wait_ge(rest1, 1)
            nc.scalar.copy(xsplit[:, :, 1, :], part[:, :, :]).then_inc(hi_cast, 1)
            act.wait_ge(lo_int, 1)
            nc.scalar.copy(lo[0:GW, :, :], lo_i[0:GW, :, :]).then_inc(lo_ready, 1)
            for g in range(G):
                act.wait_ge(turned, g + 1)
                for q, table in enumerate((key_t, lo_t)):
                    nc.scalar.copy(
                        table[:, g * GW * TILES:(g + 1) * GW * TILES].rearrange("p (w t) -> p t w", t=TILES),
                        tps[g % 4][:, TILES * q:TILES * q + TILES, 0:GW]).then_inc(tabled, 1)
            for m in range(EBANKS):
                act.wait_ge(turned, G + m + 1)
                n = min(4, EJ - 4 * m)
                nc.scalar.copy(ekey_t[:, :, 4 * m:4 * m + n].rearrange("p w j -> p j w"),
                               tps[(G + m) % 4][:, 0:n, 0:NE]).then_inc(tabled, 2)

        @block.tensor
        def _(pe):
            pe.wait_ge(heads_f, 1)
            pe.wait_ge(consts, 2)
            nc.tensor.matmul(heads_ps[:, 0:R], ones[0:1, :], heads[0:1, :], start=True, stop=True)\
              .then_inc(heads_out, 1)
            pe.wait_ge(keys_ready, 1)
            pe.wait_ge(lo_ready, 1)
            for g in range(G):
                if g >= 4:
                    pe.wait_ge(tabled, 2 * (g - 3))
                for q, t in ((0, 0), (0, 1), (1, 0), (1, 1)):
                    of = (key, lo)[q]
                    last = nc.tensor.transpose(tps[g % 4][:, 2 * q + t, 0:GW],
                                               of[0:GW, g, t * P:(t + 1) * P], ident[0:GW, 0:GW])
                last.then_inc(turned, 1)
            pe.wait_ge(ekeys_ready, 1)
            by_edge = edl[0:NE, :].rearrange("w (p j) -> w j p", j=EJ)
            for m in range(EBANKS):
                if G + m >= 4:
                    pe.wait_ge(tabled, 2 * (G + m - 3))
                for j in range(4 * m, min(4 * m + 4, EJ)):
                    last = nc.tensor.transpose(tps[(G + m) % 4][:, j - 4 * m, 0:NE], by_edge[:, j, :],
                                               ident[0:NE, 0:NE])
                last.then_inc(turned, 1)
            pe.wait_ge(totals_ready, 1)
            nc.tensor.matmul(total_ps[0:1, 0:2], ones[:, 0:1], total[:, :], start=True, stop=True)\
              .then_inc(totals_out, 1)


def aggregate_fast(nc, d, ea, keep, scratch):
    xsplit, flag, iota, key_t, lo_t, ekey_t, startrow, iota_e = (
        keep[k] for k in ("xsplit", "flag", "iota", "key_t", "lo_t", "ekey_t", "startrow", "iota_e"))
    HI, NB, E = d.HI, d.NB, d.E
    KW = WN * HI
    PRODUCTS = 3 * HI
    PER = -(-PRODUCTS // PAIRS)
    NT = TILES * BW
    with ExitStack() as ctx:
        sb = lambda name, shape, dt: ctx.enter_context(nc.sbuf_tensor(name, shape, dt))
        ps = lambda name: ctx.enter_context(nc.psum_tensor(name, [P, 512], F32))
        sem = lambda name: ctx.enter_context(nc.semaphore(name))
        counts = [sb(f"counts{i}", [P, HI, BN], BF16) for i in range(2)]
        key_oh = sb("key_oh", [P, RING, 4, 256], BF16)
        lo_oh = sb("lo_oh", [P, RING, 4, P], BF16)
        ebuf = [sb(f"ebuf{i}", [P, EJ, F], F32) for i in range(EK)]
        e_oh = [sb(f"e_oh{i}", [P, EJ, EW], F32) for i in range(2)]
        keys = [sb(f"keys{i}", [P, NT], F32) for i in range(2)]
        los = [sb(f"los{i}", [P, NT], F32) for i in range(2)]
        ekeys = [sb(f"ekeys{i}", [P, EK, EJ], F32) for i in range(2)]
        sx = [sb(f"sx{i}", [P, BN], F32) for i in range(2)]
        se = [sb(f"se{i}", [P, BN], F32) for i in range(2)]
        pair_ps = [ps(f"pair_ps{i}") for i in range(RING)]
        e_ps = ps("e_ps")
        x_ps = ps("x_ps")

        block_keys = sem("block_keys")
        key_hot, lo_hot, lo_hot_pool = sem("key_hot"), sem("lo_hot"), sem("lo_hot_pool")
        pair_built, pair_out = sem("pair_built"), sem("pair_out")
        e_hot, e_summed = sem("e_hot"), sem("e_summed")
        e_in = [sem(f"e_in{i}") for i in range(EK)]
        sp_passed, pool_passed = sem("sp_passed"), sem("pool_passed")
        product_done, sx_out, se_out = sem("product_done"), sem("sx_out"), sem("se_out")
        counts_kept = [sem(f"counts_kept{i}") for i in range(2)]
        sx_kept = [sem(f"sx_kept{i}") for i in range(2)]
        se_kept = [sem(f"se_kept{i}") for i in range(2)]
        block = ctx.enter_context(nc.Block())

        @block.sync
        def _(sp):
            fast = sp.value_load(flag[0:1, 0:1], min_val=0, max_val=1)
            with sp.If(fast > 0):
                def step(b, par, i):
                    for k in range(EK):
                        wait_alone(sp, e_summed, (b - 1) * EK + k + 1, sp_passed)
                        at = sp.value_load(startrow[0:1, bass.ds(b * EK + k, 1)], min_val=0, max_val=E - EE)
                        sp.dma_start(ebuf[k][:, :, :].rearrange("p j f -> p (j f)"),
                                     ea[bass.ds(at, EE), :].rearrange("(p j) f -> p (j f)", j=EJ))\
                          .then_inc(e_in[k], 16)
                all_blocks(sp, NB, step)

        @block.gpsimd
        def _(pool):
            fast = pool.value_load(flag[0:1, 0:1], min_val=0, max_val=1)
            with pool.If(fast > 0):
                def step(b, par, i):
                    nc.gpsimd.tensor_copy(keys[par][:, :], key_t[:, bass.ds(b * NT, NT)]).then_inc(block_keys, 1)
                    nc.gpsimd.tensor_copy(los[par][:, :], lo_t[:, bass.ds(b * NT, NT)]).then_inc(block_keys, 1)
                    nc.gpsimd.tensor_copy(ekeys[par][:, :, :], ekey_t[:, bass.ds(b * EK, EK), :])\
                      .then_inc(block_keys, 1)
                    wait_alone(pool, block_keys, b * 3 + 3, pool_passed)
                    for p in range(PAIRS):
                        wait_alone(pool, pair_built, b * PAIRS + (p + 1 - RING), pool_passed)
                        for w in range(2):
                            c = (2 * p + w) * TILES + 1
                            last = nc.gpsimd.tensor_scalar(lo_oh[:, p % RING, 2 * w + 1, :], iota[:, 0:P],
                                                           los[par][:, c:c + 1], None, ALU.is_equal)
                        last.then_inc(lo_hot_pool, 1)
                all_blocks(pool, NB, step)

        @block.vector
        def _(dve):
            fast = dve.value_load(flag[0:1, 0:1], min_val=0, max_val=1)
            with dve.If(fast > 0):
                def step(b, par, i):
                    dve.wait_ge(block_keys, b * 3 + 3)
                    for p in range(PAIRS):
                        reach(dve, pair_built, b * PAIRS + (p + 1 - RING))
                        for w in range(2):
                            c = (2 * p + w) * TILES
                            nc.vector.tensor_scalar(lo_oh[:, p % RING, 2 * w, :], iota[:, 0:P],
                                                    los[par][:, c:c + 1], None, ALU.is_equal)
                            for t in range(TILES):
                                last = nc.vector.tensor_scalar(
                                    key_oh[:, p % RING, 2 * w + t, 0:KW], iota[:, 0:KW],
                                    keys[par][:, c + t:c + t + 1], None, ALU.is_equal)
                        last.then_inc(key_hot, 1)
                        if p % 6 == 0 and p // 6 < EK:
                            k = p // 6
                            reach(dve, e_summed, b * EK + (k - 1))
                            nc.vector.tensor_tensor(
                                e_oh[k % 2][:, :, :], iota_e[:, :].unsqueeze(1).to_broadcast([P, EJ, EW]),
                                ekeys[par][:, k, :].unsqueeze(2).to_broadcast([P, EJ, EW]), ALU.is_equal)\
                              .then_inc(e_hot, 1)
                all_blocks(dve, NB, step)

        @block.tensor
        def _(pe):
            fast = pe.value_load(flag[0:1, 0:1], min_val=0, max_val=1)
            with pe.If(fast > 0):
                def product(b, par, p):
                    if p == 0:
                        pe.wait_ge(pair_out, b * PAIRS)
                    for q in range(PER * p, min(PER * (p + 1), PRODUCTS)):
                        last = nc.tensor.matmul(x_ps[:, 0:BN], xsplit[:, q // 3, q % 3, :],
                                                counts[1 - par][:, q // 3, :],
                                                start=(q == 0), stop=(q == PRODUCTS - 1))
                        if q == PRODUCTS - 1:
                            last.then_inc(product_done, 1)

                def step(b, par, i):
                    for p in range(PAIRS):
                        pe.wait_ge(key_hot, b * PAIRS + p + 1)
                        pe.wait_ge(lo_hot_pool, b * PAIRS + p + 1)
                        reach(pe, pair_out, b * PAIRS + (p + 1 - RING))
                        for w in range(2):
                            for t in range(TILES):
                                last = nc.tensor.matmul(pair_ps[p % RING][:, w * KW:(w + 1) * KW],
                                                        lo_oh[:, p % RING, 2 * w + t, :],
                                                        key_oh[:, p % RING, 2 * w + t, 0:KW],
                                                        start=(t == 0), stop=(t == TILES - 1))
                        last.then_inc(pair_built, 1)
                        if p >= 1:
                            k, part = (p - 1) // 6, (p - 1) % 6
                            if part == 0:
                                pe.wait_ge(e_hot, b * EK + k + 1)
                                pe.wait_ge(e_in[k], b * 16 + 16)
                            if k == 0 and part == 0:
                                reach(pe, se_out, b)
                            n = EW if k < EK - 1 else BN - EW * (EK - 1)
                            for j in range(3 * part, 3 * part + 3):
                                last = nc.tensor.matmul(e_ps[:, EW * k:EW * k + n], ebuf[k][:, j, :],
                                                        e_oh[k % 2][:, j, 0:n], start=(j == 0),
                                                        stop=(j == EJ - 1))
                            if part == 5:
                                last.then_inc(e_summed, 1)
                        if not (isinstance(b, int) and b == 0):
                            if p == 0:
                                reach(pe, sx_out, b - 1)
                            product(b, par, p)
                all_blocks(pe, NB, step)
                pe.wait_ge(sx_out, NB - 1)
                for p in range(PAIRS):
                    product(NB, NB % 2, p)

        @block.scalar
        def _(act):
            fast = act.value_load(flag[0:1, 0:1], min_val=0, max_val=1)
            with act.If(fast > 0):
                def product_out(b, par, old):
                    act.wait_ge(product_done, b)
                    reach(act, sx_kept[1 - par], old)
                    nc.scalar.copy(sx[1 - par][:, :], x_ps[:, 0:BN]).then_inc(sx_out, 1)
                    act.wait_ge(sx_out, b)
                    act.dma_start(scratch["sx"][:, bass.ds((b - 1) * BN, BN)], sx[1 - par][:, :])\
                       .then_inc(sx_kept[1 - par], 16)

                def step(b, par, i):
                    reach(act, product_done, b - 1)
                    reach(act, counts_kept[par], i * 16 if par else i * 16 + 16)
                    for p in range(PAIRS):
                        act.wait_ge(pair_built, b * PAIRS + p + 1)
                        nc.scalar.copy(counts[par][:, :, 2 * WN * p:2 * WN * (p + 1)],
                                       pair_ps[p % RING][:, 0:2 * KW].rearrange("p (n h) -> p h n", h=HI))\
                          .then_inc(pair_out, 1)
                    act.wait_ge(pair_out, (b + 1) * PAIRS)
                    act.dma_start(scratch["counts"][bass.ds(b * P, P), :],
                                  counts[par][:, :, :].rearrange("p h n -> p (h n)"))\
                       .then_inc(counts_kept[par], 16)
                    act.wait_ge(e_summed, (b + 1) * EK)
                    reach(act, se_kept[par], i * 16 if par else i * 16 + 16)
                    nc.scalar.copy(se[par][:, :], e_ps[:, 0:BN]).then_inc(se_out, 1)
                    act.wait_ge(se_out, b + 1)
                    act.dma_start(scratch["se"][:, bass.ds(b * BN, BN)], se[par][:, :])\
                       .then_inc(se_kept[par], 16)
                    if not (isinstance(b, int) and b == 0):
                        product_out(b, par, i * 16)
                all_blocks(act, NB, step)
                product_out(NB, NB % 2, (NB - 1) // 2 * 16)
                half = (NB - 1) // 2 * 16
                for kept in (counts_kept, se_kept, sx_kept):
                    act.wait_ge(kept[0], half + 16)
                    act.wait_ge(kept[1], half)


def aggregate_fast_again(nc, d, keep, scratch):
    zsplit, flag = keep["xsplit"], keep["flag"]
    HI, NB = d.HI, d.NB
    PRODUCTS = 3 * HI
    with ExitStack() as ctx:
        counts = [ctx.enter_context(nc.sbuf_tensor(f"counts_again{i}", [P, HI, BN], BF16)) for i in range(2)]
        s1 = [ctx.enter_context(nc.sbuf_tensor(f"s1_{i}", [P, BN], F32)) for i in range(2)]
        z_ps = [ctx.enter_context(nc.psum_tensor(f"z_ps{i}", [P, 512], F32)) for i in range(2)]
        sem = lambda name: ctx.enter_context(nc.semaphore(name))
        counts_in = [sem(f"counts_in{i}") for i in range(2)]
        s1_kept = [sem(f"s1_kept{i}") for i in range(2)]
        multiplied, s1_out, sp_passed = sem("multiplied"), sem("s1_out"), sem("sp_passed")
        block = ctx.enter_context(nc.Block())

        @block.sync
        def _(sp):
            fast = sp.value_load(flag[0:1, 0:1], min_val=0, max_val=1)
            with sp.If(fast > 0):
                def step(b, par, i):
                    wait_alone(sp, multiplied, b - 1, sp_passed)
                    sp.dma_start(counts[par][:, :, :].rearrange("p h n -> p (h n)"),
                                 scratch["counts"][bass.ds(b * P, P), :]).then_inc(counts_in[par], 16)
                all_blocks(sp, NB, step)

        @block.tensor
        def _(pe):
            fast = pe.value_load(flag[0:1, 0:1], min_val=0, max_val=1)
            with pe.If(fast > 0):
                def step(b, par, i):
                    pe.wait_ge(counts_in[par], i * 16 + (16 if par else 32))
                    reach(pe, s1_out, b - 1)
                    for q in range(PRODUCTS):
                        last = nc.tensor.matmul(z_ps[par][:, 0:BN], zsplit[:, q // 3, q % 3, :],
                                                counts[par][:, q // 3, :],
                                                start=(q == 0), stop=(q == PRODUCTS - 1))
                    last.then_inc(multiplied, 1)
                all_blocks(pe, NB, step)

        @block.scalar
        def _(act):
            fast = act.value_load(flag[0:1, 0:1], min_val=0, max_val=1)
            with act.If(fast > 0):
                def step(b, par, i):
                    act.wait_ge(multiplied, b + 1)
                    reach(act, s1_kept[par], i * 16 if par else i * 16 + 16)
                    nc.scalar.copy(s1[par][:, :], z_ps[par][:, 0:BN]).then_inc(s1_out, 1)
                    act.wait_ge(s1_out, b + 1)
                    act.dma_start(scratch["s1"][:, bass.ds(b * BN, BN)], s1[par][:, :])\
                       .then_inc(s1_kept[par], 16)
                all_blocks(act, NB, step)
                half = (NB - 1) // 2 * 16
                act.wait_ge(s1_kept[0], half + 16)
                act.wait_ge(s1_kept[1], half)


def aggregate_any(nc, d, name, table, ea, src, dst, keep, sum_out, esum_out, deg_out):
    flag = keep["flag"]
    N, E = d.N, d.E
    GR = -(-N // GN)
    NT = E // GE
    kinds = 3 if ea is not None else 1
    with ExitStack() as ctx:
        sb = lambda n, shape, dt: ctx.enter_context(nc.sbuf_tensor(f"{name}_{n}", shape, dt))
        sem = lambda n: ctx.enter_context(nc.semaphore(f"{name}_{n}"))
        acc = [sb(f"acc{k}", [P, GR * GN], F32) for k in range(kinds)]
        data = [sb(f"data{k}", [P, F], F32) for k in range(kinds)]
        ones = data[2] if kinds == 3 else None
        src_i, dst_i, dst_f = sb("src_i", [P, 1], I32), sb("dst_i", [P, 1], I32), sb("dst_f", [P, 1], F32)
        node_i, node = sb("node_i", [P, GR * GN], I32), sb("node", [P, GR * GN], F32)
        hot = [sb(f"hot{i}", [P, GN], F32) for i in range(2)]
        sums = [[ctx.enter_context(nc.psum_tensor(f"{name}_sum{k}_{i}", [P, 512], F32)) for i in range(2)]
                for k in range(kinds)]
        idx_in, row_in, ea_in, ready = sem("idx_in"), sem("row_in"), sem("ea_in"), sem("ready")
        made, cast, summed, added, stored = sem("made"), sem("cast"), sem("summed"), sem("added"), sem("stored")
        nodes_made, pool_passed, sp_passed = sem("nodes_made"), sem("pool_passed"), sem("sp_passed")
        block = ctx.enter_context(nc.Block())

        @block.sync
        def _(sp):
            fast = sp.value_load(flag[0:1, 0:1], min_val=0, max_val=1)
            with sp.If(fast < 1):
                def turn(t):
                    wait_alone(sp, summed, t * GR, sp_passed)
                    wait_alone(sp, made, t * GR, sp_passed)
                    sp.dma_start(src_i[0:GE, :], src[bass.ds(t * GE, GE)].rearrange("(p o) -> p o", o=1))\
                      .then_inc(idx_in, 16)
                    sp.dma_start(dst_i[0:GE, :], dst[bass.ds(t * GE, GE)].rearrange("(p o) -> p o", o=1))\
                      .then_inc(idx_in, 16)
                    if kinds == 3:
                        sp.dma_start(data[1][0:GE, :], ea[bass.ds(t * GE, GE), :]).then_inc(ea_in, 16)
                    sp.wait_ge(idx_in, t * 32 + 32)
                    wait_alone(sp, row_in, t * 16 + 16, sp_passed)
                all_turns(sp, NT, turn)
                sp.wait_ge(added, NT * GR)
                sp.dma_start(sum_out[:, 0:N], acc[0][:, 0:N]).then_inc(stored, 16)
                if kinds == 3:
                    sp.dma_start(esum_out[:, 0:N], acc[1][:, 0:N]).then_inc(stored, 16)
                    sp.dma_start(deg_out[0:N].rearrange("(o n) -> o n", o=1), acc[2][0:1, 0:N])\
                      .then_inc(stored, 16)
                sp.wait_ge(stored, 16 * kinds)

        @block.gpsimd
        def _(pool):
            fast = pool.value_load(flag[0:1, 0:1], min_val=0, max_val=1)
            with pool.If(fast < 1):
                nc.gpsimd.iota(node_i[:, :], pattern=[[1, GR * GN]], base=0, channel_multiplier=0)\
                  .then_inc(nodes_made, 1)
                def turn(t):
                    wait_alone(pool, idx_in, t * 32 + 32, pool_passed)
                    nc.gpsimd.indirect_dma_start(
                        out=data[0][0:GE, :], out_offset=None, in_=table,
                        in_offset=bass.IndirectOffsetOnAxis(ap=src_i[0:GE, :], axis=0)).then_inc(row_in, 16)
                all_turns(pool, NT, turn)

        @block.vector
        def _(dve):
            fast = dve.value_load(flag[0:1, 0:1], min_val=0, max_val=1)
            with dve.If(fast < 1):
                for a in acc:
                    nc.vector.memset(a[:, :], 0.0).then_inc(ready, 1)
                if kinds == 3:
                    nc.vector.memset(ones[:, :], 1.0).then_inc(ready, 1)
                else:
                    dve.sem_inc(ready, 1)
                dve.wait_ge(nodes_made, 1)
                nc.vector.tensor_copy(node[:, :], node_i[:, :]).then_inc(ready, 1)
                dve.wait_ge(ready, kinds + 2)
                def turn(t):
                    dve.wait_ge(idx_in, t * 32 + 32)
                    nc.vector.tensor_copy(dst_f[0:GE, :], dst_i[0:GE, :]).then_inc(cast, 1)
                    dve.wait_ge(cast, t + 1)
                    for g in range(GR + 1):
                        if g < GR:
                            if g >= 2:
                                reach(dve, summed, t * GR + (g - 1))
                            nc.vector.tensor_scalar(hot[g % 2][0:GE, :], node[0:GE, g * GN:(g + 1) * GN],
                                                    dst_f[0:GE, 0:1], None, ALU.is_equal).then_inc(made, 1)
                        if g >= 1:
                            h = g - 1
                            dve.wait_ge(summed, t * GR + h + 1)
                            for k in range(kinds):
                                at = acc[k][:, h * GN:(h + 1) * GN]
                                last = nc.vector.tensor_tensor(at, at, sums[k][h % 2][:, :], ALU.add)
                            last.then_inc(added, 1)
                    dve.wait_ge(added, t * GR + GR)
                all_turns(dve, NT, turn)

        @block.tensor
        def _(pe):
            fast = pe.value_load(flag[0:1, 0:1], min_val=0, max_val=1)
            with pe.If(fast < 1):
                pe.wait_ge(ready, kinds + 2)
                def turn(t):
                    pe.wait_ge(row_in, t * 16 + 16)
                    if kinds == 3:
                        pe.wait_ge(ea_in, t * 16 + 16)
                    reach(pe, added, t * GR)
                    for g in range(GR):
                        pe.wait_ge(made, t * GR + g + 1)
                        if g >= 2:
                            reach(pe, added, t * GR + (g - 1))
                        for k in range(kinds):
                            last = nc.tensor.matmul(sums[k][g % 2][:, :], data[k][0:GE, :],
                                                    hot[g % 2][0:GE, :], start=True, stop=True)
                        last.then_inc(summed, 1)
                all_turns(pe, NT, turn)


def norm_rows(nc, dve, step, v, C, t, eps, scaled_by):
    mean, var, sq = t
    n = v.shape[2]
    wide = lambda a: a[:, 0:C].unsqueeze(2).to_broadcast([P, C, n])
    step(nc.vector.tensor_reduce(out=mean[:, :], in_=v[:, :, :], axis=AX.X, op=ALU.add))
    step(nc.vector.tensor_scalar(mean[:, :], mean[:, :], 1.0 / n, None, ALU.mult))
    step(nc.vector.tensor_tensor(v[:, :, :], v[:, :, :], wide(mean), ALU.subtract))
    step(nc.vector.tensor_tensor(sq[:, :, :], v[:, :, :], v[:, :, :], ALU.mult))
    step(nc.vector.tensor_reduce(out=var[:, :], in_=sq[:, :, :], axis=AX.X, op=ALU.add))
    step(nc.vector.tensor_scalar(var[:, :], var[:, :], 1.0 / n, eps, ALU.mult, ALU.add))
    scaled_by()
    step(nc.vector.reciprocal(var[:, :], var[:, :]))
    step(nc.vector.tensor_tensor(v[:, :, :], v[:, :, :], wide(var), ALU.mult))


class LoopSteps:

    def __init__(self, engine, sem, i, per_turn):
        self.engine, self.sem, self.i, self.per, self.n = engine, sem, i, per_turn, 0

    def __call__(self, ins):
        self.n += 1
        ins.then_inc(self.sem, 1)
        self.engine.wait_ge(self.sem, self.i * self.per + self.n)

    def close(self):
        assert self.n == self.per, self.n


def update_first(nc, d, W, bW, We, bWe, keep, scratch):
    xrows, xsplit, ident, zT = (keep[k] for k in ("xrows", "xsplit", "ident", "zT"))
    HI, C, NCH, NP, N = d.HI, d.CH, d.NC, d.NP, d.N
    VS = 12
    with ExitStack() as ctx:
        sb = lambda n, shape, dt: ctx.enter_context(nc.sbuf_tensor(f"u0_{n}", shape, dt))
        sem = lambda n: ctx.enter_context(nc.semaphore(f"u0_{n}"))
        wi, wj, we = sb("wi", [P, F], F32), sb("wj", [P, F], F32), sb("we", [P, F], F32)
        bi, bj, bje, be = (sb(n, [1, F], F32) for n in ("bi", "bj", "bje", "be"))
        ones = sb("ones", [1, P], F32)
        zero = sb("zero", [P, P], F32)
        deg, rdeg, dinv = sb("deg", [P, HI], F32), sb("rdeg", [P, HI], F32), sb("dinv", [P, HI], F32)
        rdc, dic = sb("rdc", [P, C], F32), sb("dic", [P, C], F32)
        sxc, sec = sb("sxc", [P, C, P], F32), sb("sec", [P, C, P], F32)
        degrow = sb("degrow", [1, C, P], F32)
        xc, xT = sb("xc", [P, C, F], F32), sb("xT", [P, C, P], F32)
        msg, v = sb("msg", [P, C, F], F32), sb("v", [P, C, F], F32)
        sq = sb("sq", [P, C, F], F32)
        z, rest = sb("z", [P, C, F], F32), sb("rest", [P, C, F], F32)
        hm = sb("hm", [P, C, 2, F], BF16)
        mean, var = sb("mean", [P, C], F32), sb("var", [P, C], F32)
        H = -(-C // 2)
        pst = lambda n: ctx.enter_context(nc.psum_tensor(f"u0_{n}", [P, 4, P], F32))
        t_ps, i_ps, j_ps, z_ps = ([pst(f"{n}{k}") for k in range(2)] for n in ("t", "i", "j", "z"))
        w_in, deg_in, ready, cols = sem("w_in"), sem("deg_in"), sem("ready"), sem("cols_done")
        pads, dinv_out, root = sem("pads_out"), sem("dinv_out"), sem("deg_root")
        chunk_in, small = sem("chunk_in"), sem("chunk_cols")
        x_copied, turned, turned_out = sem("x_copied"), sem("turned"), sem("turned_out")
        multiplied, msg_out, vstep = sem("multiplied"), sem("msg_out"), sem("vstep")
        var_ready, std_ready = sem("var_ready"), sem("std_ready")
        z_ready, cast, rest_ready = sem("z_ready"), sem("cast"), sem("rest_ready")
        sp_passed = sem("sp_passed")
        z_turned, z_out, z_kept, low_done = sem("z_turned"), sem("z_turned_out"), sem("z_kept"), sem("low_done")
        block = ctx.enter_context(nc.Block())
        psk = lambda pss, k: pss[k // 4][:, k % 4, :]

        @block.sync
        def _(sp):
            row = lambda a: a.rearrange("(o n) -> o n", o=1)
            for out, in_ in ((wi[:, :], W[:, 0:F]), (wj[:, :], W[:, F:2 * F]), (we[:, :], We),
                             (bi[:, :], row(bW[0:F])), (bj[:, :], row(bW[F:2 * F])), (be[:, :], row(bWe))):
                sp.dma_start(out, in_).then_inc(w_in, 16)
            sp.dma_start(deg[:, :], scratch["deg"].rearrange("(h p) -> p h", p=P),
                         allow_slow_non_contiguous=True).then_inc(deg_in, 16)
            sp.wait_ge(ready, 1)
            pad = NP - N
            sp.dma_start(scratch["sx"][:, N:NP], zero[:, 0:pad]).then_inc(pads, 16)
            sp.dma_start(scratch["se"][:, N:NP], zero[:, 0:pad]).then_inc(pads, 16)
            sp.wait_ge(pads, 32)
            sp.wait_ge(cols, 1)
            sp.dma_start(scratch["dinv"].rearrange("(h p) -> p h", p=P), dinv[:, :],
                         allow_slow_non_contiguous=True).then_inc(dinv_out, 16)
            def turn(i):
                wait_alone(sp, multiplied, i, sp_passed)
                cols_of = bass.ds(i * (C * P), C * P)
                sp.dma_start(sxc[:, :, :].rearrange("p c n -> p (c n)"), scratch["sx"][:, cols_of])\
                  .then_inc(chunk_in, 16)
                sp.dma_start(sec[:, :, :].rearrange("p c n -> p (c n)"), scratch["se"][:, cols_of])\
                  .then_inc(chunk_in, 16)
                sp.dma_start(degrow[:, :, :].rearrange("p c n -> p (c n)"),
                             scratch["deg"][cols_of].rearrange("(o n) -> o n", o=1)).then_inc(chunk_in, 16)
                wait_alone(sp, z_ready, i + 1, sp_passed)
                sp.dma_start(scratch["z"][cols_of, :].rearrange("(c p) f -> p c f", p=P), z[:, :, :])\
                  .then_inc(z_kept, 16)
            all_turns(sp, NCH, turn)
            sp.wait_ge(z_kept, NCH * 16)
            sp.wait_ge(dinv_out, 16)

        @block.scalar
        def _(act):
            act.wait_ge(root, 1)
            nc.scalar.activation(dinv[:, :], dinv[:, :], ACT.Sqrt).then_inc(root, 1)
            def turn(i):
                reach(act, multiplied, i)
                reach(act, vstep, i * VS)
                nc.scalar.copy(xc[:, :, :], xrows[:, bass.ds(i * C, C), :]).then_inc(x_copied, 1)
                act.wait_ge(turned, i + 1)
                for h in range(2):
                    n = (4, C - 4)[h] if C > 4 else (C, 0)[h]
                    if n:
                        nc.scalar.copy(xT[:, 4 * h:4 * h + n, :], t_ps[h][:, 0:n, :]).then_inc(turned_out, 1)
                    else:
                        act.sem_inc(turned_out, 1)
                act.wait_ge(multiplied, i + 1)
                act.wait_ge(small, i + 1)
                for k in range(C):
                    last = nc.scalar.activation(msg[:, k, :], psk(j_ps, k), ACT.Copy, scale=rdc[:, k:k + 1])
                last.then_inc(msg_out, 1)
                act.wait_ge(var_ready, i + 1)
                nc.scalar.activation(var[:, :], var[:, :], ACT.Sqrt).then_inc(std_ready, 1)
                act.wait_ge(z_ready, i + 1)
                nc.scalar.copy(hm[:, :, 0, :], z[:, :, :]).then_inc(cast, 1)
                act.wait_ge(cast, i * 2 + 1)
                nc.scalar.copy(xsplit[:, bass.ds(i * C, C), 0, :], hm[:, :, 0, :])
                act.wait_ge(z_turned, i + 1)
                for h in range(2):
                    n = (4, C - 4)[h] if C > 4 else (C, 0)[h]
                    if n:
                        nc.scalar.copy(zT[:, bass.ds(i * (C * P) + 4 * h * P, n * P)].rearrange("p (c n) -> p c n", n=P),
                                       z_ps[h][:, 0:n, :]).then_inc(z_out, 1)
                    else:
                        act.sem_inc(z_out, 1)
                act.wait_ge(rest_ready, i + 1)
                nc.scalar.copy(hm[:, :, 1, :], rest[:, :, :]).then_inc(cast, 1)
                act.wait_ge(cast, i * 2 + 2)
                nc.scalar.copy(xsplit[:, bass.ds(i * C, C), 1, :], hm[:, :, 1, :])
            all_turns(act, NCH, turn)

        @block.vector
        def _(dve):
            vv = nc.vector
            pre = Steps(dve, sem("pre_step"))
            vv.memset(zero[:, :], 0.0)
            vv.memset(ones[:, :], 1.0).then_inc(ready, 1)
            dve.wait_ge(w_in, 96)
            pre(vv.tensor_tensor(bje[:, :], bj[:, :], be[:, :], ALU.add))
            dve.sem_inc(ready, 1)
            dve.wait_ge(deg_in, 16)
            pre(vv.tensor_scalar(dinv[:, :], deg[:, :], 1.0, None, ALU.add))
            dve.sem_inc(root, 1)
            pre(vv.tensor_scalar(rdeg[:, :], deg[:, :], 1e-6, None, ALU.add))
            pre(vv.reciprocal(rdeg[:, :], rdeg[:, :]))
            dve.wait_ge(root, 2)
            pre(vv.reciprocal(dinv[:, :], dinv[:, :]))
            dve.sem_inc(cols, 1)
            def turn(i):
                step = LoopSteps(dve, vstep, i, VS)
                reach(dve, msg_out, i)
                vv.tensor_copy(dic[:, :], dinv[:, bass.ds(i * C, C)])
                vv.tensor_copy(rdc[:, :], rdeg[:, bass.ds(i * C, C)]).then_inc(small, 1)
                dve.wait_ge(msg_out, i + 1)
                for h in range(2):
                    n = (4, C - 4)[h] if C > 4 else (C, 0)[h]
                    if n:
                        last = vv.tensor_tensor(v[:, 4 * h:4 * h + n, :], msg[:, 4 * h:4 * h + n, :],
                                                i_ps[h][:, 0:n, :], ALU.add)
                step(last)
                step(vv.tensor_tensor(v[:, :, :], v[:, :, :], xc[:, :, :], ALU.add))

                def root_of_var():
                    dve.sem_inc(var_ready, 1)
                    dve.wait_ge(std_ready, i + 1)

                norm_rows(nc, dve, step, v, C, (mean, var, sq), 1e-5, root_of_var)
                vv.tensor_copy(xrows[:, bass.ds(i * C, C), :], v[:, :, :])
                reach(dve, z_kept, i * 16)
                reach(dve, z_turned, i)
                step(vv.tensor_tensor(z[:, :, :], v[:, :, :],
                                      dic[:, :].unsqueeze(2).to_broadcast([P, C, F]), ALU.mult))
                dve.sem_inc(z_ready, 1)
                dve.wait_ge(cast, i * 2 + 1)
                step(vv.tensor_tensor(rest[:, :, :], z[:, :, :], hm[:, :, 0, :], ALU.subtract))
                dve.sem_inc(rest_ready, 1)
                dve.wait_ge(cast, i * 2 + 2)
                vv.tensor_tensor(xsplit[:, bass.ds(i * C, C), 2, :], rest[:, :, :], hm[:, :, 1, :], ALU.subtract)\
                  .then_inc(low_done, 1)
                dve.wait_ge(low_done, i + 1)
                step.close()
            all_turns(dve, NCH, turn)

        @block.tensor
        def _(pe):
            pe.wait_ge(ready, 2)
            def turn(i):
                pe.wait_ge(x_copied, i + 1)
                for k in range(C):
                    last = nc.tensor.transpose(psk(t_ps, k), xc[:, k, :], ident[:, :])
                last.then_inc(turned, 1)
                pe.wait_ge(chunk_in, i * 48 + 48)
                pe.wait_ge(turned_out, i * 2 + 2)
                for k in range(C):
                    nc.tensor.matmul(psk(i_ps, k), xT[:, k, :], wi[:, :], start=True, stop=False)
                    nc.tensor.matmul(psk(i_ps, k), ones[0:1, :], bi[0:1, :], start=False, stop=True)
                    nc.tensor.matmul(psk(j_ps, k), sxc[:, k, :], wj[:, :], start=True, stop=False)
                    nc.tensor.matmul(psk(j_ps, k), sec[:, k, :], we[:, :], start=False, stop=False)
                    last = nc.tensor.matmul(psk(j_ps, k), degrow[0:1, k, :], bje[0:1, :], start=False, stop=True)
                last.then_inc(multiplied, 1)
                pe.wait_ge(z_ready, i + 1)
                reach(pe, z_out, i * 2)
                for k in range(C):
                    last = nc.tensor.transpose(psk(z_ps, k), z[:, k, :], ident[:, :])
                last.then_inc(z_turned, 1)
            all_turns(pe, NCH, turn)


def update_second(nc, d, W, b, gamma, beta, out, keep, scratch):
    xrows, ident, zT = (keep[k] for k in ("xrows", "ident", "zT"))
    HI, C, NCH, NP, N, NB = d.HI, d.CH, d.NC, d.NP, d.N, d.NB
    VS = 9
    with ExitStack() as ctx:
        sb = lambda n, shape, dt: ctx.enter_context(nc.sbuf_tensor(f"u1_{n}", shape, dt))
        sem = lambda n: ctx.enter_context(nc.semaphore(f"u1_{n}"))
        w = sb("w", [P, F], F32)
        vec = sb("vec", [P, 3], F32)
        s1 = sb("s1", [P, NP], F32)
        dinv = sb("dinv", [P, NP], F32)
        y = sb("y", [P, NP], F32)
        stats = sb("stats", [P, NB, 6], F32)
        mv, sc = sb("mv", [P, 2], F32), sb("sc", [P, 4], F32)
        t = sb("t", [P, C, P], F32)
        r = sb("r", [P, C, P], F32)
        v, sq, xo = sb("v", [P, C, F], F32), sb("sq", [P, C, F], F32), sb("xo", [P, C, F], F32)
        mean, var = sb("mean", [P, C], F32), sb("var", [P, C], F32)
        y_ps = [ctx.enter_context(nc.psum_tensor(f"u1_y{k}", [P, 512], F32)) for k in range(5)]
        r_ps = [ctx.enter_context(nc.psum_tensor(f"u1_r{k}", [P, 4, P], F32)) for k in range(2)]
        loads, dinv_in, s1_in = sem("loads"), sem("dinv_in"), sem("s1_in")
        own_added, multiplied, scaled, biased = sem("own_added"), sem("multiplied"), sem("scaled"), sem("biased")
        stat, vpre, root = sem("stat"), sem("pre_step"), sem("batch_root")
        t_ready, r_ready, turned, vstep = sem("t_ready"), sem("r_ready"), sem("turned"), sem("vstep")
        var_ready, std_ready, xo_ready, kept = sem("var_ready"), sem("std_ready"), sem("xo_ready"), sem("kept")
        coeff, sp_passed = sem("coefficients"), sem("sp_passed")
        block = ctx.enter_context(nc.Block())
        psk = lambda pss, k: pss[k // 4][:, k % 4, :]
        U = 5
        assert NB % U == 0

        @block.sync
        def _(sp):
            sp.dma_start(w[:, :], W).then_inc(loads, 16)
            for k, a in enumerate((b, gamma, beta)):
                sp.dma_start(vec[:, k:k + 1], a.rearrange("(p o) -> p o", o=1)).then_inc(loads, 16)
            sp.dma_start(s1[:, 0:N], scratch["s1"][:, 0:N]).then_inc(s1_in, 16)
            sp.dma_start(dinv[:, :], scratch["dinv"].rearrange("(o n) -> o n", o=1).to_broadcast([P, NP]))\
              .then_inc(dinv_in, 16)

            def turn(i):
                wait_alone(sp, xo_ready, i + 1, sp_passed)
                sp.dma_start(out[bass.ds(i * (C * P), C * P), :].rearrange("(c p) f -> p c f", p=P), xo[:, :, :])\
                  .then_inc(kept, 16)
            all_turns(sp, NCH - 1, turn)
            sp.wait_ge(xo_ready, NCH)
            base = (NCH - 1) * C * P
            if C > 1:
                sp.dma_start(out[base:base + (C - 1) * P, :].rearrange("(c p) f -> p c f", p=P),
                             xo[:, 0:C - 1, :]).then_inc(kept, 16)
            sp.dma_start(out[(HI - 1) * P:N, :], xo[0:d.REM, C - 1, :]).then_inc(kept, 16)
            sp.wait_ge(kept, 16 * (NCH + (1 if C > 1 else 0)))

        @block.scalar
        def _(act):
            act.wait_ge(loads, 64)
            def turn(i):
                for u in range(U):
                    act.wait_ge(scaled, i * U + u + 1)
                    at = y[:, bass.ds(i * (U * BN) + u * BN, BN)]
                    nc.scalar.activation(at, at, ACT.Identity, bias=vec[:, 0:1]).then_inc(biased, 1)
            all_turns(act, NB // U, turn)
            act.wait_ge(root, 1)
            nc.scalar.activation(sc[:, 0:1], sc[:, 0:1], ACT.Sqrt).then_inc(root, 1)
            act.wait_ge(coeff, 1)
            def turn(i):
                reach(act, r_ready, i)
                nc.scalar.activation(t[:, :, :].rearrange("p c n -> p (c n)"), y[:, bass.ds(i * (C * P), C * P)],
                                     ACT.Identity, bias=sc[:, 2:3], scale=sc[:, 1:2]).then_inc(t_ready, 1)
                act.wait_ge(var_ready, i + 1)
                nc.scalar.activation(var[:, :], var[:, :], ACT.Sqrt).then_inc(std_ready, 1)
            all_turns(act, NCH, turn)

        @block.vector
        def _(dve):
            vv = nc.vector
            step0 = Steps(dve, vpre)
            step0(vv.memset(y[:, N:NP], 0.0))
            dve.wait_ge(s1_in, 16)
            step0(vv.tensor_tensor(s1[:, 0:N], s1[:, 0:N], zT[:, 0:N], ALU.add))
            dve.sem_inc(own_added, 1)
            dve.wait_ge(dinv_in, 16)
            def turn(i):
                for u in range(U):
                    dve.wait_ge(multiplied, i * U + u + 1)
                    cols = bass.ds(i * (U * BN) + u * BN, BN)
                    vv.tensor_tensor(y[:, cols], y_ps[u][:, 0:BN], dinv[:, cols], ALU.mult).then_inc(scaled, 1)
                for u in range(U):
                    dve.wait_ge(biased, i * U + u + 1)
                    vv.bn_stats(stats[:, bass.ds(i * U + u, 1), :].rearrange("p a b -> p (a b)"),
                                y[:, bass.ds(i * (U * BN) + u * BN, BN)]).then_inc(stat, 1)
            all_turns(dve, NB // U, turn)
            dve.wait_ge(stat, NB)
            step0(vv.bn_aggr(mv[:, :], stats[:, :, :].rearrange("p a b -> p (a b)")))
            step0(vv.tensor_scalar(sc[:, 0:1], mv[:, 1:2], 1e-5, None, ALU.add))
            dve.sem_inc(root, 1)
            dve.wait_ge(root, 2)
            step0(vv.reciprocal(sc[:, 1:2], sc[:, 0:1]))
            dve.wait_ge(loads, 64)
            step0(vv.tensor_tensor(sc[:, 1:2], sc[:, 1:2], vec[:, 1:2], ALU.mult))
            step0(vv.tensor_tensor(sc[:, 3:4], mv[:, 0:1], sc[:, 1:2], ALU.mult))
            step0(vv.tensor_tensor(sc[:, 2:3], vec[:, 2:3], sc[:, 3:4], ALU.subtract))
            dve.sem_inc(coeff, 1)
            def turn(i):
                step = LoopSteps(dve, vstep, i, VS)
                dve.wait_ge(t_ready, i + 1)
                reach(dve, turned, i)
                vv.scalar_tensor_tensor(out=r[:, :, :], in0=t[:, :, :], scalar=0.01, in1=t[:, :, :],
                                        op0=ALU.mult, op1=ALU.max).then_inc(r_ready, 1)
                dve.wait_ge(turned, i + 1)
                for h in range(2):
                    n = (4, C - 4)[h] if C > 4 else (C, 0)[h]
                    if n:
                        last = vv.tensor_tensor(v[:, 4 * h:4 * h + n, :],
                                                xrows[:, bass.ds(i * C + 4 * h, n), :], r_ps[h][:, 0:n, :], ALU.add)
                step(last)

                def root_of_var():
                    dve.sem_inc(var_ready, 1)
                    dve.wait_ge(std_ready, i + 1)

                norm_rows(nc, dve, step, v, C, (mean, var, sq), 1e-5, root_of_var)
                reach(dve, kept, i * 16)
                vv.tensor_copy(xo[:, :, :], v[:, :, :]).then_inc(xo_ready, 1)
                dve.wait_ge(xo_ready, i + 1)
                step.close()
            all_turns(dve, NCH, turn)

        @block.tensor
        def _(pe):
            pe.wait_ge(loads, 64)
            pe.wait_ge(own_added, 1)
            def turn(i):
                for u in range(U):
                    reach(pe, scaled, i * U)
                    nc.tensor.matmul(y_ps[u][:, 0:BN], w[:, :], s1[:, bass.ds(i * (U * BN) + u * BN, BN)],
                                     start=True, stop=True).then_inc(multiplied, 1)
            all_turns(pe, NB // U, turn)
            def turn(i):
                pe.wait_ge(r_ready, i + 1)
                reach(pe, vstep, i * VS)
                for k in range(C):
                    last = nc.tensor.transpose(psk(r_ps, k), r[:, k, :], ident[:, :])
                last.then_inc(turned, 1)
            all_turns(pe, NCH, turn)


def build(nc, x, src, dst, ea, W0, b0, We, be, W1, b1, gamma, beta, out):
    d = Dims(x.shape[0], src.shape[0])
    NE = d.NB * EK
    dram = lambda name, shape, dt: nc.dram_tensor(name, shape, dt)
    scratch = {
        "starts": dram("starts", [NE, 1], I32)[:, :],
        "deg": dram("deg_rows", [d.NP], F32)[:],
        "dinv": dram("dinv_rows", [d.NP], F32)[:],
        "sx": dram("sums_x", [P, d.NP], F32)[:, :],
        "se": dram("sums_e", [P, d.NP], F32)[:, :],
        "s1": dram("sums_z", [P, d.NP], F32)[:, :],
        "z": dram("z_rows", [d.NP, F], F32)[:, :],
        "counts": dram("counts_kept", [d.NB * P, d.HI * BN], BF16)[:, :],
    }
    with ExitStack() as ctx:
        sb = lambda name, shape, dt: ctx.enter_context(nc.sbuf_tensor(name, shape, dt))
        keep = {
            "xrows": sb("xrows", [P, d.HI, F], F32),
            "xsplit": sb("xsplit", [P, d.HI, 3, F], BF16),
            "ident": sb("ident", [P, P], F32),
            "flag": sb("flag", [1, 1], I32),
        }
        with ExitStack() as tables:
            tb = lambda name, shape, dt: tables.enter_context(nc.sbuf_tensor(name, shape, dt))
            keep.update({
                "iota": tb("iota", [P, 256], BF16), "iota_e": tb("iota_e", [P, EW], F32),
                "key_t": tb("key_t", [P, d.NW * TILES], F32), "lo_t": tb("lo_t", [P, d.NW * TILES], F32),
                "ekey_t": tb("ekey_t", [P, NE, EJ], F32), "startrow": tb("startrow", [1, NE], I32),
            })
            prepare(nc, d, x, src, dst, keep, scratch)
            aggregate_fast(nc, d, ea, keep, scratch)
        aggregate_any(nc, d, "any0", x, ea, src, dst, keep, scratch["sx"], scratch["se"], scratch["deg"])
        keep["zT"] = sb("zT", [P, d.NP], F32)
        update_first(nc, d, W0, b0, We, be, keep, scratch)
        aggregate_fast_again(nc, d, keep, scratch)
        aggregate_any(nc, d, "any1", scratch["z"], None, src, dst, keep, scratch["s1"], None, None)
        update_second(nc, d, W1, b1, gamma, beta, out, keep, scratch)


_INS = ["x", "src", "dst", "edge_attr_128", "L0_gnn_W", "L0_gnn_b_W", "L0_gnn_W_e", "L0_gnn_b_We",
        "L1_gnn_W", "L1_gnn_b", "L1_gnn_gamma", "L1_gnn_beta"]


def kernel(**inputs):
    import numpy as np
    import concourse.bacc as bacc
    from concourse.bass_utils import run_bass_kernel_spmd

    nc = bacc.Bacc("TRN2", target_bir_lowering=False, num_devices=1)
    arrays, args = {}, []
    for name in _INS:
        a = np.ascontiguousarray(inputs[name])
        arrays[f"in_{name}"] = a
        args.append(nc.dram_tensor(f"in_{name}", a.shape, mybir.dt.from_np(a.dtype), kind="ExternalInput").ap())
    out = nc.dram_tensor("out_rows", inputs["x"].shape, F32, kind="ExternalOutput").ap()
    build(nc, *args, out)
    result = run_bass_kernel_spmd(nc, [arrays], core_ids=[0])
    return result.results[0]["out_rows"]
```

```python
import concourse.bass as bass
from concourse import mybir
from contextlib import ExitStack

F32 = mybir.dt.float32
BF16 = mybir.dt.bfloat16
F16 = mybir.dt.float16
I32 = mybir.dt.int32
ALU = mybir.AluOpType
ACT = mybir.ActivationFunctionType
AX = mybir.AxisListType

P = 128
F = 128
WN = 5
TILES = 2
WE = TILES * P
BN = 250
BW = BN // WN
PAIRS = BW // 2
GW = 125
EW = 63
EK = 4
EJ = 18
EE = EJ * P
RING = 5
HR = 500
GE = 125
GN = 512
LN_EPS = 1e-5
Z_SCALE = 4096.0


class Dims:
    def __init__(self, n, e):
        self.N, self.E = n, e
        self.HI = -(-n // P)
        self.NP = self.HI * P
        self.REM = n - (self.HI - 1) * P
        self.NB = n // BN
        self.NW = n // WN
        self.G = self.NW // GW
        self.R = e // HR
        self.CH = max(c for c in range(1, 8) if self.HI % c == 0 and self.HI // c % 2)
        self.NC = self.HI // self.CH
        assert n % BN == 0 and self.NW % GW == 0 and e % HR == 0 and e % GE == 0
        assert self.NB % 2 == 1 and self.NB * EK <= P and self.R <= 512 and WN * self.HI * 2 <= 512


class Steps:

    def __init__(self, engine, sem):
        self.engine, self.sem, self.n = engine, sem, 0

    def __call__(self, ins):
        self.n += 1
        ins.then_inc(self.sem, 1)
        self.engine.wait_ge(self.sem, self.n)


def reach(engine, sem, value):
    if not isinstance(value, int) or value > 0:
        engine.wait_ge(sem, value)


def wait_alone(engine, sem, value, passed):
    if not isinstance(value, int) or value > 0:
        engine.wait_ge(sem, value)
        engine.sem_inc(passed, 1)


def all_blocks(engine, nb, step):
    step(0, 0, -1)
    step(1, 1, 0)
    step(2, 0, 0)
    if nb > 3:
        with engine.Fori(1, (nb - 1) // 2) as i:
            step(i * 2 + 1, 1, i)
            step(i * 2 + 2, 0, i)


def all_turns(engine, n, step):
    step(0)
    if n > 1:
        with engine.Fori(1, n) as i:
            step(i)


def prepare(nc, d, x, src, dst, keep, scratch):
    xrows, xsplit, ident, flag, iota, key_t, lo_t, ekey_t, startrow, iota_e = (
        keep[k] for k in ("xrows", "xsplit", "ident", "flag", "iota", "key_t", "lo_t", "ekey_t",
                          "startrow", "iota_e"))
    N, E, HI, G, R, NB = d.N, d.E, d.HI, d.G, d.R, d.NB
    NE = NB * EK
    with ExitStack() as ctx:
        sb = lambda name, shape, dt: ctx.enter_context(nc.sbuf_tensor(name, shape, dt))
        sem = lambda name: ctx.enter_context(nc.semaphore(name))
        heads_i, heads = sb("heads_i", [1, R], I32), sb("heads", [1, R], F32)
        ones = sb("ones", [P, P], F32)
        iota_i, iota_ei = sb("iota_i", [P, 256], I32), sb("iota_ei", [P, EW], I32)
        th_i, th = sb("th_i", [P, G + 1], I32), sb("th", [P, G + 1], F32)
        e_b, e_k, e_w = sb("e_b", [P, 1], I32), sb("e_k", [P, 1], I32), sb("e_w", [P, 1], F32)
        cnt1, cnt2 = sb("cnt1", [P, G + 1], F32), sb("cnt2", [P, G + 1], F32)
        row_f, row_i = sb("row_f", [P, G + 1], F32), sb("row_i", [P, G + 1], I32)
        start_i = sb("start_i", [P, G + 1], I32)
        rows = sb("rows", [P, G + 1, HR], I32)
        junk = sb("junk", [P, max(G * WE, EE)], F32)
        gdst, gsrc = sb("gdst", [P, G, WE], I32), sb("gsrc", [P, G, WE], I32)
        edst = sb("edst", [P, EE], I32)
        edl = edst[:, :].bitcast(F32)
        dl, key = sb("dl", [P, G, WE], F32), sb("key", [P, G, WE], F32)
        spare = rows[:, :, :].rearrange("p g e -> p (g e)")
        hi_i, lo_i = (spare[:, k * G * WE:(k + 1) * G * WE].rearrange("p (g e) -> p g e", g=G) for k in range(2))
        lo = gdst[:, :, :].bitcast(F32)
        deg = sb("deg", [P, G, WN], F32)
        below, total = sb("below", [P, 2], F32), sb("total", [P, 2], F32)
        ok, ok1 = sb("ok", [1, 2], F32), sb("ok1", [1, 1], F32)
        zpad = sb("zpad", [1, P], F32)
        part = sb("part", [P, HI, F], F32)
        heads_ps = ctx.enter_context(nc.psum_tensor("heads_ps", [P, 512], F32))
        total_ps = ctx.enter_context(nc.psum_tensor("total_ps", [P, 2], F32))
        tps = [ctx.enter_context(nc.psum_tensor(f"tps{i}", [P, 4, P], F32)) for i in range(4)]

        heads_in, x_cleared, x_in = sem("heads_in"), sem("x_cleared"), sem("x_in")
        consts, vstep, pstep = sem("consts"), sem("prep_vector_step"), sem("prep_pool_step")
        heads_f, heads_out = sem("heads_float"), sem("heads_broadcast")
        rows_known, starts_known = sem("rows_known"), sem("starts_known")
        row_in = [sem(f"row_in{g}") for g in range(G + 1)]
        dst_in, src_in, edst_in = sem("window_dst_in"), sem("window_src_in"), sem("edge_window_dst_in")
        keys_ready, lo_ready, ekeys_ready = sem("keys_ready"), sem("lo_ready"), sem("edge_keys_ready")
        lo_int = sem("lo_int")
        turned, tabled = sem("transposed"), sem("tabled")
        deg_ready, totals_ready, totals_out = sem("deg_ready"), sem("totals_ready"), sem("totals_out")
        start_out, start_back, deg_out = sem("start_out"), sem("start_back"), sem("deg_out")
        hi_cast, mid_cast, rest1 = sem("x_hi"), sem("x_mid"), sem("x_rest")
        block = ctx.enter_context(nc.Block())
        EBANKS = -(-EJ // 4)

        @block.sync
        def _(sp):
            sp.dma_start(heads_i[:, :], dst.rearrange("(r c) -> c r", c=HR)[0:1, :],
                         allow_slow_non_contiguous=True).then_inc(heads_in, 16)
            sp.dma_start(xrows[:, 0:HI - 1, :],
                         x[0:(HI - 1) * P, :].rearrange("(h p) f -> p h f", p=P)).then_inc(x_in, 16)
            sp.wait_ge(x_cleared, 1)
            sp.dma_start(xrows[0:d.REM, HI - 1, :], x[(HI - 1) * P:N, :]).then_inc(x_in, 16)
            sp.wait_ge(starts_known, 1)
            sp.dma_start(scratch["starts"], start_i[0:NE, G:G + 1]).then_inc(start_out, 16)
            sp.wait_ge(start_out, 16)
            sp.dma_start(startrow[:, :], scratch["starts"].rearrange("n o -> o n")).then_inc(start_back, 16)
            sp.wait_ge(deg_ready, 1)
            sp.dma_start(scratch["deg"][0:N].rearrange("(g p k) -> p g k", p=GW, k=WN),
                         deg[0:GW, :, :]).then_inc(deg_out, 16)
            sp.dma_start(scratch["deg"][N:d.NP].rearrange("(o n) -> o n", o=1),
                         zpad[:, 0:d.NP - N]).then_inc(deg_out, 16)
            sp.wait_ge(start_back, 16)
            sp.wait_ge(deg_out, 32)

        @block.gpsimd
        def _(pool):
            step = Steps(pool, pstep)
            nc.gpsimd.memset(xrows[:, HI - 1, :], 0.0).then_inc(x_cleared, 1)
            step(nc.gpsimd.memset(ident[:, :], 0.0))
            nc.gpsimd.affine_select(out=ident[:, :], in_=ident[:, :], compare_op=ALU.not_equal, fill=1.0,
                                    base=0, pattern=[[-1, P]], channel_multiplier=1).then_inc(consts, 1)
            nc.gpsimd.memset(ones[:, :], 1.0).then_inc(consts, 1)
            nc.gpsimd.iota(th_i[:, 0:G], pattern=[[WN * GW, G]], base=0, channel_multiplier=WN).then_inc(consts, 1)
            nc.gpsimd.iota(th_i[:, G:G + 1], pattern=[[0, 1]], base=0, channel_multiplier=1).then_inc(consts, 1)
            nc.gpsimd.iota(iota_i[:, :], pattern=[[1, 256]], base=0, channel_multiplier=0).then_inc(consts, 1)
            nc.gpsimd.iota(iota_ei[:, :], pattern=[[1, EW]], base=0, channel_multiplier=0).then_inc(consts, 1)
            nc.gpsimd.memset(zpad[:, :], 0.0).then_inc(consts, 1)
            pool.wait_ge(rows_known, 1)
            flat_dst, flat_src = dst.rearrange("(n o) -> n o", o=1), src.rearrange("(n o) -> n o", o=1)

            def gather(out, table, at, done):
                nc.gpsimd.indirect_dma_start(
                    out=out, out_offset=None, in_=table,
                    in_offset=bass.IndirectOffsetOnAxis(ap=at, axis=0)).then_inc(done, 16)

            for g in range(G):
                gather(rows[0:GW, g, :], flat_dst, row_i[0:GW, g:g + 1], row_in[g])
            gather(rows[0:NE, G, :], flat_dst, row_i[0:NE, G:G + 1], row_in[G])
            pool.wait_ge(starts_known, 1)
            for g in range(G):
                gather(gdst[0:GW, g, :], flat_dst, start_i[0:GW, g:g + 1], dst_in)
            for g in range(G):
                gather(gsrc[0:GW, g, :], flat_src, start_i[0:GW, g:g + 1], src_in)
            gather(edst[0:NE, :], flat_dst, start_i[0:NE, G:G + 1], edst_in)

        @block.vector
        def _(dve):
            step = Steps(dve, vstep)
            v = nc.vector
            dve.wait_ge(heads_in, 16)
            v.tensor_copy(heads[:, :], heads_i[:, :]).then_inc(heads_f, 1)
            dve.wait_ge(consts, 7)
            v.tensor_copy(iota[:, :], iota_i[:, :])
            v.tensor_copy(iota_e[:, :], iota_ei[:, :])
            v.tensor_copy(th[:, 0:G], th_i[:, 0:G])
            v.memset(total[:, :], 0.0)
            v.tensor_scalar(e_b[:, :], th_i[:, G:G + 1], 2, None, ALU.logical_shift_right)
            v.tensor_scalar(e_k[:, :], th_i[:, G:G + 1], 3, None, ALU.bitwise_and)
            step(v.tensor_scalar(th[:, G:G + 1], th_i[:, G:G + 1], float(EW), None, ALU.mult))
            step(v.scalar_tensor_tensor(out=th[:, G:G + 1], in0=e_b[:, :], scalar=float(BN - EK * EW),
                                        in1=th[:, G:G + 1], op0=ALU.mult, op1=ALU.add))
            step(v.tensor_scalar(e_w[:, :], e_k[:, :], float(EK - 1), float(BN - EK * EW), ALU.is_equal, ALU.mult))
            step(v.tensor_scalar(e_w[:, :], e_w[:, :], float(EW), None, ALU.add))
            dve.wait_ge(heads_out, 1)
            for g in range(G + 1):
                n = GW if g < G else NE
                step(v.tensor_scalar(junk[0:n, 0:R], heads_ps[0:n, 0:R], th[0:n, g:g + 1], 0.0, ALU.is_lt,
                                     ALU.add, accum_out=cnt1[0:n, g:g + 1]))

            def each(f):
                f(slice(0, GW), slice(0, G))
                f(slice(0, NE), slice(G, G + 1))
                step(v.memset(junk[0:1, 0:1], 0.0))

            each(lambda p, c: v.tensor_scalar(row_f[p, c], cnt1[p, c], -1.0, 0.0, ALU.add, ALU.max))
            each(lambda p, c: v.tensor_scalar(row_f[p, c], row_f[p, c], float(HR), None, ALU.mult))
            each(lambda p, c: v.tensor_copy(row_i[p, c], row_f[p, c]))
            dve.sem_inc(rows_known, 1)
            for g in range(G + 1):
                n = GW if g < G else NE
                dve.wait_ge(row_in[g], 16)
                step(v.tensor_scalar(junk[0:n, 0:HR], rows[0:n, g, :], th[0:n, g:g + 1], 0.0, ALU.is_lt,
                                     ALU.add, accum_out=cnt2[0:n, g:g + 1]))
            each(lambda p, c: v.tensor_tensor(row_f[p, c], row_f[p, c], cnt2[p, c], ALU.add))
            step(v.tensor_scalar(start_i[0:GW, 0:G], row_f[0:GW, 0:G], float(E - WE), None, ALU.min))
            step(v.tensor_scalar(start_i[0:NE, G:G + 1], row_f[0:NE, G:G + 1], float(E - EE), None, ALU.min))
            dve.sem_inc(starts_known, 1)
            dve.wait_ge(x_in, 32)
            dve.wait_ge(hi_cast, 1)
            v.tensor_tensor(part[:, :, :], xrows[:, :, :], xsplit[:, :, 0, :], ALU.subtract).then_inc(rest1, 1)
            dve.wait_ge(dst_in, 16 * G)
            thb = th[0:GW, 0:G].unsqueeze(2).to_broadcast([GW, G, WE])
            step(v.tensor_tensor(dl[0:GW, :, :], gdst[0:GW, :, :], thb, ALU.subtract))
            dve.wait_ge(src_in, 16 * G)
            v.tensor_scalar(lo_i[0:GW, :, :], gsrc[0:GW, :, :], P - 1, None, ALU.bitwise_and).then_inc(lo_int, 1)
            step(v.tensor_scalar(hi_i[0:GW, :, :], gsrc[0:GW, :, :], 7, None, ALU.logical_shift_right))
            v.scalar_tensor_tensor(out=key[0:GW, :, :], in0=dl[0:GW, :, :], scalar=float(HI),
                                   in1=hi_i[0:GW, :, :], op0=ALU.mult, op1=ALU.add).then_inc(keys_ready, 1)
            dve.wait_ge(edst_in, 16)
            v.tensor_scalar(edl[0:NE, :], edst[0:NE, :], th[0:NE, G:G + 1], None, ALU.subtract)\
             .then_inc(ekeys_ready, 1)
            jw = junk[0:GW, 0:G * WE].rearrange("p (g e) -> p g e", g=G)
            for k in range(WN):
                step(v.tensor_scalar(jw, dl[0:GW, :, :], float(k), None, ALU.is_equal))
                step(v.tensor_reduce(out=deg[0:GW, :, k], in_=jw, axis=AX.X, op=ALU.add))
            dve.sem_inc(deg_ready, 1)
            dve.wait_ge(ekeys_ready, 1)
            step(v.tensor_scalar(junk[0:NE, 0:EE], edl[0:NE, :], 0.0, 0.0, ALU.is_lt, ALU.add,
                                 accum_out=below[0:NE, 0:1]))
            step(v.tensor_scalar(junk[0:NE, 0:EE], edl[0:NE, :], e_w[0:NE, 0:1], 0.0, ALU.is_lt, ALU.add,
                                 accum_out=below[0:NE, 1:2]))
            step(v.tensor_tensor(total[0:NE, 1:2], below[0:NE, 1:2], below[0:NE, 0:1], ALU.subtract))
            step(v.tensor_reduce(out=total[0:GW, 0:1], in_=deg[0:GW, :, :], axis=AX.XY, op=ALU.add))
            dve.sem_inc(totals_ready, 1)
            dve.wait_ge(hi_cast, 2)
            v.tensor_tensor(xsplit[:, :, 2, :], part[:, :, :], xsplit[:, :, 1, :], ALU.subtract)
            dve.wait_ge(totals_out, 1)
            step(v.tensor_scalar(ok[:, :], total_ps[0:1, 0:2], float(E), None, ALU.is_equal))
            step(v.tensor_tensor(ok1[:, :], ok[:, 0:1], ok[:, 1:2], ALU.mult))
            step(v.tensor_copy(flag[:, :], ok1[:, :]))

        @block.scalar
        def _(act):
            act.wait_ge(x_in, 32)
            nc.scalar.copy(xsplit[:, :, 0, :], xrows[:, :, :]).then_inc(hi_cast, 1)
            act.wait_ge(rest1, 1)
            nc.scalar.copy(xsplit[:, :, 1, :], part[:, :, :]).then_inc(hi_cast, 1)
            act.wait_ge(lo_int, 1)
            nc.scalar.copy(lo[0:GW, :, :], lo_i[0:GW, :, :]).then_inc(lo_ready, 1)
            for g in range(G):
                act.wait_ge(turned, g + 1)
                for q, table in enumerate((key_t, lo_t)):
                    nc.scalar.copy(
                        table[:, g * GW * TILES:(g + 1) * GW * TILES].rearrange("p (w t) -> p t w", t=TILES),
                        tps[g % 4][:, TILES * q:TILES * q + TILES, 0:GW]).then_inc(tabled, 1)
            for m in range(EBANKS):
                act.wait_ge(turned, G + m + 1)
                n = min(4, EJ - 4 * m)
                nc.scalar.copy(ekey_t[:, :, 4 * m:4 * m + n].rearrange("p w j -> p j w"),
                               tps[(G + m) % 4][:, 0:n, 0:NE]).then_inc(tabled, 2)

        @block.tensor
        def _(pe):
            pe.wait_ge(heads_f, 1)
            pe.wait_ge(consts, 2)
            nc.tensor.matmul(heads_ps[:, 0:R], ones[0:1, :], heads[0:1, :], start=True, stop=True)\
              .then_inc(heads_out, 1)
            pe.wait_ge(keys_ready, 1)
            pe.wait_ge(lo_ready, 1)
            for g in range(G):
                if g >= 4:
                    pe.wait_ge(tabled, 2 * (g - 3))
                for q, t in ((0, 0), (0, 1), (1, 0), (1, 1)):
                    of = (key, lo)[q]
                    last = nc.tensor.transpose(tps[g % 4][:, 2 * q + t, 0:GW],
                                               of[0:GW, g, t * P:(t + 1) * P], ident[0:GW, 0:GW])
                last.then_inc(turned, 1)
            pe.wait_ge(ekeys_ready, 1)
            by_edge = edl[0:NE, :].rearrange("w (p j) -> w j p", j=EJ)
            for m in range(EBANKS):
                if G + m >= 4:
                    pe.wait_ge(tabled, 2 * (G + m - 3))
                for j in range(4 * m, min(4 * m + 4, EJ)):
                    last = nc.tensor.transpose(tps[(G + m) % 4][:, j - 4 * m, 0:NE], by_edge[:, j, :],
                                               ident[0:NE, 0:NE])
                last.then_inc(turned, 1)
            pe.wait_ge(totals_ready, 1)
            nc.tensor.matmul(total_ps[0:1, 0:2], ones[:, 0:1], total[:, :], start=True, stop=True)\
              .then_inc(totals_out, 1)


def aggregate_fast(nc, d, ea, keep, scratch):
    xsplit, flag, iota, key_t, lo_t, ekey_t, startrow, iota_e = (
        keep[k] for k in ("xsplit", "flag", "iota", "key_t", "lo_t", "ekey_t", "startrow", "iota_e"))
    HI, NB, E = d.HI, d.NB, d.E
    KW = WN * HI
    PRODUCTS = 3 * HI
    PER = -(-PRODUCTS // PAIRS)
    NT = TILES * BW
    with ExitStack() as ctx:
        sb = lambda name, shape, dt: ctx.enter_context(nc.sbuf_tensor(name, shape, dt))
        ps = lambda name: ctx.enter_context(nc.psum_tensor(name, [P, 512], F32))
        sem = lambda name: ctx.enter_context(nc.semaphore(name))
        counts = [sb(f"counts{i}", [P, HI, BN], BF16) for i in range(2)]
        key_oh = sb("key_oh", [P, RING, 4, 256], BF16)
        lo_oh = sb("lo_oh", [P, RING, 4, P], BF16)
        ebuf = [sb(f"ebuf{i}", [P, EJ, F], F32) for i in range(EK)]
        e_oh = [sb(f"e_oh{i}", [P, EJ, EW], F32) for i in range(2)]
        keys = [sb(f"keys{i}", [P, NT], F32) for i in range(2)]
        los = [sb(f"los{i}", [P, NT], F32) for i in range(2)]
        ekeys = [sb(f"ekeys{i}", [P, EK, EJ], F32) for i in range(2)]
        sx = [sb(f"sx{i}", [P, BN], F32) for i in range(2)]
        se = [sb(f"se{i}", [P, BN], F32) for i in range(2)]
        pair_ps = [ps(f"pair_ps{i}") for i in range(RING)]
        e_ps = ps("e_ps")
        x_ps = ps("x_ps")

        block_keys = sem("block_keys")
        key_hot, lo_hot, lo_hot_pool = sem("key_hot"), sem("lo_hot"), sem("lo_hot_pool")
        pair_built, pair_out = sem("pair_built"), sem("pair_out")
        e_hot, e_summed = sem("e_hot"), sem("e_summed")
        e_in = [sem(f"e_in{i}") for i in range(EK)]
        sp_passed, pool_passed = sem("sp_passed"), sem("pool_passed")
        product_done, sx_out, se_out = sem("product_done"), sem("sx_out"), sem("se_out")
        counts_kept = [sem(f"counts_kept{i}") for i in range(2)]
        sx_kept = [sem(f"sx_kept{i}") for i in range(2)]
        se_kept = [sem(f"se_kept{i}") for i in range(2)]
        block = ctx.enter_context(nc.Block())

        @block.sync
        def _(sp):
            fast = sp.value_load(flag[0:1, 0:1], min_val=0, max_val=1)
            with sp.If(fast > 0):
                def step(b, par, i):
                    for k in range(EK):
                        wait_alone(sp, e_summed, (b - 1) * EK + k + 1, sp_passed)
                        at = sp.value_load(startrow[0:1, bass.ds(b * EK + k, 1)], min_val=0, max_val=E - EE)
                        sp.dma_start(ebuf[k][:, :, :].rearrange("p j f -> p (j f)"),
                                     ea[bass.ds(at, EE), :].rearrange("(p j) f -> p (j f)", j=EJ))\
                          .then_inc(e_in[k], 16)
                all_blocks(sp, NB, step)

        @block.gpsimd
        def _(pool):
            fast = pool.value_load(flag[0:1, 0:1], min_val=0, max_val=1)
            with pool.If(fast > 0):
                def step(b, par, i):
                    nc.gpsimd.tensor_copy(keys[par][:, :], key_t[:, bass.ds(b * NT, NT)]).then_inc(block_keys, 1)
                    nc.gpsimd.tensor_copy(los[par][:, :], lo_t[:, bass.ds(b * NT, NT)]).then_inc(block_keys, 1)
                    nc.gpsimd.tensor_copy(ekeys[par][:, :, :], ekey_t[:, bass.ds(b * EK, EK), :])\
                      .then_inc(block_keys, 1)
                    wait_alone(pool, block_keys, b * 3 + 3, pool_passed)
                    for p in range(PAIRS):
                        wait_alone(pool, pair_built, b * PAIRS + (p + 1 - RING), pool_passed)
                        for w in range(2):
                            c = (2 * p + w) * TILES + 1
                            last = nc.gpsimd.tensor_scalar(lo_oh[:, p % RING, 2 * w + 1, :], iota[:, 0:P],
                                                           los[par][:, c:c + 1], None, ALU.is_equal)
                        last.then_inc(lo_hot_pool, 1)
                all_blocks(pool, NB, step)

        @block.vector
        def _(dve):
            fast = dve.value_load(flag[0:1, 0:1], min_val=0, max_val=1)
            with dve.If(fast > 0):
                def step(b, par, i):
                    dve.wait_ge(block_keys, b * 3 + 3)
                    for p in range(PAIRS):
                        reach(dve, pair_built, b * PAIRS + (p + 1 - RING))
                        for w in range(2):
                            c = (2 * p + w) * TILES
                            nc.vector.tensor_scalar(lo_oh[:, p % RING, 2 * w, :], iota[:, 0:P],
                                                    los[par][:, c:c + 1], None, ALU.is_equal)
                            for t in range(TILES):
                                last = nc.vector.tensor_scalar(
                                    key_oh[:, p % RING, 2 * w + t, 0:KW], iota[:, 0:KW],
                                    keys[par][:, c + t:c + t + 1], None, ALU.is_equal)
                        last.then_inc(key_hot, 1)
                        if p % 6 == 0 and p // 6 < EK:
                            k = p // 6
                            reach(dve, e_summed, b * EK + (k - 1))
                            nc.vector.tensor_tensor(
                                e_oh[k % 2][:, :, :], iota_e[:, :].unsqueeze(1).to_broadcast([P, EJ, EW]),
                                ekeys[par][:, k, :].unsqueeze(2).to_broadcast([P, EJ, EW]), ALU.is_equal)\
                              .then_inc(e_hot, 1)
                all_blocks(dve, NB, step)

        @block.tensor
        def _(pe):
            fast = pe.value_load(flag[0:1, 0:1], min_val=0, max_val=1)
            with pe.If(fast > 0):
                def product(b, par, p):
                    if p == 0:
                        pe.wait_ge(pair_out, b * PAIRS)
                    for q in range(PER * p, min(PER * (p + 1), PRODUCTS)):
                        last = nc.tensor.matmul(x_ps[:, 0:BN], xsplit[:, q // 3, q % 3, :],
                                                counts[1 - par][:, q // 3, :],
                                                start=(q == 0), stop=(q == PRODUCTS - 1))
                        if q == PRODUCTS - 1:
                            last.then_inc(product_done, 1)

                def step(b, par, i):
                    for p in range(PAIRS):
                        pe.wait_ge(key_hot, b * PAIRS + p + 1)
                        pe.wait_ge(lo_hot_pool, b * PAIRS + p + 1)
                        reach(pe, pair_out, b * PAIRS + (p + 1 - RING))
                        for w in range(2):
                            for t in range(TILES):
                                last = nc.tensor.matmul(pair_ps[p % RING][:, w * KW:(w + 1) * KW],
                                                        lo_oh[:, p % RING, 2 * w + t, :],
                                                        key_oh[:, p % RING, 2 * w + t, 0:KW],
                                                        start=(t == 0), stop=(t == TILES - 1))
                        last.then_inc(pair_built, 1)
                        if p >= 1:
                            k, part = (p - 1) // 6, (p - 1) % 6
                            if part == 0:
                                pe.wait_ge(e_hot, b * EK + k + 1)
                                pe.wait_ge(e_in[k], b * 16 + 16)
                            if k == 0 and part == 0:
                                reach(pe, se_out, b)
                            n = EW if k < EK - 1 else BN - EW * (EK - 1)
                            for j in range(3 * part, 3 * part + 3):
                                last = nc.tensor.matmul(e_ps[:, EW * k:EW * k + n], ebuf[k][:, j, :],
                                                        e_oh[k % 2][:, j, 0:n], start=(j == 0),
                                                        stop=(j == EJ - 1))
                            if part == 5:
                                last.then_inc(e_summed, 1)
                        if not (isinstance(b, int) and b == 0):
                            if p == 0:
                                reach(pe, sx_out, b - 1)
                            product(b, par, p)
                all_blocks(pe, NB, step)
                pe.wait_ge(sx_out, NB - 1)
                for p in range(PAIRS):
                    product(NB, NB % 2, p)

        @block.scalar
        def _(act):
            fast = act.value_load(flag[0:1, 0:1], min_val=0, max_val=1)
            with act.If(fast > 0):
                def product_out(b, par, old):
                    act.wait_ge(product_done, b)
                    reach(act, sx_kept[1 - par], old)
                    nc.scalar.copy(sx[1 - par][:, :], x_ps[:, 0:BN]).then_inc(sx_out, 1)
                    act.wait_ge(sx_out, b)
                    act.dma_start(scratch["sx"][:, bass.ds((b - 1) * BN, BN)], sx[1 - par][:, :])\
                       .then_inc(sx_kept[1 - par], 16)

                def step(b, par, i):
                    reach(act, product_done, b - 1)
                    reach(act, counts_kept[par], i * 16 if par else i * 16 + 16)
                    for p in range(PAIRS):
                        act.wait_ge(pair_built, b * PAIRS + p + 1)
                        nc.scalar.copy(counts[par][:, :, 2 * WN * p:2 * WN * (p + 1)],
                                       pair_ps[p % RING][:, 0:2 * KW].rearrange("p (n h) -> p h n", h=HI))\
                          .then_inc(pair_out, 1)
                    act.wait_ge(pair_out, (b + 1) * PAIRS)
                    act.dma_start(scratch["counts"][bass.ds(b * P, P), :],
                                  counts[par][:, :, :].rearrange("p h n -> p (h n)"))\
                       .then_inc(counts_kept[par], 16)
                    act.wait_ge(e_summed, (b + 1) * EK)
                    reach(act, se_kept[par], i * 16 if par else i * 16 + 16)
                    nc.scalar.copy(se[par][:, :], e_ps[:, 0:BN]).then_inc(se_out, 1)
                    act.wait_ge(se_out, b + 1)
                    act.dma_start(scratch["se"][:, bass.ds(b * BN, BN)], se[par][:, :])\
                       .then_inc(se_kept[par], 16)
                    if not (isinstance(b, int) and b == 0):
                        product_out(b, par, i * 16)
                all_blocks(act, NB, step)
                product_out(NB, NB % 2, (NB - 1) // 2 * 16)
                half = (NB - 1) // 2 * 16
                for kept in (counts_kept, se_kept, sx_kept):
                    act.wait_ge(kept[0], half + 16)
                    act.wait_ge(kept[1], half)


def project(nc, d, fast, keep, scratch):
    zsplit, flag, zT, y, dinv, w, vec, stats = (
        keep[k] for k in ("zsplit", "flag", "zT", "y", "dinv", "w1", "vec", "stats"))
    HI, NB = d.HI, d.NB
    PRODUCTS = 2 * HI
    name = "fast1" if fast else "any1"
    with ExitStack() as ctx:
        sb = lambda n, shape, dt: ctx.enter_context(nc.sbuf_tensor(f"{name}_{n}", shape, dt))
        ps = lambda n: ctx.enter_context(nc.psum_tensor(f"{name}_{n}", [P, 512], F32))
        sem = lambda n: ctx.enter_context(nc.semaphore(f"{name}_{n}"))
        if fast:
            counts = [sb(f"counts{i}", [P, HI, BN], BF16) for i in range(2)]
        else:
            sums = [sb(f"sums{i}", [P, BN], F32) for i in range(2)]
        s1 = [sb(f"s1_{i}", [P, BN], F32) for i in range(2)]
        z_ps = [ps(f"z{i}") for i in range(2)]
        y_ps = [ps(f"y{i}") for i in range(2)]
        block_in = [sem(f"block_in{i}") for i in range(2)]
        multiplied, s1_ready, projected = sem("multiplied"), sem("s1_ready"), sem("projected")
        scaled, biased, counted, sp_passed = sem("scaled"), sem("biased"), sem("counted"), sem("sp_passed")
        block = ctx.enter_context(nc.Block())
        ours = lambda loaded: (loaded > 0) if fast else (loaded < 1)
        cols = lambda b: bass.ds(b * BN, BN)

        @block.sync
        def _(sp):
            on = sp.value_load(flag[0:1, 0:1], min_val=0, max_val=1)
            with sp.If(ours(on)):
                def step(b, par, i):
                    if fast:
                        wait_alone(sp, multiplied, b - 1, sp_passed)
                        sp.dma_start(counts[par][:, :, :].rearrange("p h n -> p (h n)"),
                                     scratch["counts"][bass.ds(b * P, P), :]).then_inc(block_in[par], 16)
                    else:
                        wait_alone(sp, s1_ready, b - 1, sp_passed)
                        sp.dma_start(sums[par][:, :], scratch["s1"][:, cols(b)]).then_inc(block_in[par], 16)
                all_blocks(sp, NB, step)

        @block.tensor
        def _(pe):
            on = pe.value_load(flag[0:1, 0:1], min_val=0, max_val=1)
            with pe.If(ours(on)):
                def weights(b, par):
                    pe.wait_ge(s1_ready, b)
                    reach(pe, scaled, b - 2)
                    nc.tensor.matmul(y_ps[1 - par][:, 0:BN], w[:, :], s1[1 - par][:, :], start=True, stop=True)\
                      .then_inc(projected, 1)

                def step(b, par, i):
                    if fast:
                        pe.wait_ge(block_in[par], i * 16 + (16 if par else 32))
                        reach(pe, s1_ready, b - 1)
                        for q in range(PRODUCTS):
                            last = nc.tensor.matmul(z_ps[par][:, 0:BN], zsplit[:, q // 2, q % 2, :],
                                                    counts[par][:, q // 2, :],
                                                    start=(q == 0), stop=(q == PRODUCTS - 1))
                        last.then_inc(multiplied, 1)
                    if not (isinstance(b, int) and b == 0):
                        weights(b, par)
                all_blocks(pe, NB, step)
                weights(NB, NB % 2)

        @block.vector
        def _(dve):
            on = dve.value_load(flag[0:1, 0:1], min_val=0, max_val=1)
            with dve.If(ours(on)):
                def finish(b, par):
                    dve.wait_ge(projected, b)
                    nc.vector.tensor_tensor(y[:, cols(b - 1)], y_ps[1 - par][:, 0:BN], dinv[:, cols(b - 1)],
                                            ALU.mult).then_inc(scaled, 1)
                    dve.wait_ge(biased, b)
                    nc.vector.bn_stats(stats[:, bass.ds((b - 1) * 6, 6)], y[:, cols(b - 1)]).then_inc(counted, 1)

                def step(b, par, i):
                    reach(dve, projected, b - 1)
                    if fast:
                        dve.wait_ge(multiplied, b + 1)
                        nc.vector.scalar_tensor_tensor(out=s1[par][:, :], in0=z_ps[par][:, 0:BN],
                                                       scalar=1.0 / Z_SCALE, in1=zT[:, cols(b)],
                                                       op0=ALU.mult, op1=ALU.add).then_inc(s1_ready, 1)
                    else:
                        dve.wait_ge(block_in[par], i * 16 + (16 if par else 32))
                        nc.vector.tensor_tensor(s1[par][:, :], sums[par][:, :], zT[:, cols(b)], ALU.add)\
                          .then_inc(s1_ready, 1)
                    if not (isinstance(b, int) and b == 0):
                        finish(b, par)
                all_blocks(dve, NB, step)
                finish(NB, NB % 2)
                dve.wait_ge(counted, NB)

        @block.scalar
        def _(act):
            on = act.value_load(flag[0:1, 0:1], min_val=0, max_val=1)
            with act.If(ours(on)):
                def turn(b):
                    act.wait_ge(scaled, b + 1)
                    nc.scalar.activation(y[:, cols(b)], y[:, cols(b)], ACT.Identity, bias=vec[:, 0:1])\
                      .then_inc(biased, 1)
                all_turns(act, NB, turn)


def aggregate_any(nc, d, name, table, ea, src, dst, keep, sum_out, esum_out, deg_out):
    flag = keep["flag"]
    N, E = d.N, d.E
    GR = -(-N // GN)
    NT = E // GE
    kinds = 3 if ea is not None else 1
    with ExitStack() as ctx:
        sb = lambda n, shape, dt: ctx.enter_context(nc.sbuf_tensor(f"{name}_{n}", shape, dt))
        sem = lambda n: ctx.enter_context(nc.semaphore(f"{name}_{n}"))
        acc = [sb(f"acc{k}", [P, GR * GN], F32) for k in range(kinds)]
        data = [sb(f"data{k}", [P, F], F32) for k in range(kinds)]
        ones = data[2] if kinds == 3 else None
        src_i, dst_i, dst_f = sb("src_i", [P, 1], I32), sb("dst_i", [P, 1], I32), sb("dst_f", [P, 1], F32)
        node_i, node = sb("node_i", [P, GR * GN], I32), sb("node", [P, GR * GN], F32)
        hot = [sb(f"hot{i}", [P, GN], F32) for i in range(2)]
        sums = [[ctx.enter_context(nc.psum_tensor(f"{name}_sum{k}_{i}", [P, 512], F32)) for i in range(2)]
                for k in range(kinds)]
        idx_in, row_in, ea_in, ready = sem("idx_in"), sem("row_in"), sem("ea_in"), sem("ready")
        made, cast, summed, added, stored = sem("made"), sem("cast"), sem("summed"), sem("added"), sem("stored")
        nodes_made, pool_passed, sp_passed = sem("nodes_made"), sem("pool_passed"), sem("sp_passed")
        block = ctx.enter_context(nc.Block())

        @block.sync
        def _(sp):
            fast = sp.value_load(flag[0:1, 0:1], min_val=0, max_val=1)
            with sp.If(fast < 1):
                def turn(t):
                    wait_alone(sp, summed, t * GR, sp_passed)
                    wait_alone(sp, made, t * GR, sp_passed)
                    sp.dma_start(src_i[0:GE, :], src[bass.ds(t * GE, GE)].rearrange("(p o) -> p o", o=1))\
                      .then_inc(idx_in, 16)
                    sp.dma_start(dst_i[0:GE, :], dst[bass.ds(t * GE, GE)].rearrange("(p o) -> p o", o=1))\
                      .then_inc(idx_in, 16)
                    if kinds == 3:
                        sp.dma_start(data[1][0:GE, :], ea[bass.ds(t * GE, GE), :]).then_inc(ea_in, 16)
                    sp.wait_ge(idx_in, t * 32 + 32)
                    wait_alone(sp, row_in, t * 16 + 16, sp_passed)
                all_turns(sp, NT, turn)
                sp.wait_ge(added, NT * GR)
                sp.dma_start(sum_out[:, 0:N], acc[0][:, 0:N]).then_inc(stored, 16)
                if kinds == 3:
                    sp.dma_start(esum_out[:, 0:N], acc[1][:, 0:N]).then_inc(stored, 16)
                    sp.dma_start(deg_out[0:N].rearrange("(o n) -> o n", o=1), acc[2][0:1, 0:N])\
                      .then_inc(stored, 16)
                sp.wait_ge(stored, 16 * kinds)

        @block.gpsimd
        def _(pool):
            fast = pool.value_load(flag[0:1, 0:1], min_val=0, max_val=1)
            with pool.If(fast < 1):
                nc.gpsimd.iota(node_i[:, :], pattern=[[1, GR * GN]], base=0, channel_multiplier=0)\
                  .then_inc(nodes_made, 1)
                def turn(t):
                    wait_alone(pool, idx_in, t * 32 + 32, pool_passed)
                    nc.gpsimd.indirect_dma_start(
                        out=data[0][0:GE, :], out_offset=None, in_=table,
                        in_offset=bass.IndirectOffsetOnAxis(ap=src_i[0:GE, :], axis=0)).then_inc(row_in, 16)
                all_turns(pool, NT, turn)

        @block.vector
        def _(dve):
            fast = dve.value_load(flag[0:1, 0:1], min_val=0, max_val=1)
            with dve.If(fast < 1):
                for a in acc:
                    nc.vector.memset(a[:, :], 0.0).then_inc(ready, 1)
                if kinds == 3:
                    nc.vector.memset(ones[:, :], 1.0).then_inc(ready, 1)
                else:
                    dve.sem_inc(ready, 1)
                dve.wait_ge(nodes_made, 1)
                nc.vector.tensor_copy(node[:, :], node_i[:, :]).then_inc(ready, 1)
                dve.wait_ge(ready, kinds + 2)
                def turn(t):
                    dve.wait_ge(idx_in, t * 32 + 32)
                    nc.vector.tensor_copy(dst_f[0:GE, :], dst_i[0:GE, :]).then_inc(cast, 1)
                    dve.wait_ge(cast, t + 1)
                    for g in range(GR + 1):
                        if g < GR:
                            if g >= 2:
                                reach(dve, summed, t * GR + (g - 1))
                            nc.vector.tensor_scalar(hot[g % 2][0:GE, :], node[0:GE, g * GN:(g + 1) * GN],
                                                    dst_f[0:GE, 0:1], None, ALU.is_equal).then_inc(made, 1)
                        if g >= 1:
                            h = g - 1
                            dve.wait_ge(summed, t * GR + h + 1)
                            for k in range(kinds):
                                at = acc[k][:, h * GN:(h + 1) * GN]
                                last = nc.vector.tensor_tensor(at, at, sums[k][h % 2][:, :], ALU.add)
                            last.then_inc(added, 1)
                    dve.wait_ge(added, t * GR + GR)
                all_turns(dve, NT, turn)

        @block.tensor
        def _(pe):
            fast = pe.value_load(flag[0:1, 0:1], min_val=0, max_val=1)
            with pe.If(fast < 1):
                pe.wait_ge(ready, kinds + 2)
                def turn(t):
                    pe.wait_ge(row_in, t * 16 + 16)
                    if kinds == 3:
                        pe.wait_ge(ea_in, t * 16 + 16)
                    reach(pe, added, t * GR)
                    for g in range(GR):
                        pe.wait_ge(made, t * GR + g + 1)
                        if g >= 2:
                            reach(pe, added, t * GR + (g - 1))
                        for k in range(kinds):
                            last = nc.tensor.matmul(sums[k][g % 2][:, :], data[k][0:GE, :],
                                                    hot[g % 2][0:GE, :], start=True, stop=True)
                        last.then_inc(summed, 1)
                all_turns(pe, NT, turn)


def norm_rows(nc, step, x, v, out, small, ready_for_root, root_taken):
    mean, var, sq = small
    C, n = v.shape[1], v.shape[2]
    wide = lambda a: a[:, :].unsqueeze(2).to_broadcast([P, C, n])
    step(nc.vector.tensor_reduce(out=mean[:, :], in_=x, axis=AX.X, op=ALU.add))
    step(nc.vector.tensor_scalar(mean[:, :], mean[:, :], 1.0 / n, None, ALU.mult))
    step(nc.vector.tensor_tensor(v[:, :, :], x, wide(mean), ALU.subtract))
    step(nc.vector.tensor_tensor(sq[:, :, :], v[:, :, :], v[:, :, :], ALU.mult))
    step(nc.vector.tensor_reduce(out=var[:, :], in_=sq[:, :, :], axis=AX.X, op=ALU.add))
    step(nc.vector.tensor_scalar(var[:, :], var[:, :], 1.0 / n, LN_EPS, ALU.mult, ALU.add))
    ready_for_root()
    root_taken()
    step(nc.vector.reciprocal(var[:, :], var[:, :]))
    step(nc.vector.tensor_tensor(out, v[:, :, :], wide(var), ALU.mult))


NORM_STEPS = 8


class TurnSteps:

    def __init__(self, engine, sem, turn, per_turn):
        self.engine, self.sem, self.turn, self.per, self.n = engine, sem, turn, per_turn, 0

    def __call__(self, ins):
        self.n += 1
        assert self.n <= self.per
        ins.then_inc(self.sem, 1)
        self.engine.wait_ge(self.sem, self.turn * self.per + self.n)


def halves(C):
    return [(h, 4 * h, min(4, C - 4 * h)) for h in range(2) if C > 4 * h]


def update_first(nc, d, W, bW, We, bWe, keep, scratch):
    xrows, zsplit, ident, zT = (keep[k] for k in ("xrows", "zsplit", "ident", "zT"))
    HI, C, NCH, NP, N = d.HI, d.CH, d.NC, d.NP, d.N
    HS = halves(C)
    with ExitStack() as ctx:
        sb = lambda n, shape, dt: ctx.enter_context(nc.sbuf_tensor(f"u0_{n}", shape, dt))
        sem = lambda n: ctx.enter_context(nc.semaphore(f"u0_{n}"))
        wi, wj, we = sb("wi", [P, F], F32), sb("wj", [P, F], F32), sb("we", [P, F], F32)
        bi, bj, bje, be = (sb(n, [1, F], F32) for n in ("bi", "bj", "bje", "be"))
        ones, zero = sb("ones", [1, P], F32), sb("zero", [P, P], F32)
        deg, rdeg, dinv = sb("deg", [P, HI], F32), sb("rdeg", [P, HI], F32), sb("dinv", [P, HI], F32)
        rdc = sb("rdc", [P, C], F32)
        sxc, sec = ([sb(f"{n}{i}", [P, C, P], F32) for i in range(2)] for n in ("sxc", "sec"))
        degrow = [sb(f"degrow{i}", [1, C, P], F32) for i in range(2)]
        xc, xT = [sb(f"xc{i}", [P, C, F], F32) for i in range(2)], sb("xT", [P, C, P], F32)
        msg, own = sb("msg", [P, C, F], F32), sb("own", [P, C, F], F32)
        v, sq, z = (sb(n, [P, C, F], F32) for n in ("v", "sq", "z"))
        mean, var = sb("mean", [P, C], F32), sb("var", [P, C], F32)
        t_ps, i_ps, j_ps, z_ps = (
            [ctx.enter_context(nc.psum_tensor(f"u0_{n}{k}", [P, 4, P], F32)) for k in range(2)]
            for n in ("t", "i", "j", "z"))
        w_in, deg_in, ready, cols_done = sem("w_in"), sem("deg_in"), sem("ready"), sem("cols_done")
        pads, dinv_out, root, pre = sem("pads_out"), sem("dinv_out"), sem("deg_root"), sem("pre_step")
        chunk_in = [sem(f"chunk_in{i}") for i in range(2)]
        x_copied, turned, turned_out, rdc_ready = sem("x_copied"), sem("turned"), sem("turned_out"), sem("rdc_ready")
        multiplied, msg_out, own_step, summed = sem("multiplied"), sem("msg_out"), sem("own_step"), sem("summed")
        norm_step, var_ready, std_ready = sem("norm_step"), sem("var_ready"), sem("std_ready")
        z_ready, high_ready, low_ready = sem("z_ready"), sem("high_ready"), sem("low_ready")
        z_turned, z_out, z_kept, sp_passed = sem("z_turned"), sem("z_turned_out"), sem("z_kept"), sem("sp_passed")
        dve_passed = sem("dve_passed")
        block = ctx.enter_context(nc.Block())
        bank = lambda pss, k: pss[k // 4][:, k % 4, :]
        chunk = lambda c: bass.ds(c * C, C)
        later = lambda c: not (isinstance(c, int) and c == 0)

        @block.sync
        def _(sp):
            row = lambda a: a.rearrange("(o n) -> o n", o=1)
            sp.dma_start(deg[:, :], scratch["deg"].rearrange("(h p) -> p h", p=P),
                         allow_slow_non_contiguous=True).then_inc(deg_in, 16)
            for out, in_ in ((wi[:, :], W[:, 0:F]), (wj[:, :], W[:, F:2 * F]), (we[:, :], We),
                             (bi[:, :], row(bW[0:F])), (bj[:, :], row(bW[F:2 * F])), (be[:, :], row(bWe))):
                sp.dma_start(out, in_).then_inc(w_in, 16)
            sp.wait_ge(ready, 1)
            sp.dma_start(scratch["sx"][:, N:NP], zero[:, 0:NP - N]).then_inc(pads, 16)
            sp.dma_start(scratch["se"][:, N:NP], zero[:, 0:NP - N]).then_inc(pads, 16)
            sp.wait_ge(pads, 32)

            def keep_z(c):
                wait_alone(sp, z_ready, c, sp_passed)
                sp.dma_start(scratch["z"][bass.ds((c - 1) * (C * P), C * P), :].rearrange("(c p) f -> p c f", p=P),
                             z[:, :, :]).then_inc(z_kept, 16)

            def step(c, par, i):
                wait_alone(sp, multiplied, c - 1, sp_passed)
                cols = bass.ds(c * (C * P), C * P)
                flat = lambda a: a[:, :, :].rearrange("p c n -> p (c n)")
                sp.dma_start(flat(sxc[par]), scratch["sx"][:, cols]).then_inc(chunk_in[par], 16)
                sp.dma_start(flat(sec[par]), scratch["se"][:, cols]).then_inc(chunk_in[par], 16)
                sp.dma_start(flat(degrow[par]), row(scratch["deg"][cols])).then_inc(chunk_in[par], 16)
                if later(c):
                    keep_z(c)
            all_blocks(sp, NCH, step)
            keep_z(NCH)
            sp.wait_ge(cols_done, 1)
            sp.dma_start(scratch["dinv"].rearrange("(h p) -> p h", p=P), dinv[:, :],
                         allow_slow_non_contiguous=True).then_inc(dinv_out, 16)
            sp.wait_ge(z_kept, NCH * 16)
            sp.wait_ge(dinv_out, 16)

        @block.scalar
        def _(act):
            act.wait_ge(root, 1)
            nc.scalar.activation(dinv[:, :], dinv[:, :], ACT.Sqrt).then_inc(root, 1)
            act.wait_ge(cols_done, 1)

            def norm_part(c):
                act.wait_ge(var_ready, c)
                nc.scalar.activation(var[:, :], var[:, :], ACT.Sqrt).then_inc(std_ready, 1)
                act.wait_ge(z_ready, c)
                nc.scalar.activation(zsplit[:, chunk(c - 1), 0, :], z[:, :, :], ACT.Copy, scale=Z_SCALE)\
                  .then_inc(high_ready, 1)

            def transpose_out(c):
                act.wait_ge(z_turned, c)
                for h, k, n in HS:
                    last = nc.scalar.copy(zT[:, bass.ds((c - 1) * (C * P) + k * P, n * P)]
                                          .rearrange("p (c n) -> p c n", n=P), z_ps[h][:, 0:n, :])
                last.then_inc(z_out, 1)

            def step(c, par, i):
                nc.scalar.copy(xc[par][:, :, :], xrows[:, chunk(c), :]).then_inc(x_copied, 1)
                reach(act, msg_out, c)
                nc.scalar.copy(rdc[:, :], rdeg[:, chunk(c)]).then_inc(rdc_ready, 1)
                act.wait_ge(turned, c + 1)
                reach(act, multiplied, c)
                for h, k, n in HS:
                    last = nc.scalar.copy(xT[:, k:k + n, :], t_ps[h][:, 0:n, :])
                last.then_inc(turned_out, 1)
                if later(c):
                    norm_part(c)
                act.wait_ge(multiplied, c + 1)
                act.wait_ge(rdc_ready, c + 1)
                reach(act, summed, c)
                for k in range(C):
                    last = nc.scalar.activation(msg[:, k, :], bank(j_ps, k), ACT.Copy, scale=rdc[:, k:k + 1])
                last.then_inc(msg_out, 1)
                if later(c):
                    transpose_out(c)
            all_blocks(act, NCH, step)
            norm_part(NCH)
            transpose_out(NCH)

        @block.vector
        def _(dve):
            vv = nc.vector
            pstep = Steps(dve, pre)
            pstep(vv.memset(zero[:, :], 0.0))
            dve.sem_inc(ready, 1)
            vv.memset(ones[:, :], 1.0).then_inc(ready, 1)
            dve.wait_ge(deg_in, 16)
            pstep(vv.tensor_scalar(dinv[:, :], deg[:, :], 1.0, None, ALU.add))
            dve.sem_inc(root, 1)
            pstep(vv.tensor_scalar(rdeg[:, :], deg[:, :], 1e-6, None, ALU.add))
            pstep(vv.reciprocal(rdeg[:, :], rdeg[:, :]))
            dve.wait_ge(root, 2)
            pstep(vv.reciprocal(dinv[:, :], dinv[:, :]))
            dve.sem_inc(cols_done, 1)
            dve.wait_ge(w_in, 96)
            pstep(vv.tensor_tensor(bje[:, :], bj[:, :], be[:, :], ALU.add))
            dve.sem_inc(ready, 1)

            def normalise(c):
                step = TurnSteps(dve, norm_step, c - 1, NORM_STEPS)
                rows = xrows[:, chunk(c - 1), :]
                norm_rows(nc, step, rows, v, rows, (mean, var, sq),
                          lambda: dve.sem_inc(var_ready, 1), lambda: dve.wait_ge(std_ready, c))
                reach(dve, z_kept, (c - 1) * 16)
                reach(dve, z_turned, c - 1)
                vv.tensor_tensor(z[:, :, :], rows, dinv[:, chunk(c - 1)].unsqueeze(2).to_broadcast([P, C, F]),
                                 ALU.mult).then_inc(z_ready, 1)
                dve.wait_ge(high_ready, c)
                vv.scalar_tensor_tensor(out=zsplit[:, chunk(c - 1), 1, :], in0=z[:, :, :], scalar=Z_SCALE,
                                        in1=zsplit[:, chunk(c - 1), 0, :], op0=ALU.mult, op1=ALU.subtract)\
                  .then_inc(low_ready, 1)
                dve.wait_ge(low_ready, c)

            def step(c, par, i):
                if later(c):
                    normalise(c)
                dve.wait_ge(multiplied, c + 1)
                dve.wait_ge(x_copied, c + 1)
                for h, k, n in HS:
                    last = vv.tensor_tensor(own[:, k:k + n, :], xc[par][:, k:k + n, :], i_ps[h][:, 0:n, :], ALU.add)
                last.then_inc(own_step, 1)
                dve.wait_ge(own_step, c + 1)
                dve.wait_ge(msg_out, c + 1)
                vv.tensor_tensor(xrows[:, chunk(c), :], own[:, :, :], msg[:, :, :], ALU.add).then_inc(summed, 1)
                wait_alone(dve, summed, c + 1, dve_passed)
            all_blocks(dve, NCH, step)
            normalise(NCH)

        @block.tensor
        def _(pe):
            pe.wait_ge(ready, 3)

            def turn_z(c):
                pe.wait_ge(z_ready, c)
                reach(pe, z_out, c - 1)
                for k in range(C):
                    last = nc.tensor.transpose(bank(z_ps, k), z[:, k, :], ident[:, :])
                last.then_inc(z_turned, 1)

            def step(c, par, i):
                pe.wait_ge(x_copied, c + 1)
                reach(pe, turned_out, c)
                for k in range(C):
                    last = nc.tensor.transpose(bank(t_ps, k), xc[par][:, k, :], ident[:, :])
                last.then_inc(turned, 1)
                pe.wait_ge(chunk_in[par], i * 48 + (48 if par else 96))
                reach(pe, msg_out, c)
                reach(pe, own_step, c)
                for k in range(C):
                    nc.tensor.matmul(bank(j_ps, k), sxc[par][:, k, :], wj[:, :], start=True, stop=False)
                    nc.tensor.matmul(bank(j_ps, k), sec[par][:, k, :], we[:, :], start=False, stop=False)
                    nc.tensor.matmul(bank(j_ps, k), degrow[par][0:1, k, :], bje[0:1, :], start=False, stop=True)
                pe.wait_ge(turned_out, c + 1)
                for k in range(C):
                    nc.tensor.matmul(bank(i_ps, k), xT[:, k, :], wi[:, :], start=True, stop=False)
                    last = nc.tensor.matmul(bank(i_ps, k), ones[0:1, :], bi[0:1, :], start=False, stop=True)
                last.then_inc(multiplied, 1)
                if later(c):
                    turn_z(c)
            all_blocks(pe, NCH, step)
            turn_z(NCH)


def update_load(nc, d, W, b, gamma, beta, keep, scratch):
    with nc.semaphore("layer1_loaded") as loaded, nc.semaphore("padding_cleared") as cleared, nc.Block() as block:
        @block.sync
        def _(sp):
            sp.dma_start(keep["dinv"][:, :], scratch["dinv"].rearrange("(o n) -> o n", o=1).to_broadcast([P, d.NP]))\
              .then_inc(loaded, 16)
            sp.dma_start(keep["w1"][:, :], W).then_inc(loaded, 16)
            for k, a in enumerate((b, gamma, beta)):
                sp.dma_start(keep["vec"][:, k:k + 1], a.rearrange("(p o) -> p o", o=1)).then_inc(loaded, 16)
            sp.wait_ge(loaded, 80)

        @block.vector
        def _(dve):
            nc.vector.memset(keep["y"][:, d.N:d.NP], 0.0).then_inc(cleared, 1)
            dve.wait_ge(cleared, 1)


def update_second(nc, d, out, keep, scratch):
    xrows, ident, y, vec, stats = (keep[k] for k in ("xrows", "ident", "y", "vec", "stats"))
    HI, C, NCH, NP, N = d.HI, d.CH, d.NC, d.NP, d.N
    HS = halves(C)
    NS = NORM_STEPS + 1
    with ExitStack() as ctx:
        sb = lambda n, shape, dt: ctx.enter_context(nc.sbuf_tensor(f"u1_{n}", shape, dt))
        sem = lambda n: ctx.enter_context(nc.semaphore(f"u1_{n}"))
        mv, co = sb("mv", [P, 2], F32), sb("co", [P, 4], F32)
        t = [sb(f"t{i}", [P, C, P], F32) for i in range(2)]
        r = [sb(f"r{i}", [P, C, P], F32) for i in range(2)]
        xo = [sb(f"xo{i}", [P, C, F], F32) for i in range(2)]
        v, sq = sb("v", [P, C, F], F32), sb("sq", [P, C, F], F32)
        mean, var = sb("mean", [P, C], F32), sb("var", [P, C], F32)
        r_ps = [[ctx.enter_context(nc.psum_tensor(f"u1_r{i}{k}", [P, 4, P], F32)) for k in range(2)] for i in range(2)]
        pre, root, coeff = sem("pre_step"), sem("batch_root"), sem("coefficients")
        t_ready, r_ready, turned, norm_step = sem("t_ready"), sem("r_ready"), sem("turned"), sem("norm_step")
        var_ready, std_ready, xo_ready, sp_passed = sem("var_ready"), sem("std_ready"), sem("xo_ready"), sem("sp_passed")
        kept = [sem(f"kept{i}") for i in range(2)]
        block = ctx.enter_context(nc.Block())
        chunk = lambda c: bass.ds(c * C, C)
        later = lambda c: not (isinstance(c, int) and c == 0)

        @block.sync
        def _(sp):
            def step(c, par, i):
                if later(c):
                    wait_alone(sp, xo_ready, c, sp_passed)
                    sp.dma_start(out[bass.ds((c - 1) * (C * P), C * P), :].rearrange("(c p) f -> p c f", p=P),
                                 xo[1 - par][:, :, :]).then_inc(kept[1 - par], 16)
            all_blocks(sp, NCH, step)
            sp.wait_ge(xo_ready, NCH)
            base = (NCH - 1) * C * P
            sp.dma_start(out[base:base + (C - 1) * P, :].rearrange("(c p) f -> p c f", p=P),
                         xo[(NCH - 1) % 2][:, 0:C - 1, :]).then_inc(kept[0], 16)
            sp.dma_start(out[(HI - 1) * P:N, :], xo[(NCH - 1) % 2][0:d.REM, C - 1, :]).then_inc(kept[0], 16)
            sp.wait_ge(kept[0], (NCH // 2 + 2) * 16)
            sp.wait_ge(kept[1], NCH // 2 * 16)

        @block.scalar
        def _(act):
            act.wait_ge(root, 1)
            nc.scalar.activation(co[:, 0:1], co[:, 0:1], ACT.Sqrt).then_inc(root, 1)
            act.wait_ge(coeff, 1)

            def take_root(c):
                act.wait_ge(var_ready, c)
                nc.scalar.activation(var[:, :], var[:, :], ACT.Sqrt).then_inc(std_ready, 1)

            def step(c, par, i):
                reach(act, r_ready, c - 1)
                nc.scalar.activation(t[par][:, :, :].rearrange("p c n -> p (c n)"),
                                     y[:, bass.ds(c * (C * P), C * P)], ACT.Identity,
                                     bias=co[:, 2:3], scale=co[:, 1:2]).then_inc(t_ready, 1)
                if later(c):
                    take_root(c)
            all_blocks(act, NCH, step)
            take_root(NCH)

        @block.vector
        def _(dve):
            vv = nc.vector
            pstep = Steps(dve, pre)
            pstep(vv.bn_aggr(mv[:, :], stats[:, :]))
            pstep(vv.tensor_scalar(co[:, 0:1], mv[:, 1:2], LN_EPS, None, ALU.add))
            dve.sem_inc(root, 1)
            dve.wait_ge(root, 2)
            pstep(vv.reciprocal(co[:, 1:2], co[:, 0:1]))
            pstep(vv.tensor_tensor(co[:, 1:2], co[:, 1:2], vec[:, 1:2], ALU.mult))
            pstep(vv.tensor_tensor(co[:, 3:4], mv[:, 0:1], co[:, 1:2], ALU.mult))
            pstep(vv.tensor_tensor(co[:, 2:3], vec[:, 2:3], co[:, 3:4], ALU.subtract))
            dve.sem_inc(coeff, 1)

            def normalise(c, par, i):
                step = TurnSteps(dve, norm_step, c - 1, NS)
                dve.wait_ge(turned, c)
                for h, k, n in HS:
                    last = vv.tensor_tensor(v[:, k:k + n, :], xrows[:, bass.ds((c - 1) * C + k, n), :],
                                            r_ps[1 - par][h][:, 0:n, :], ALU.add)
                step(last)
                reach(dve, kept[1 - par], i * 16)
                norm_rows(nc, step, v[:, :, :], v, xo[1 - par][:, :, :], (mean, var, sq),
                          lambda: dve.sem_inc(var_ready, 1), lambda: dve.wait_ge(std_ready, c))
                dve.sem_inc(xo_ready, 1)

            def step(c, par, i):
                dve.wait_ge(t_ready, c + 1)
                reach(dve, turned, c - 1)
                vv.scalar_tensor_tensor(out=r[par][:, :, :], in0=t[par][:, :, :], scalar=0.01,
                                        in1=t[par][:, :, :], op0=ALU.mult, op1=ALU.max).then_inc(r_ready, 1)
                if later(c):
                    normalise(c, par, i)
            all_blocks(dve, NCH, step)
            normalise(NCH, NCH % 2, NCH // 2)

        @block.tensor
        def _(pe):
            def step(c, par, i):
                pe.wait_ge(r_ready, c + 1)
                reach(pe, norm_step, (c - 2) * NS + 1)
                for k in range(C):
                    last = nc.tensor.transpose(r_ps[par][k // 4][:, k % 4, :], r[par][:, k, :], ident[:, :])
                last.then_inc(turned, 1)
            all_blocks(pe, NCH, step)


def build(nc, x, src, dst, ea, W0, b0, We, be, W1, b1, gamma, beta, out):
    d = Dims(x.shape[0], src.shape[0])
    NE = d.NB * EK
    dram = lambda name, shape, dt: nc.dram_tensor(name, shape, dt)
    scratch = {
        "starts": dram("starts", [NE, 1], I32)[:, :],
        "deg": dram("deg_rows", [d.NP], F32)[:],
        "dinv": dram("dinv_rows", [d.NP], F32)[:],
        "sx": dram("sums_x", [P, d.NP], F32)[:, :],
        "se": dram("sums_e", [P, d.NP], F32)[:, :],
        "s1": dram("sums_z", [P, d.NP], F32)[:, :],
        "z": dram("z_rows", [d.NP, F], F32)[:, :],
        "counts": dram("counts_kept", [d.NB * P, d.HI * BN], BF16)[:, :],
    }
    with ExitStack() as ctx:
        sb = lambda name, shape, dt: ctx.enter_context(nc.sbuf_tensor(name, shape, dt))
        keep = {
            "xrows": sb("xrows", [P, d.HI, F], F32),
            "ident": sb("ident", [P, P], F32),
            "flag": sb("flag", [1, 1], I32),
        }
        with ExitStack() as tables:
            tb = lambda name, shape, dt: tables.enter_context(nc.sbuf_tensor(name, shape, dt))
            keep.update({
                "xsplit": tb("xsplit", [P, d.HI, 3, F], BF16),
                "iota": tb("iota", [P, 256], BF16), "iota_e": tb("iota_e", [P, EW], F32),
                "key_t": tb("key_t", [P, d.NW * TILES], F32), "lo_t": tb("lo_t", [P, d.NW * TILES], F32),
                "ekey_t": tb("ekey_t", [P, NE, EJ], F32), "startrow": tb("startrow", [1, NE], I32),
            })
            prepare(nc, d, x, src, dst, keep, scratch)
            aggregate_fast(nc, d, ea, keep, scratch)
        aggregate_any(nc, d, "any0", x, ea, src, dst, keep, scratch["sx"], scratch["se"], scratch["deg"])
        keep.update({
            "zsplit": sb("zsplit", [P, d.HI, 2, F], F16),
            "zT": sb("zT", [P, d.NP], F32),
        })
        update_first(nc, d, W0, b0, We, be, keep, scratch)
        aggregate_any(nc, d, "any1sum", scratch["z"], None, src, dst, keep, scratch["s1"], None, None)
        keep.update({
            "y": sb("y", [P, d.NP], F32), "dinv": sb("dinv", [P, d.NP], F32),
            "w1": sb("w1", [P, F], F32), "vec": sb("vec", [P, 3], F32),
            "stats": sb("stats", [P, 6 * d.NB], F32),
        })
        update_load(nc, d, W1, b1, gamma, beta, keep, scratch)
        project(nc, d, True, keep, scratch)
        project(nc, d, False, keep, scratch)
        update_second(nc, d, out, keep, scratch)


_INS = ["x", "src", "dst", "edge_attr_128", "L0_gnn_W", "L0_gnn_b_W", "L0_gnn_W_e", "L0_gnn_b_We",
        "L1_gnn_W", "L1_gnn_b", "L1_gnn_gamma", "L1_gnn_beta"]


def kernel(**inputs):
    import numpy as np
    import concourse.bacc as bacc
    from concourse.bass_utils import run_bass_kernel_spmd

    nc = bacc.Bacc("TRN2", target_bir_lowering=False, num_devices=1)
    arrays, args = {}, []
    for name in _INS:
        a = np.ascontiguousarray(inputs[name])
        arrays[f"in_{name}"] = a
        args.append(nc.dram_tensor(f"in_{name}", a.shape, mybir.dt.from_np(a.dtype), kind="ExternalInput").ap())
    out = nc.dram_tensor("out_rows", inputs["x"].shape, F32, kind="ExternalOutput").ap()
    build(nc, *args, out)
    result = run_bass_kernel_spmd(nc, [arrays], core_ids=[0])
    return result.results[0]["out_rows"]
```

```python
import concourse.bass as bass
from concourse import mybir
from contextlib import ExitStack

F32 = mybir.dt.float32
BF16 = mybir.dt.bfloat16
F16 = mybir.dt.float16
I32 = mybir.dt.int32
ALU = mybir.AluOpType
ACT = mybir.ActivationFunctionType
AX = mybir.AxisListType

P = 128
F = 128
WN = 5
TILES = 2
WE = TILES * P
BN = 250
BW = BN // WN
PAIRS = BW // 2
GW = 125
EW = 63
EK = 4
EJ = 18
EE = EJ * P
RING = 5
HR = 500
GE = 125
GN = 512
LN_EPS = 1e-5
Z_SCALE = 4096.0
X_TOP = 14
ROW_LEAST = 2.0 ** -10
X_LEAST, X_MOST = 2.0 ** -60, 2.0 ** 60
EXP_BITS, ONE_EXP = 0x7F800000, 1 << 23


class Dims:
    def __init__(self, n, e):
        self.N, self.E = n, e
        self.HI = -(-n // P)
        self.NP = self.HI * P
        self.REM = n - (self.HI - 1) * P
        self.NB = n // BN
        self.NW = n // WN
        self.G = self.NW // GW
        self.R = e // HR
        self.CH = max(c for c in range(1, 8) if self.HI % c == 0 and self.HI // c % 2)
        self.NC = self.HI // self.CH
        assert n % BN == 0 and self.NW % GW == 0 and e % HR == 0 and e % GE == 0
        assert self.NB % 2 == 1 and self.NB * EK <= P and self.R <= 512 and WN * self.HI * 2 <= 512


class Steps:

    def __init__(self, engine, sem):
        self.engine, self.sem, self.n = engine, sem, 0

    def __call__(self, ins):
        self.n += 1
        ins.then_inc(self.sem, 1)
        self.engine.wait_ge(self.sem, self.n)


def reach(engine, sem, value):
    if not isinstance(value, int) or value > 0:
        engine.wait_ge(sem, value)


def wait_alone(engine, sem, value, passed):
    if not isinstance(value, int) or value > 0:
        engine.wait_ge(sem, value)
        engine.sem_inc(passed, 1)


def all_blocks(engine, nb, step):
    step(0, 0, -1)
    step(1, 1, 0)
    step(2, 0, 0)
    if nb > 3:
        with engine.Fori(1, (nb - 1) // 2) as i:
            step(i * 2 + 1, 1, i)
            step(i * 2 + 2, 0, i)


def all_turns(engine, n, step):
    step(0)
    if n > 1:
        with engine.Fori(1, n) as i:
            step(i)


def prepare(nc, d, x, src, dst, keep, scratch):
    xrows, xsplit, xscale, ident, total, dl, iota, key_t, lo_t, ekey_t, startrow, iota_e = (
        keep[k] for k in ("xrows", "xsplit", "xscale", "ident", "total", "dl", "iota", "key_t", "lo_t", "ekey_t",
                          "startrow", "iota_e"))
    N, E, HI, G, R, NB = d.N, d.E, d.HI, d.G, d.R, d.NB
    NE = NB * EK
    with ExitStack() as ctx:
        sb = lambda name, shape, dt: ctx.enter_context(nc.sbuf_tensor(name, shape, dt))
        sem = lambda name: ctx.enter_context(nc.semaphore(name))
        heads_i, heads = sb("heads_i", [1, R], I32), sb("heads", [1, R], F32)
        ones = sb("ones", [P, P], F32)
        iota_i, iota_ei = sb("iota_i", [P, 256], I32), sb("iota_ei", [P, EW], I32)
        th_i, th = sb("th_i", [P, G + 1], I32), sb("th", [P, G + 1], F32)
        e_b, e_k, e_w = sb("e_b", [P, 1], I32), sb("e_k", [P, 1], I32), sb("e_w", [P, 1], F32)
        cnt1, cnt2 = sb("cnt1", [P, G + 1], F32), sb("cnt2", [P, G + 1], F32)
        row_f, row_i = sb("row_f", [P, G + 1], F32), sb("row_i", [P, G + 1], I32)
        start_i = sb("start_i", [P, G + 1], I32)
        rows = sb("rows", [P, G + 1, HR], I32)
        junk = sb("junk", [P, max(G * WE, EE)], F32)
        gdst, gsrc = sb("gdst", [P, G, WE], I32), sb("gsrc", [P, G, WE], I32)
        edst = sb("edst", [P, EE], I32)
        edl = edst[:, :].bitcast(F32)
        key = sb("key", [P, G, WE], F32)
        spare = rows[:, :, :].rearrange("p g e -> p (g e)")
        hi_i, lo_i = (spare[:, k * G * WE:(k + 1) * G * WE].rearrange("p (g e) -> p g e", g=G) for k in range(2))
        lo = gdst[:, :, :].bitcast(F32)
        below, sound = sb("below", [P, 2], F32), sb("sound", [1, 1], F32)
        rowmax, rowok, pmax = sb("rowmax", [P, HI], F32), sb("rowok", [P, HI], F32), sb("pmax", [P, 1], F32)
        top, expo, few = sb("top", [1, 1], F32), sb("expo", [1, 1], I32), sb("few", [1, 4], I32)
        heads_ps = ctx.enter_context(nc.psum_tensor("heads_ps", [P, 512], F32))
        pmax_ps = ctx.enter_context(nc.psum_tensor("pmax_ps", [P, P], F32))
        few_ps = ctx.enter_context(nc.psum_tensor("few_ps", [P, 4], F32))
        tps = [ctx.enter_context(nc.psum_tensor(f"tps{i}", [P, 4, P], F32)) for i in range(4)]

        heads_in, x_cleared, x_in = sem("heads_in"), sem("x_cleared"), sem("x_in")
        consts, vstep, pstep = sem("consts"), sem("prep_vector_step"), sem("prep_pool_step")
        heads_f, heads_out = sem("heads_float"), sem("heads_broadcast")
        rows_known, starts_known = sem("rows_known"), sem("starts_known")
        row_in = [sem(f"row_in{g}") for g in range(G + 1)]
        dst_in, src_in, edst_in = sem("window_dst_in"), sem("window_src_in"), sem("edge_window_dst_in")
        keys_ready, lo_ready, ekeys_ready = sem("keys_ready"), sem("lo_ready"), sem("edge_keys_ready")
        lo_int = sem("lo_int")
        turned, tabled = sem("transposed"), sem("tabled")
        start_out, start_back = sem("start_out"), sem("start_back")
        pmax_ready, pmax_out, few_ready, few_out = sem("pmax_ready"), sem("pmax_out"), sem("few_ready"), sem("few_out")
        scale_ready, x_high = sem("scale_ready"), sem("x_high")
        block = ctx.enter_context(nc.Block())
        EBANKS = -(-EJ // 4)

        @block.sync
        def _(sp):
            sp.dma_start(heads_i[:, :], dst.rearrange("(r c) -> c r", c=HR)[0:1, :],
                         allow_slow_non_contiguous=True).then_inc(heads_in, 16)
            sp.dma_start(xrows[:, 0:HI - 1, :],
                         x[0:(HI - 1) * P, :].rearrange("(h p) f -> p h f", p=P)).then_inc(x_in, 16)
            sp.wait_ge(x_cleared, 1)
            sp.dma_start(xrows[0:d.REM, HI - 1, :], x[(HI - 1) * P:N, :]).then_inc(x_in, 16)
            sp.wait_ge(starts_known, 1)
            sp.dma_start(scratch["starts"], start_i[0:NE, G:G + 1]).then_inc(start_out, 16)
            sp.wait_ge(start_out, 16)
            sp.dma_start(startrow[:, :], scratch["starts"].rearrange("n o -> o n")).then_inc(start_back, 16)
            sp.wait_ge(start_back, 16)

        @block.gpsimd
        def _(pool):
            step = Steps(pool, pstep)
            nc.gpsimd.memset(xrows[:, HI - 1, :], 0.0).then_inc(x_cleared, 1)
            step(nc.gpsimd.memset(ident[:, :], 0.0))
            nc.gpsimd.affine_select(out=ident[:, :], in_=ident[:, :], compare_op=ALU.not_equal, fill=1.0,
                                    base=0, pattern=[[-1, P]], channel_multiplier=1).then_inc(consts, 1)
            nc.gpsimd.memset(ones[:, :], 1.0).then_inc(consts, 1)
            nc.gpsimd.iota(th_i[:, 0:G], pattern=[[WN * GW, G]], base=0, channel_multiplier=WN).then_inc(consts, 1)
            nc.gpsimd.iota(th_i[:, G:G + 1], pattern=[[0, 1]], base=0, channel_multiplier=1).then_inc(consts, 1)
            nc.gpsimd.iota(iota_i[:, :], pattern=[[1, 256]], base=0, channel_multiplier=0).then_inc(consts, 1)
            nc.gpsimd.iota(iota_ei[:, :], pattern=[[1, EW]], base=0, channel_multiplier=0).then_inc(consts, 1)
            pool.wait_ge(rows_known, 1)
            flat_dst, flat_src = dst.rearrange("(n o) -> n o", o=1), src.rearrange("(n o) -> n o", o=1)

            def gather(out, table, at, done):
                nc.gpsimd.indirect_dma_start(
                    out=out, out_offset=None, in_=table,
                    in_offset=bass.IndirectOffsetOnAxis(ap=at, axis=0)).then_inc(done, 16)

            for g in range(G):
                gather(rows[0:GW, g, :], flat_dst, row_i[0:GW, g:g + 1], row_in[g])
            gather(rows[0:NE, G, :], flat_dst, row_i[0:NE, G:G + 1], row_in[G])
            pool.wait_ge(starts_known, 1)
            for g in range(G):
                gather(gdst[0:GW, g, :], flat_dst, start_i[0:GW, g:g + 1], dst_in)
            for g in range(G):
                gather(gsrc[0:GW, g, :], flat_src, start_i[0:GW, g:g + 1], src_in)
            gather(edst[0:NE, :], flat_dst, start_i[0:NE, G:G + 1], edst_in)

        @block.vector
        def _(dve):
            step = Steps(dve, vstep)
            v = nc.vector
            dve.wait_ge(heads_in, 16)
            v.tensor_copy(heads[:, :], heads_i[:, :]).then_inc(heads_f, 1)
            dve.wait_ge(consts, 6)
            v.tensor_copy(iota[:, :], iota_i[:, :])
            v.tensor_copy(iota_e[:, :], iota_ei[:, :])
            v.tensor_copy(th[:, 0:G], th_i[:, 0:G])
            v.memset(total[:, :], 0.0)
            v.tensor_scalar(e_b[:, :], th_i[:, G:G + 1], 2, None, ALU.logical_shift_right)
            v.tensor_scalar(e_k[:, :], th_i[:, G:G + 1], 3, None, ALU.bitwise_and)
            step(v.tensor_scalar(th[:, G:G + 1], th_i[:, G:G + 1], float(EW), None, ALU.mult))
            step(v.scalar_tensor_tensor(out=th[:, G:G + 1], in0=e_b[:, :], scalar=float(BN - EK * EW),
                                        in1=th[:, G:G + 1], op0=ALU.mult, op1=ALU.add))
            step(v.tensor_scalar(e_w[:, :], e_k[:, :], float(EK - 1), float(BN - EK * EW), ALU.is_equal, ALU.mult))
            step(v.tensor_scalar(e_w[:, :], e_w[:, :], float(EW), None, ALU.add))
            dve.wait_ge(heads_out, 1)
            for g in range(G + 1):
                n = GW if g < G else NE
                step(v.tensor_scalar(junk[0:n, 0:R], heads_ps[0:n, 0:R], th[0:n, g:g + 1], 0.0, ALU.is_lt,
                                     ALU.add, accum_out=cnt1[0:n, g:g + 1]))

            def each(f):
                f(slice(0, GW), slice(0, G))
                f(slice(0, NE), slice(G, G + 1))
                step(v.memset(junk[0:1, 0:1], 0.0))

            each(lambda p, c: v.tensor_scalar(row_f[p, c], cnt1[p, c], -1.0, 0.0, ALU.add, ALU.max))
            each(lambda p, c: v.tensor_scalar(row_f[p, c], row_f[p, c], float(HR), None, ALU.mult))
            each(lambda p, c: v.tensor_copy(row_i[p, c], row_f[p, c]))
            dve.sem_inc(rows_known, 1)
            dve.wait_ge(x_in, 32)
            step(v.tensor_reduce(out=rowmax[:, :], in_=xrows[:, :, :], axis=AX.X, op=ALU.max,
                                 apply_absolute_value=True))
            step(v.tensor_reduce(out=pmax[:, :], in_=rowmax[:, :], axis=AX.X, op=ALU.max))
            dve.sem_inc(pmax_ready, 1)
            dve.wait_ge(pmax_out, 1)
            step(v.tensor_reduce(out=top[:, :], in_=pmax_ps[0:1, 0:P], axis=AX.X, op=ALU.max))
            step(v.tensor_scalar(expo[:, :], top[:, :].bitcast(I32), EXP_BITS, None, ALU.bitwise_and))
            step(v.tensor_scalar(few[:, 0:1], expo[:, :], -1.0, float((2 * 127 + X_TOP) * ONE_EXP),
                                 ALU.mult, ALU.add))
            step(v.tensor_scalar(few[:, 1:2], expo[:, :], -float(X_TOP * ONE_EXP), None, ALU.add))
            few_f = few[:, :].bitcast(F32)
            step(v.tensor_scalar(few_f[:, 2:3], top[:, :], ROW_LEAST, None, ALU.mult))
            step(v.tensor_scalar(few_f[:, 3:4], top[:, :], X_LEAST, None, ALU.is_ge))
            step(v.tensor_scalar(sound[:, :], top[:, :], X_MOST, None, ALU.is_le))
            step(v.tensor_tensor(few_f[:, 3:4], few_f[:, 3:4], sound[:, :], ALU.mult))
            dve.sem_inc(few_ready, 1)
            dve.wait_ge(few_out, 1)
            v.tensor_copy(xscale[:, :], few_ps[:, 0:4]).then_inc(scale_ready, 1)
            dve.wait_ge(scale_ready, 1)
            step(v.tensor_scalar(rowok[:, :], rowmax[:, :], xscale[:, 2:3], None, ALU.is_ge))
            step(v.tensor_scalar(rowmax[:, :], rowmax[:, :], 0.0, None, ALU.is_equal))
            step(v.tensor_tensor(rowok[:, :], rowok[:, :], rowmax[:, :], ALU.max))
            step(v.tensor_reduce(out=total[:, 2:3], in_=rowok[:, :], axis=AX.X, op=ALU.add))
            step(v.tensor_scalar(total[:, 3:4], xscale[:, 3:4], 1.0, None, ALU.mult))
            for g in range(G + 1):
                n = GW if g < G else NE
                dve.wait_ge(row_in[g], 16)
                step(v.tensor_scalar(junk[0:n, 0:HR], rows[0:n, g, :], th[0:n, g:g + 1], 0.0, ALU.is_lt,
                                     ALU.add, accum_out=cnt2[0:n, g:g + 1]))
            each(lambda p, c: v.tensor_tensor(row_f[p, c], row_f[p, c], cnt2[p, c], ALU.add))
            step(v.tensor_scalar(start_i[0:GW, 0:G], row_f[0:GW, 0:G], float(E - WE), None, ALU.min))
            step(v.tensor_scalar(start_i[0:NE, G:G + 1], row_f[0:NE, G:G + 1], float(E - EE), None, ALU.min))
            dve.sem_inc(starts_known, 1)
            dve.wait_ge(x_high, 1)
            v.scalar_tensor_tensor(out=xsplit[:, :, 1, :], in0=xrows[:, :, :], scalar=xscale[:, 0:1],
                                   in1=xsplit[:, :, 0, :], op0=ALU.mult, op1=ALU.subtract)
            dve.wait_ge(dst_in, 16 * G)
            thb = th[0:GW, 0:G].unsqueeze(2).to_broadcast([GW, G, WE])
            step(v.tensor_tensor(dl[0:GW, :, :], gdst[0:GW, :, :], thb, ALU.subtract))
            dve.wait_ge(src_in, 16 * G)
            v.tensor_scalar(lo_i[0:GW, :, :], gsrc[0:GW, :, :], P - 1, None, ALU.bitwise_and).then_inc(lo_int, 1)
            step(v.tensor_scalar(hi_i[0:GW, :, :], gsrc[0:GW, :, :], 7, None, ALU.logical_shift_right))
            v.scalar_tensor_tensor(out=key[0:GW, :, :], in0=dl[0:GW, :, :], scalar=float(HI),
                                   in1=hi_i[0:GW, :, :], op0=ALU.mult, op1=ALU.add).then_inc(keys_ready, 1)
            dve.wait_ge(edst_in, 16)
            v.tensor_scalar(edl[0:NE, :], edst[0:NE, :], th[0:NE, G:G + 1], None, ALU.subtract)\
             .then_inc(ekeys_ready, 1)
            dve.wait_ge(ekeys_ready, 1)
            step(v.tensor_scalar(junk[0:NE, 0:EE], edl[0:NE, :], 0.0, 0.0, ALU.is_lt, ALU.add,
                                 accum_out=below[0:NE, 0:1]))
            step(v.tensor_scalar(junk[0:NE, 0:EE], edl[0:NE, :], e_w[0:NE, 0:1], 0.0, ALU.is_lt, ALU.add,
                                 accum_out=below[0:NE, 1:2]))
            step(v.tensor_tensor(total[0:NE, 1:2], below[0:NE, 1:2], below[0:NE, 0:1], ALU.subtract))

        @block.scalar
        def _(act):
            act.wait_ge(scale_ready, 1)
            nc.scalar.activation(xsplit[:, :, 0, :], xrows[:, :, :], ACT.Copy, scale=xscale[:, 0:1])\
              .then_inc(x_high, 1)
            act.wait_ge(lo_int, 1)
            nc.scalar.copy(lo[0:GW, :, :], lo_i[0:GW, :, :]).then_inc(lo_ready, 1)
            for g in range(G):
                act.wait_ge(turned, g + 1)
                for q, table in enumerate((key_t, lo_t)):
                    nc.scalar.copy(
                        table[:, g * GW * TILES:(g + 1) * GW * TILES].rearrange("p (w t) -> p t w", t=TILES),
                        tps[g % 4][:, TILES * q:TILES * q + TILES, 0:GW]).then_inc(tabled, 1)
            for m in range(EBANKS):
                act.wait_ge(turned, G + m + 1)
                n = min(4, EJ - 4 * m)
                nc.scalar.copy(ekey_t[:, :, 4 * m:4 * m + n].rearrange("p w j -> p j w"),
                               tps[(G + m) % 4][:, 0:n, 0:NE]).then_inc(tabled, 2)

        @block.tensor
        def _(pe):
            pe.wait_ge(heads_f, 1)
            pe.wait_ge(consts, 2)
            nc.tensor.matmul(heads_ps[:, 0:R], ones[0:1, :], heads[0:1, :], start=True, stop=True)\
              .then_inc(heads_out, 1)
            pe.wait_ge(pmax_ready, 1)
            nc.tensor.transpose(pmax_ps[0:1, 0:P], pmax[:, :], ident[:, :]).then_inc(pmax_out, 1)
            pe.wait_ge(few_ready, 1)
            nc.tensor.matmul(few_ps[:, 0:4], ones[0:1, :], few[0:1, :].bitcast(F32), start=True, stop=True)\
              .then_inc(few_out, 1)
            pe.wait_ge(keys_ready, 1)
            pe.wait_ge(lo_ready, 1)
            for g in range(G):
                if g >= 4:
                    pe.wait_ge(tabled, 2 * (g - 3))
                for q, t in ((0, 0), (0, 1), (1, 0), (1, 1)):
                    of = (key, lo)[q]
                    last = nc.tensor.transpose(tps[g % 4][:, 2 * q + t, 0:GW],
                                               of[0:GW, g, t * P:(t + 1) * P], ident[0:GW, 0:GW])
                last.then_inc(turned, 1)
            pe.wait_ge(ekeys_ready, 1)
            by_edge = edl[0:NE, :].rearrange("w (p j) -> w j p", j=EJ)
            for m in range(EBANKS):
                if G + m >= 4:
                    pe.wait_ge(tabled, 2 * (G + m - 3))
                for j in range(4 * m, min(4 * m + 4, EJ)):
                    last = nc.tensor.transpose(tps[(G + m) % 4][:, j - 4 * m, 0:NE], by_edge[:, j, :],
                                               ident[0:NE, 0:NE])
                last.then_inc(turned, 1)


def aggregate_fast(nc, d, ea, keep, scratch):
    xsplit, xscale, total, dl, flag, iota, key_t, lo_t, ekey_t, startrow, iota_e = (
        keep[k] for k in ("xsplit", "xscale", "total", "dl", "flag", "iota", "key_t", "lo_t", "ekey_t", "startrow", "iota_e"))
    HI, NB, E = d.HI, d.NB, d.E
    KW = WN * HI
    PRODUCTS = 2 * HI
    PER = -(-PRODUCTS // PAIRS)
    NT = TILES * BW
    with ExitStack() as ctx:
        sb = lambda name, shape, dt: ctx.enter_context(nc.sbuf_tensor(name, shape, dt))
        ps = lambda name: ctx.enter_context(nc.psum_tensor(name, [P, 512], F32))
        sem = lambda name: ctx.enter_context(nc.semaphore(name))
        counts = [sb(f"counts{i}", [P, HI, BN], BF16) for i in range(2)]
        key_oh = sb("key_oh", [P, RING, 4, 256], BF16)
        lo_oh = sb("lo_oh", [P, RING, 4, P], BF16)
        ebuf = [sb(f"ebuf{i}", [P, EJ, F], F32) for i in range(EK)]
        e_oh = [sb(f"e_oh{i}", [P, EJ, EW], F32) for i in range(2)]
        keys = [sb(f"keys{i}", [P, NT], F32) for i in range(2)]
        los = [sb(f"los{i}", [P, NT], F32) for i in range(2)]
        ekeys = [sb(f"ekeys{i}", [P, EK, EJ], F32) for i in range(2)]
        sx = [sb(f"sx{i}", [P, BN], F32) for i in range(2)]
        se = [sb(f"se{i}", [P, BN], F32) for i in range(2)]
        is_k, deg = sb("is_k", [P, d.G, WE], BF16), sb("deg", [P, d.G, WN], F32)
        ones, zpad = sb("fast_ones", [P, 1], F32), sb("zpad", [1, P], F32)
        wanted, ok, ok1 = sb("wanted", [1, 4], F32), sb("ok", [1, 4], F32), sb("ok1", [1, 1], F32)
        total_ps = ps("total_ps")
        pair_ps = [ps(f"pair_ps{i}") for i in range(RING)]
        e_ps = ps("e_ps")
        x_ps = ps("x_ps")

        block_keys = sem("block_keys")
        key_hot, lo_hot, lo_hot_pool = sem("key_hot"), sem("lo_hot"), sem("lo_hot_pool")
        pair_built, pair_out = sem("pair_built"), sem("pair_out")
        e_hot, e_summed = sem("e_hot"), sem("e_summed")
        e_in = [sem(f"e_in{i}") for i in range(EK)]
        sp_passed, pool_passed = sem("sp_passed"), sem("pool_passed")
        product_done, sx_out, se_out = sem("product_done"), sem("sx_out"), sem("se_out")
        counts_kept = [sem(f"counts_kept{i}") for i in range(2)]
        sx_kept = [sem(f"sx_kept{i}") for i in range(2)]
        se_kept = [sem(f"se_kept{i}") for i in range(2)]
        deg_step, deg_ready, totals_ready, totals_out = (
            sem(n) for n in ("deg_step", "deg_ready", "totals_ready", "totals_out"))
        totals_wanted, deg_out = sem("totals_wanted"), sem("deg_out")
        block = ctx.enter_context(nc.Block())

        @block.sync
        def _(sp):
            def step(b, par, i):
                for k in range(EK):
                    wait_alone(sp, e_summed, (b - 1) * EK + k + 1, sp_passed)
                    at = sp.value_load(startrow[0:1, bass.ds(b * EK + k, 1)], min_val=0, max_val=E - EE)
                    sp.dma_start(ebuf[k][:, :, :].rearrange("p j f -> p (j f)"),
                                 ea[bass.ds(at, EE), :].rearrange("(p j) f -> p (j f)", j=EJ))\
                      .then_inc(e_in[k], 16)
            all_blocks(sp, NB, step)
            sp.wait_ge(deg_ready, 1)
            sp.dma_start(scratch["deg"][0:d.N].rearrange("(g p k) -> p g k", p=GW, k=WN),
                         deg[0:GW, :, :]).then_inc(deg_out, 16)
            sp.dma_start(scratch["deg"][d.N:d.NP].rearrange("(o n) -> o n", o=1),
                         zpad[:, 0:d.NP - d.N]).then_inc(deg_out, 16)
            sp.wait_ge(deg_out, 32)

        @block.gpsimd
        def _(pool):
            def step(b, par, i):
                nc.gpsimd.tensor_copy(keys[par][:, :], key_t[:, bass.ds(b * NT, NT)]).then_inc(block_keys, 1)
                nc.gpsimd.tensor_copy(los[par][:, :], lo_t[:, bass.ds(b * NT, NT)]).then_inc(block_keys, 1)
                nc.gpsimd.tensor_copy(ekeys[par][:, :, :], ekey_t[:, bass.ds(b * EK, EK), :])\
                  .then_inc(block_keys, 1)
                wait_alone(pool, block_keys, b * 3 + 3, pool_passed)
                for p in range(PAIRS):
                    wait_alone(pool, pair_built, b * PAIRS + (p + 1 - RING), pool_passed)
                    for w in range(2):
                        c = (2 * p + w) * TILES + 1
                        last = nc.gpsimd.tensor_scalar(lo_oh[:, p % RING, 2 * w + 1, :], iota[:, 0:P],
                                                       los[par][:, c:c + 1], None, ALU.is_equal)
                    last.then_inc(lo_hot_pool, 1)
            all_blocks(pool, NB, step)

        @block.vector
        def _(dve):
            def step(b, par, i):
                dve.wait_ge(block_keys, b * 3 + 3)
                for p in range(PAIRS):
                    reach(dve, pair_built, b * PAIRS + (p + 1 - RING))
                    for w in range(2):
                        c = (2 * p + w) * TILES
                        nc.vector.tensor_scalar(lo_oh[:, p % RING, 2 * w, :], iota[:, 0:P],
                                                los[par][:, c:c + 1], None, ALU.is_equal)
                        for t in range(TILES):
                            last = nc.vector.tensor_scalar(
                                key_oh[:, p % RING, 2 * w + t, 0:KW], iota[:, 0:KW],
                                keys[par][:, c + t:c + t + 1], None, ALU.is_equal)
                    last.then_inc(key_hot, 1)
                    if p % 6 == 0 and p // 6 < EK:
                        k = p // 6
                        reach(dve, e_summed, b * EK + (k - 1))
                        nc.vector.tensor_tensor(
                            e_oh[k % 2][:, :, :], iota_e[:, :].unsqueeze(1).to_broadcast([P, EJ, EW]),
                            ekeys[par][:, k, :].unsqueeze(2).to_broadcast([P, EJ, EW]), ALU.is_equal)\
                          .then_inc(e_hot, 1)
            all_blocks(dve, NB, step)

            v = nc.vector
            dstep = Steps(dve, deg_step)
            dstep(v.memset(zpad[:, :], 0.0))
            for k, n in enumerate((E, E, d.NP, P)):
                v.memset(wanted[:, k:k + 1], float(n)).then_inc(totals_wanted, 1)
            v.memset(ones[:, :], 1.0).then_inc(totals_wanted, 1)
            for k in range(WN):
                dstep(v.tensor_scalar(is_k[0:GW, :, :], dl[0:GW, :, :], float(k), None, ALU.is_equal))
                dstep(v.tensor_reduce(out=deg[0:GW, :, k], in_=is_k[0:GW, :, :], axis=AX.X, op=ALU.add))
            dve.sem_inc(deg_ready, 1)
            dstep(v.tensor_reduce(out=total[0:GW, 0:1], in_=deg[0:GW, :, :], axis=AX.XY, op=ALU.add))
            dve.sem_inc(totals_ready, 1)
            dve.wait_ge(totals_wanted, 5)
            dve.wait_ge(totals_out, 1)
            dstep(v.tensor_tensor(ok[:, :], total_ps[0:1, 0:4], wanted[:, :], ALU.is_equal))
            dstep(v.tensor_reduce(out=ok1[:, :], in_=ok[:, :], axis=AX.X, op=ALU.min))
            dstep(v.tensor_copy(flag[:, :], ok1[:, :]))

        @block.tensor
        def _(pe):
            def product(b, par, p):
                if p == 0:
                    pe.wait_ge(pair_out, b * PAIRS)
                for q in range(PER * p, min(PER * (p + 1), PRODUCTS)):
                    last = nc.tensor.matmul(x_ps[:, 0:BN], xsplit[:, q // 2, q % 2, :],
                                            counts[1 - par][:, q // 2, :],
                                            start=(q == 0), stop=(q == PRODUCTS - 1))
                    if q == PRODUCTS - 1:
                        last.then_inc(product_done, 1)

            def step(b, par, i):
                for p in range(PAIRS):
                    pe.wait_ge(key_hot, b * PAIRS + p + 1)
                    pe.wait_ge(lo_hot_pool, b * PAIRS + p + 1)
                    reach(pe, pair_out, b * PAIRS + (p + 1 - RING))
                    for w in range(2):
                        for t in range(TILES):
                            last = nc.tensor.matmul(pair_ps[p % RING][:, w * KW:(w + 1) * KW],
                                                    lo_oh[:, p % RING, 2 * w + t, :],
                                                    key_oh[:, p % RING, 2 * w + t, 0:KW],
                                                    start=(t == 0), stop=(t == TILES - 1))
                    last.then_inc(pair_built, 1)
                    if p >= 1:
                        k, part = (p - 1) // 6, (p - 1) % 6
                        if part == 0:
                            pe.wait_ge(e_hot, b * EK + k + 1)
                            pe.wait_ge(e_in[k], b * 16 + 16)
                        if k == 0 and part == 0:
                            reach(pe, se_out, b)
                        n = EW if k < EK - 1 else BN - EW * (EK - 1)
                        for j in range(3 * part, 3 * part + 3):
                            last = nc.tensor.matmul(e_ps[:, EW * k:EW * k + n], ebuf[k][:, j, :],
                                                    e_oh[k % 2][:, j, 0:n], start=(j == 0),
                                                    stop=(j == EJ - 1))
                        if part == 5:
                            last.then_inc(e_summed, 1)
                    if not (isinstance(b, int) and b == 0):
                        if p == 0:
                            reach(pe, sx_out, b - 1)
                        product(b, par, p)
            all_blocks(pe, NB, step)
            pe.wait_ge(sx_out, NB - 1)
            for p in range(PAIRS):
                product(NB, NB % 2, p)
            pe.wait_ge(totals_ready, 1)
            nc.tensor.matmul(total_ps[0:1, 0:4], ones[:, 0:1], total[:, :], start=True, stop=True)\
              .then_inc(totals_out, 1)

        @block.scalar
        def _(act):
            def product_out(b, par, old):
                act.wait_ge(product_done, b)
                reach(act, sx_kept[1 - par], old)
                nc.scalar.activation(sx[1 - par][:, :], x_ps[:, 0:BN], ACT.Copy, scale=xscale[:, 1:2])\
                  .then_inc(sx_out, 1)
                act.wait_ge(sx_out, b)
                act.dma_start(scratch["sx"][:, bass.ds((b - 1) * BN, BN)], sx[1 - par][:, :])\
                   .then_inc(sx_kept[1 - par], 16)

            def step(b, par, i):
                reach(act, product_done, b - 1)
                reach(act, counts_kept[par], i * 16 if par else i * 16 + 16)
                for p in range(PAIRS):
                    act.wait_ge(pair_built, b * PAIRS + p + 1)
                    nc.scalar.copy(counts[par][:, :, 2 * WN * p:2 * WN * (p + 1)],
                                   pair_ps[p % RING][:, 0:2 * KW].rearrange("p (n h) -> p h n", h=HI))\
                      .then_inc(pair_out, 1)
                act.wait_ge(pair_out, (b + 1) * PAIRS)
                act.dma_start(scratch["counts"][bass.ds(b * P, P), :],
                              counts[par][:, :, :].rearrange("p h n -> p (h n)"))\
                   .then_inc(counts_kept[par], 16)
                act.wait_ge(e_summed, (b + 1) * EK)
                reach(act, se_kept[par], i * 16 if par else i * 16 + 16)
                nc.scalar.copy(se[par][:, :], e_ps[:, 0:BN]).then_inc(se_out, 1)
                act.wait_ge(se_out, b + 1)
                act.dma_start(scratch["se"][:, bass.ds(b * BN, BN)], se[par][:, :])\
                   .then_inc(se_kept[par], 16)
                if not (isinstance(b, int) and b == 0):
                    product_out(b, par, i * 16)
            all_blocks(act, NB, step)
            product_out(NB, NB % 2, (NB - 1) // 2 * 16)
            half = (NB - 1) // 2 * 16
            for kept in (counts_kept, se_kept, sx_kept):
                act.wait_ge(kept[0], half + 16)
                act.wait_ge(kept[1], half)


def project(nc, d, fast, keep, scratch):
    zsplit, flag, zT, y, dinv, w, vec, stats = (
        keep[k] for k in ("zsplit", "flag", "zT", "y", "dinv", "w1", "vec", "stats"))
    HI, NB = d.HI, d.NB
    PRODUCTS = 2 * HI
    name = "fast1" if fast else "any1"
    with ExitStack() as ctx:
        sb = lambda n, shape, dt: ctx.enter_context(nc.sbuf_tensor(f"{name}_{n}", shape, dt))
        ps = lambda n: ctx.enter_context(nc.psum_tensor(f"{name}_{n}", [P, 512], F32))
        sem = lambda n: ctx.enter_context(nc.semaphore(f"{name}_{n}"))
        if fast:
            counts = [sb(f"counts{i}", [P, HI, BN], BF16) for i in range(2)]
        else:
            sums = [sb(f"sums{i}", [P, BN], F32) for i in range(2)]
        s1 = [sb(f"s1_{i}", [P, BN], F32) for i in range(2)]
        z_ps = [ps(f"z{i}") for i in range(2)]
        y_ps = [ps(f"y{i}") for i in range(2)]
        block_in = [sem(f"block_in{i}") for i in range(2)]
        multiplied, s1_ready, projected = sem("multiplied"), sem("s1_ready"), sem("projected")
        scaled, biased, counted, sp_passed = sem("scaled"), sem("biased"), sem("counted"), sem("sp_passed")
        block = ctx.enter_context(nc.Block())
        ours = lambda loaded: (loaded > 0) if fast else (loaded < 1)
        cols = lambda b: bass.ds(b * BN, BN)

        @block.sync
        def _(sp):
            on = sp.value_load(flag[0:1, 0:1], min_val=0, max_val=1)
            with sp.If(ours(on)):
                def step(b, par, i):
                    if fast:
                        wait_alone(sp, multiplied, b - 1, sp_passed)
                        sp.dma_start(counts[par][:, :, :].rearrange("p h n -> p (h n)"),
                                     scratch["counts"][bass.ds(b * P, P), :]).then_inc(block_in[par], 16)
                    else:
                        wait_alone(sp, s1_ready, b - 1, sp_passed)
                        sp.dma_start(sums[par][:, :], scratch["s1"][:, cols(b)]).then_inc(block_in[par], 16)
                all_blocks(sp, NB, step)

        @block.tensor
        def _(pe):
            on = pe.value_load(flag[0:1, 0:1], min_val=0, max_val=1)
            with pe.If(ours(on)):
                def weights(b, par):
                    pe.wait_ge(s1_ready, b)
                    reach(pe, scaled, b - 2)
                    nc.tensor.matmul(y_ps[1 - par][:, 0:BN], w[:, :], s1[1 - par][:, :], start=True, stop=True)\
                      .then_inc(projected, 1)

                def step(b, par, i):
                    if fast:
                        pe.wait_ge(block_in[par], i * 16 + (16 if par else 32))
                        reach(pe, s1_ready, b - 1)
                        for q in range(PRODUCTS):
                            last = nc.tensor.matmul(z_ps[par][:, 0:BN], zsplit[:, q // 2, q % 2, :],
                                                    counts[par][:, q // 2, :],
                                                    start=(q == 0), stop=(q == PRODUCTS - 1))
                        last.then_inc(multiplied, 1)
                    if not (isinstance(b, int) and b == 0):
                        weights(b, par)
                all_blocks(pe, NB, step)
                weights(NB, NB % 2)

        @block.vector
        def _(dve):
            on = dve.value_load(flag[0:1, 0:1], min_val=0, max_val=1)
            with dve.If(ours(on)):
                def finish(b, par):
                    dve.wait_ge(projected, b)
                    nc.vector.tensor_tensor(y[:, cols(b - 1)], y_ps[1 - par][:, 0:BN], dinv[:, cols(b - 1)],
                                            ALU.mult).then_inc(scaled, 1)
                    dve.wait_ge(biased, b)
                    nc.vector.bn_stats(stats[:, bass.ds((b - 1) * 6, 6)], y[:, cols(b - 1)]).then_inc(counted, 1)

                def step(b, par, i):
                    reach(dve, projected, b - 1)
                    if fast:
                        dve.wait_ge(multiplied, b + 1)
                        nc.vector.scalar_tensor_tensor(out=s1[par][:, :], in0=z_ps[par][:, 0:BN],
                                                       scalar=1.0 / Z_SCALE, in1=zT[:, cols(b)],
                                                       op0=ALU.mult, op1=ALU.add).then_inc(s1_ready, 1)
                    else:
                        dve.wait_ge(block_in[par], i * 16 + (16 if par else 32))
                        nc.vector.tensor_tensor(s1[par][:, :], sums[par][:, :], zT[:, cols(b)], ALU.add)\
                          .then_inc(s1_ready, 1)
                    if not (isinstance(b, int) and b == 0):
                        finish(b, par)
                all_blocks(dve, NB, step)
                finish(NB, NB % 2)
                dve.wait_ge(counted, NB)

        @block.scalar
        def _(act):
            on = act.value_load(flag[0:1, 0:1], min_val=0, max_val=1)
            with act.If(ours(on)):
                def turn(b):
                    act.wait_ge(scaled, b + 1)
                    nc.scalar.activation(y[:, cols(b)], y[:, cols(b)], ACT.Identity, bias=vec[:, 0:1])\
                      .then_inc(biased, 1)
                all_turns(act, NB, turn)


def aggregate_any(nc, d, name, table, ea, src, dst, keep, sum_out, esum_out, deg_out):
    flag = keep["flag"]
    N, E = d.N, d.E
    GR = -(-N // GN)
    NT = E // GE
    kinds = 3 if ea is not None else 1
    with ExitStack() as ctx:
        sb = lambda n, shape, dt: ctx.enter_context(nc.sbuf_tensor(f"{name}_{n}", shape, dt))
        sem = lambda n: ctx.enter_context(nc.semaphore(f"{name}_{n}"))
        acc = [sb(f"acc{k}", [P, GR * GN], F32) for k in range(kinds)]
        data = [sb(f"data{k}", [P, F], F32) for k in range(kinds)]
        ones = data[2] if kinds == 3 else None
        src_i, dst_i, dst_f = sb("src_i", [P, 1], I32), sb("dst_i", [P, 1], I32), sb("dst_f", [P, 1], F32)
        node_i, node = sb("node_i", [P, GR * GN], I32), sb("node", [P, GR * GN], F32)
        hot = [sb(f"hot{i}", [P, GN], F32) for i in range(2)]
        sums = [[ctx.enter_context(nc.psum_tensor(f"{name}_sum{k}_{i}", [P, 512], F32)) for i in range(2)]
                for k in range(kinds)]
        idx_in, row_in, ea_in, ready = sem("idx_in"), sem("row_in"), sem("ea_in"), sem("ready")
        made, cast, summed, added, stored = sem("made"), sem("cast"), sem("summed"), sem("added"), sem("stored")
        nodes_made, pool_passed, sp_passed = sem("nodes_made"), sem("pool_passed"), sem("sp_passed")
        block = ctx.enter_context(nc.Block())

        @block.sync
        def _(sp):
            fast = sp.value_load(flag[0:1, 0:1], min_val=0, max_val=1)
            with sp.If(fast < 1):
                def turn(t):
                    wait_alone(sp, summed, t * GR, sp_passed)
                    wait_alone(sp, made, t * GR, sp_passed)
                    sp.dma_start(src_i[0:GE, :], src[bass.ds(t * GE, GE)].rearrange("(p o) -> p o", o=1))\
                      .then_inc(idx_in, 16)
                    sp.dma_start(dst_i[0:GE, :], dst[bass.ds(t * GE, GE)].rearrange("(p o) -> p o", o=1))\
                      .then_inc(idx_in, 16)
                    if kinds == 3:
                        sp.dma_start(data[1][0:GE, :], ea[bass.ds(t * GE, GE), :]).then_inc(ea_in, 16)
                    sp.wait_ge(idx_in, t * 32 + 32)
                    wait_alone(sp, row_in, t * 16 + 16, sp_passed)
                all_turns(sp, NT, turn)
                sp.wait_ge(added, NT * GR)
                sp.dma_start(sum_out[:, 0:N], acc[0][:, 0:N]).then_inc(stored, 16)
                if kinds == 3:
                    sp.dma_start(esum_out[:, 0:N], acc[1][:, 0:N]).then_inc(stored, 16)
                    sp.dma_start(deg_out[0:N].rearrange("(o n) -> o n", o=1), acc[2][0:1, 0:N])\
                      .then_inc(stored, 16)
                sp.wait_ge(stored, 16 * kinds)

        @block.gpsimd
        def _(pool):
            fast = pool.value_load(flag[0:1, 0:1], min_val=0, max_val=1)
            with pool.If(fast < 1):
                nc.gpsimd.iota(node_i[:, :], pattern=[[1, GR * GN]], base=0, channel_multiplier=0)\
                  .then_inc(nodes_made, 1)
                def turn(t):
                    wait_alone(pool, idx_in, t * 32 + 32, pool_passed)
                    nc.gpsimd.indirect_dma_start(
                        out=data[0][0:GE, :], out_offset=None, in_=table,
                        in_offset=bass.IndirectOffsetOnAxis(ap=src_i[0:GE, :], axis=0)).then_inc(row_in, 16)
                all_turns(pool, NT, turn)

        @block.vector
        def _(dve):
            fast = dve.value_load(flag[0:1, 0:1], min_val=0, max_val=1)
            with dve.If(fast < 1):
                for a in acc:
                    nc.vector.memset(a[:, :], 0.0).then_inc(ready, 1)
                if kinds == 3:
                    nc.vector.memset(ones[:, :], 1.0).then_inc(ready, 1)
                else:
                    dve.sem_inc(ready, 1)
                dve.wait_ge(nodes_made, 1)
                nc.vector.tensor_copy(node[:, :], node_i[:, :]).then_inc(ready, 1)
                dve.wait_ge(ready, kinds + 2)
                def turn(t):
                    dve.wait_ge(idx_in, t * 32 + 32)
                    nc.vector.tensor_copy(dst_f[0:GE, :], dst_i[0:GE, :]).then_inc(cast, 1)
                    dve.wait_ge(cast, t + 1)
                    for g in range(GR + 1):
                        if g < GR:
                            if g >= 2:
                                reach(dve, summed, t * GR + (g - 1))
                            nc.vector.tensor_scalar(hot[g % 2][0:GE, :], node[0:GE, g * GN:(g + 1) * GN],
                                                    dst_f[0:GE, 0:1], None, ALU.is_equal).then_inc(made, 1)
                        if g >= 1:
                            h = g - 1
                            dve.wait_ge(summed, t * GR + h + 1)
                            for k in range(kinds):
                                at = acc[k][:, h * GN:(h + 1) * GN]
                                last = nc.vector.tensor_tensor(at, at, sums[k][h % 2][:, :], ALU.add)
                            last.then_inc(added, 1)
                    dve.wait_ge(added, t * GR + GR)
                all_turns(dve, NT, turn)

        @block.tensor
        def _(pe):
            fast = pe.value_load(flag[0:1, 0:1], min_val=0, max_val=1)
            with pe.If(fast < 1):
                pe.wait_ge(ready, kinds + 2)
                def turn(t):
                    pe.wait_ge(row_in, t * 16 + 16)
                    if kinds == 3:
                        pe.wait_ge(ea_in, t * 16 + 16)
                    reach(pe, added, t * GR)
                    for g in range(GR):
                        pe.wait_ge(made, t * GR + g + 1)
                        if g >= 2:
                            reach(pe, added, t * GR + (g - 1))
                        for k in range(kinds):
                            last = nc.tensor.matmul(sums[k][g % 2][:, :], data[k][0:GE, :],
                                                    hot[g % 2][0:GE, :], start=True, stop=True)
                        last.then_inc(summed, 1)
                all_turns(pe, NT, turn)


def norm_rows(nc, step, x, out, small, ready_for_root, root_taken):
    stats, mv, std = small
    C = mv.shape[1]
    for k in range(C):
        last = nc.vector.bn_stats(stats[:, k, :], x[:, k, :])
    step(last, alone=True)
    for k in range(C):
        last = nc.vector.bn_aggr(mv[:, k, :], stats[:, k, :])
    step(last)
    step(nc.vector.tensor_scalar(std[:, :], mv[:, :, 1], LN_EPS, None, ALU.add))
    ready_for_root()
    root_taken()
    step(nc.vector.reciprocal(std[:, :], std[:, :]))
    for k in range(C):
        last = nc.vector.tensor_scalar(out[:, k, :], x[:, k, :], mv[:, k, 0:1], std[:, k:k + 1],
                                       ALU.subtract, ALU.mult)
    step(last)


NORM_STEPS = 5


class TurnSteps:

    def __init__(self, engine, sem, turn, per_turn, passed):
        self.engine, self.sem, self.turn, self.per, self.n = engine, sem, turn, per_turn, 0
        self.passed = passed

    def __call__(self, ins, alone=False):
        self.n += 1
        assert self.n <= self.per
        ins.then_inc(self.sem, 1)
        if alone:
            wait_alone(self.engine, self.sem, self.turn * self.per + self.n, self.passed)
        else:
            self.engine.wait_ge(self.sem, self.turn * self.per + self.n)


def halves(C):
    return [(h, 4 * h, min(4, C - 4 * h)) for h in range(2) if C > 4 * h]


def update_first(nc, d, W, bW, We, bWe, W1, vectors1, keep, scratch):
    xrows, zsplit, ident, zT = (keep[k] for k in ("xrows", "zsplit", "ident", "zT"))
    HI, C, NCH, NP, N = d.HI, d.CH, d.NC, d.NP, d.N
    HS = halves(C)
    with ExitStack() as ctx:
        sb = lambda n, shape, dt: ctx.enter_context(nc.sbuf_tensor(f"u0_{n}", shape, dt))
        sem = lambda n: ctx.enter_context(nc.semaphore(f"u0_{n}"))
        wi, wj, we = sb("wi", [P, F], F32), sb("wj", [P, F], F32), sb("we", [P, F], F32)
        bi, bj, bje, be = (sb(n, [1, F], F32) for n in ("bi", "bj", "bje", "be"))
        ones, zero = sb("ones", [1, P], F32), sb("zero", [P, P], F32)
        deg, rdeg, dinv = sb("deg", [P, HI], F32), sb("rdeg", [P, HI], F32), sb("dinv", [P, HI], F32)
        rdc = sb("rdc", [P, C], F32)
        sxc, sec = ([sb(f"{n}{i}", [P, C, P], F32) for i in range(2)] for n in ("sxc", "sec"))
        degrow = [sb(f"degrow{i}", [1, C, P], F32) for i in range(2)]
        xc, xT = [sb(f"xc{i}", [P, C, F], F32) for i in range(2)], sb("xT", [P, C, P], F32)
        msg, own = sb("msg", [P, C, F], F32), sb("own", [P, C, F], F32)
        v, x1, z = (sb(n, [P, C, F], F32) for n in ("v", "x1", "z"))
        stats, mv, var = sb("stats", [P, C, 6], F32), sb("mv", [P, C, 2], F32), sb("std", [P, C], F32)
        t_ps, i_ps, j_ps, z_ps = (
            [ctx.enter_context(nc.psum_tensor(f"u0_{n}{k}", [P, 4, P], F32)) for k in range(2)]
            for n in ("t", "i", "j", "z"))
        w_in, deg_in, ready, cols_done = sem("w_in"), sem("deg_in"), sem("ready"), sem("cols_done")
        pads, dinv_out, root, pre = sem("pads_out"), sem("dinv_out"), sem("deg_root"), sem("pre_step")
        chunk_in = [sem(f"chunk_in{i}") for i in range(2)]
        x_copied, turned, turned_out, rdc_ready = sem("x_copied"), sem("turned"), sem("turned_out"), sem("rdc_ready")
        multiplied, msg_out, own_step, summed = sem("multiplied"), sem("msg_out"), sem("own_step"), sem("summed")
        norm_step, var_ready, std_ready = sem("norm_step"), sem("var_ready"), sem("std_ready")
        z_ready, high_ready, low_ready = sem("z_ready"), sem("high_ready"), sem("low_ready")
        z_turned, z_out, z_kept, sp_passed = sem("z_turned"), sem("z_turned_out"), sem("z_kept"), sem("sp_passed")
        dinv_in, layer1_in = sem("dinv_in"), sem("layer1_in")
        dve_passed, pool_passed, x1_ready, x1_kept = sem("dve_passed"), sem("pool_passed"), sem("x1_ready"), sem("x1_kept")
        block = ctx.enter_context(nc.Block())
        bank = lambda pss, k: pss[k // 4][:, k % 4, :]
        chunk = lambda c: bass.ds(c * C, C)
        later = lambda c: not (isinstance(c, int) and c == 0)

        @block.sync
        def _(sp):
            row = lambda a: a.rearrange("(o n) -> o n", o=1)
            sp.dma_start(deg[:, :], scratch["deg"].rearrange("(h p) -> p h", p=P),
                         allow_slow_non_contiguous=True).then_inc(deg_in, 16)
            for out, in_ in ((wi[:, :], W[:, 0:F]), (wj[:, :], W[:, F:2 * F]), (we[:, :], We),
                             (bi[:, :], row(bW[0:F])), (bj[:, :], row(bW[F:2 * F])), (be[:, :], row(bWe))):
                sp.dma_start(out, in_).then_inc(w_in, 16)
            sp.dma_start(keep["w1"][:, :], W1).then_inc(layer1_in, 16)
            for k, a in enumerate(vectors1):
                sp.dma_start(keep["vec"][:, k:k + 1], a.rearrange("(p o) -> p o", o=1)).then_inc(layer1_in, 16)
            sp.wait_ge(ready, 1)
            sp.dma_start(scratch["sx"][:, N:NP], zero[:, 0:NP - N]).then_inc(pads, 16)
            sp.dma_start(scratch["se"][:, N:NP], zero[:, 0:NP - N]).then_inc(pads, 16)
            sp.wait_ge(pads, 32)

            def keep_z(c):
                wait_alone(sp, z_ready, c, sp_passed)
                sp.dma_start(scratch["z"][bass.ds((c - 1) * (C * P), C * P), :].rearrange("(c p) f -> p c f", p=P),
                             z[:, :, :]).then_inc(z_kept, 16)

            def step(c, par, i):
                wait_alone(sp, multiplied, c - 1, sp_passed)
                cols = bass.ds(c * (C * P), C * P)
                flat = lambda a: a[:, :, :].rearrange("p c n -> p (c n)")
                sp.dma_start(flat(sxc[par]), scratch["sx"][:, cols]).then_inc(chunk_in[par], 16)
                sp.dma_start(flat(sec[par]), scratch["se"][:, cols]).then_inc(chunk_in[par], 16)
                sp.dma_start(flat(degrow[par]), row(scratch["deg"][cols])).then_inc(chunk_in[par], 16)
                if later(c):
                    keep_z(c)
            all_blocks(sp, NCH, step)
            keep_z(NCH)
            sp.wait_ge(z_kept, NCH * 16)
            sp.wait_ge(dinv_in, 16)
            sp.wait_ge(layer1_in, 64)

        @block.scalar
        def _(act):
            act.wait_ge(root, 1)
            nc.scalar.activation(dinv[:, :], dinv[:, :], ACT.Sqrt).then_inc(root, 1)
            act.wait_ge(cols_done, 1)
            act.dma_start(scratch["dinv"].rearrange("(h p) -> p h", p=P), dinv[:, :],
                          allow_slow_non_contiguous=True).then_inc(dinv_out, 16)
            act.wait_ge(dinv_out, 16)
            act.dma_start(keep["dinv"][:, :], scratch["dinv"].rearrange("(o n) -> o n", o=1).to_broadcast([P, NP]))\
               .then_inc(dinv_in, 16)

            def norm_part(c):
                act.wait_ge(var_ready, c)
                nc.scalar.activation(var[:, :], var[:, :], ACT.Sqrt).then_inc(std_ready, 1)
                act.wait_ge(z_ready, c)
                nc.scalar.activation(zsplit[:, chunk(c - 1), 0, :], z[:, :, :], ACT.Copy, scale=Z_SCALE)\
                  .then_inc(high_ready, 1)

            def transpose_out(c):
                act.wait_ge(z_turned, c)
                for h, k, n in HS:
                    last = nc.scalar.copy(zT[:, bass.ds((c - 1) * (C * P) + k * P, n * P)]
                                          .rearrange("p (c n) -> p c n", n=P), z_ps[h][:, 0:n, :])
                last.then_inc(z_out, 1)

            def step(c, par, i):
                nc.scalar.copy(xc[par][:, :, :], xrows[:, chunk(c), :]).then_inc(x_copied, 1)
                reach(act, msg_out, c)
                nc.scalar.copy(rdc[:, :], rdeg[:, chunk(c)]).then_inc(rdc_ready, 1)
                act.wait_ge(turned, c + 1)
                reach(act, multiplied, c)
                for h, k, n in HS:
                    last = nc.scalar.copy(xT[:, k:k + n, :], t_ps[h][:, 0:n, :])
                last.then_inc(turned_out, 1)
                if later(c):
                    norm_part(c)
                act.wait_ge(multiplied, c + 1)
                act.wait_ge(rdc_ready, c + 1)
                reach(act, summed, c)
                for k in range(C):
                    last = nc.scalar.activation(msg[:, k, :], bank(j_ps, k), ACT.Copy, scale=rdc[:, k:k + 1])
                last.then_inc(msg_out, 1)
                if later(c):
                    transpose_out(c)
            all_blocks(act, NCH, step)
            norm_part(NCH)
            transpose_out(NCH)

        @block.gpsimd
        def _(pool):
            def turn(c):
                wait_alone(pool, x1_ready, c + 1, pool_passed)
                nc.gpsimd.tensor_copy(xrows[:, chunk(c), :], x1[:, :, :]).then_inc(x1_kept, 1)
            all_turns(pool, NCH, turn)

        @block.vector
        def _(dve):
            vv = nc.vector
            pstep = Steps(dve, pre)
            pstep(vv.memset(zero[:, :], 0.0))
            dve.sem_inc(ready, 1)
            vv.memset(ones[:, :], 1.0).then_inc(ready, 1)
            pstep(vv.memset(keep["y"][:, N:NP], 0.0))
            dve.wait_ge(deg_in, 16)
            pstep(vv.tensor_scalar(dinv[:, :], deg[:, :], 1.0, None, ALU.add))
            dve.sem_inc(root, 1)
            pstep(vv.tensor_scalar(rdeg[:, :], deg[:, :], 1e-6, None, ALU.add))
            pstep(vv.reciprocal(rdeg[:, :], rdeg[:, :]))
            dve.wait_ge(root, 2)
            pstep(vv.reciprocal(dinv[:, :], dinv[:, :]))
            dve.sem_inc(cols_done, 1)
            dve.wait_ge(w_in, 96)
            pstep(vv.tensor_tensor(bje[:, :], bj[:, :], be[:, :], ALU.add))
            dve.sem_inc(ready, 1)

            def normalise(c):
                step = TurnSteps(dve, norm_step, c - 1, NORM_STEPS, dve_passed)
                reach(dve, x1_kept, c - 1)
                norm_rows(nc, step, v, x1, (stats, mv, var),
                          lambda: dve.sem_inc(var_ready, 1), lambda: dve.wait_ge(std_ready, c))
                dve.sem_inc(x1_ready, 1)
                reach(dve, z_kept, (c - 1) * 16)
                reach(dve, z_turned, c - 1)
                vv.tensor_tensor(z[:, :, :], x1[:, :, :], dinv[:, chunk(c - 1)].unsqueeze(2).to_broadcast([P, C, F]),
                                 ALU.mult).then_inc(z_ready, 1)
                dve.wait_ge(high_ready, c)
                vv.scalar_tensor_tensor(out=zsplit[:, chunk(c - 1), 1, :], in0=z[:, :, :], scalar=Z_SCALE,
                                        in1=zsplit[:, chunk(c - 1), 0, :], op0=ALU.mult, op1=ALU.subtract)\
                  .then_inc(low_ready, 1)
                dve.wait_ge(low_ready, c)

            def step(c, par, i):
                if later(c):
                    normalise(c)
                dve.wait_ge(multiplied, c + 1)
                dve.wait_ge(x_copied, c + 1)
                for h, k, n in HS:
                    last = vv.tensor_tensor(own[:, k:k + n, :], xc[par][:, k:k + n, :], i_ps[h][:, 0:n, :], ALU.add)
                last.then_inc(own_step, 1)
                dve.wait_ge(own_step, c + 1)
                dve.wait_ge(msg_out, c + 1)
                vv.tensor_tensor(v[:, :, :], own[:, :, :], msg[:, :, :], ALU.add).then_inc(summed, 1)
                wait_alone(dve, summed, c + 1, dve_passed)
            all_blocks(dve, NCH, step)
            normalise(NCH)

        @block.tensor
        def _(pe):
            pe.wait_ge(ready, 3)

            def turn_z(c):
                pe.wait_ge(z_ready, c)
                reach(pe, z_out, c - 1)
                for k in range(C):
                    last = nc.tensor.transpose(bank(z_ps, k), z[:, k, :], ident[:, :])
                last.then_inc(z_turned, 1)

            def step(c, par, i):
                pe.wait_ge(x_copied, c + 1)
                reach(pe, turned_out, c)
                for k in range(C):
                    last = nc.tensor.transpose(bank(t_ps, k), xc[par][:, k, :], ident[:, :])
                last.then_inc(turned, 1)
                pe.wait_ge(chunk_in[par], i * 48 + (48 if par else 96))
                reach(pe, msg_out, c)
                reach(pe, own_step, c)
                for k in range(C):
                    nc.tensor.matmul(bank(j_ps, k), sxc[par][:, k, :], wj[:, :], start=True, stop=False)
                    nc.tensor.matmul(bank(j_ps, k), sec[par][:, k, :], we[:, :], start=False, stop=False)
                    nc.tensor.matmul(bank(j_ps, k), degrow[par][0:1, k, :], bje[0:1, :], start=False, stop=True)
                pe.wait_ge(turned_out, c + 1)
                for k in range(C):
                    nc.tensor.matmul(bank(i_ps, k), xT[:, k, :], wi[:, :], start=True, stop=False)
                    last = nc.tensor.matmul(bank(i_ps, k), ones[0:1, :], bi[0:1, :], start=False, stop=True)
                last.then_inc(multiplied, 1)
                if later(c):
                    turn_z(c)
            all_blocks(pe, NCH, step)
            turn_z(NCH)


def update_second(nc, d, out, keep, scratch):
    xrows, ident, y, vec, stats = (keep[k] for k in ("xrows", "ident", "y", "vec", "stats"))
    HI, C, NCH, NP, N = d.HI, d.CH, d.NC, d.NP, d.N
    HS = halves(C)
    NS = NORM_STEPS + 1
    with ExitStack() as ctx:
        sb = lambda n, shape, dt: ctx.enter_context(nc.sbuf_tensor(f"u1_{n}", shape, dt))
        sem = lambda n: ctx.enter_context(nc.semaphore(f"u1_{n}"))
        mv, co = sb("mv", [P, 2], F32), sb("co", [P, 4], F32)
        t = [sb(f"t{i}", [P, C, P], F32) for i in range(2)]
        r = [sb(f"r{i}", [P, C, P], F32) for i in range(2)]
        xo = [sb(f"xo{i}", [P, C, F], F32) for i in range(2)]
        v = sb("v", [P, C, F], F32)
        lstats, lmv, var = sb("lstats", [P, C, 6], F32), sb("lmv", [P, C, 2], F32), sb("std", [P, C], F32)
        r_ps = [[ctx.enter_context(nc.psum_tensor(f"u1_r{i}{k}", [P, 4, P], F32)) for k in range(2)] for i in range(2)]
        pre, root, coeff = sem("pre_step"), sem("batch_root"), sem("coefficients")
        t_ready, r_ready, turned, norm_step = sem("t_ready"), sem("r_ready"), sem("turned"), sem("norm_step")
        var_ready, std_ready, xo_ready, sp_passed = sem("var_ready"), sem("std_ready"), sem("xo_ready"), sem("sp_passed")
        kept, dve_passed = [sem(f"kept{i}") for i in range(2)], sem("dve_passed")
        block = ctx.enter_context(nc.Block())
        chunk = lambda c: bass.ds(c * C, C)
        later = lambda c: not (isinstance(c, int) and c == 0)

        @block.sync
        def _(sp):
            def step(c, par, i):
                if later(c):
                    wait_alone(sp, xo_ready, c, sp_passed)
                    sp.dma_start(out[bass.ds((c - 1) * (C * P), C * P), :].rearrange("(c p) f -> p c f", p=P),
                                 xo[1 - par][:, :, :]).then_inc(kept[1 - par], 16)
            all_blocks(sp, NCH, step)
            sp.wait_ge(xo_ready, NCH)
            base = (NCH - 1) * C * P
            sp.dma_start(out[base:base + (C - 1) * P, :].rearrange("(c p) f -> p c f", p=P),
                         xo[(NCH - 1) % 2][:, 0:C - 1, :]).then_inc(kept[0], 16)
            sp.dma_start(out[(HI - 1) * P:N, :], xo[(NCH - 1) % 2][0:d.REM, C - 1, :]).then_inc(kept[0], 16)
            sp.wait_ge(kept[0], (NCH // 2 + 2) * 16)
            sp.wait_ge(kept[1], NCH // 2 * 16)

        @block.scalar
        def _(act):
            act.wait_ge(root, 1)
            nc.scalar.activation(co[:, 0:1], co[:, 0:1], ACT.Sqrt).then_inc(root, 1)
            act.wait_ge(coeff, 1)

            def take_root(c):
                act.wait_ge(var_ready, c)
                nc.scalar.activation(var[:, :], var[:, :], ACT.Sqrt).then_inc(std_ready, 1)

            def step(c, par, i):
                reach(act, r_ready, c - 1)
                nc.scalar.activation(t[par][:, :, :].rearrange("p c n -> p (c n)"),
                                     y[:, bass.ds(c * (C * P), C * P)], ACT.Identity,
                                     bias=co[:, 2:3], scale=co[:, 1:2]).then_inc(t_ready, 1)
                if later(c):
                    take_root(c)
            all_blocks(act, NCH, step)
            take_root(NCH)

        @block.vector
        def _(dve):
            vv = nc.vector
            pstep = Steps(dve, pre)
            pstep(vv.bn_aggr(mv[:, :], stats[:, :]))
            pstep(vv.tensor_scalar(co[:, 0:1], mv[:, 1:2], LN_EPS, None, ALU.add))
            dve.sem_inc(root, 1)
            dve.wait_ge(root, 2)
            pstep(vv.reciprocal(co[:, 1:2], co[:, 0:1]))
            pstep(vv.tensor_tensor(co[:, 1:2], co[:, 1:2], vec[:, 1:2], ALU.mult))
            pstep(vv.tensor_tensor(co[:, 3:4], mv[:, 0:1], co[:, 1:2], ALU.mult))
            pstep(vv.tensor_tensor(co[:, 2:3], vec[:, 2:3], co[:, 3:4], ALU.subtract))
            dve.sem_inc(coeff, 1)

            def normalise(c, par, i):
                step = TurnSteps(dve, norm_step, c - 1, NS, dve_passed)
                dve.wait_ge(turned, c)
                for h, k, n in HS:
                    last = vv.tensor_tensor(v[:, k:k + n, :], xrows[:, bass.ds((c - 1) * C + k, n), :],
                                            r_ps[1 - par][h][:, 0:n, :], ALU.add)
                step(last)
                reach(dve, kept[1 - par], i * 16)
                norm_rows(nc, step, v, xo[1 - par], (lstats, lmv, var),
                          lambda: dve.sem_inc(var_ready, 1), lambda: dve.wait_ge(std_ready, c))
                dve.sem_inc(xo_ready, 1)

            def step(c, par, i):
                dve.wait_ge(t_ready, c + 1)
                reach(dve, turned, c - 1)
                vv.scalar_tensor_tensor(out=r[par][:, :, :], in0=t[par][:, :, :], scalar=0.01,
                                        in1=t[par][:, :, :], op0=ALU.mult, op1=ALU.max).then_inc(r_ready, 1)
                if later(c):
                    normalise(c, par, i)
            all_blocks(dve, NCH, step)
            normalise(NCH, NCH % 2, NCH // 2)

        @block.tensor
        def _(pe):
            def step(c, par, i):
                pe.wait_ge(r_ready, c + 1)
                reach(pe, norm_step, (c - 2) * NS + 1)
                for k in range(C):
                    last = nc.tensor.transpose(r_ps[par][k // 4][:, k % 4, :], r[par][:, k, :], ident[:, :])
                last.then_inc(turned, 1)
            all_blocks(pe, NCH, step)


def build(nc, x, src, dst, ea, W0, b0, We, be, W1, b1, gamma, beta, out):
    d = Dims(x.shape[0], src.shape[0])
    NE = d.NB * EK
    dram = lambda name, shape, dt: nc.dram_tensor(name, shape, dt)
    scratch = {
        "starts": dram("starts", [NE, 1], I32)[:, :],
        "deg": dram("deg_rows", [d.NP], F32)[:],
        "dinv": dram("dinv_rows", [d.NP], F32)[:],
        "sx": dram("sums_x", [P, d.NP], F32)[:, :],
        "se": dram("sums_e", [P, d.NP], F32)[:, :],
        "s1": dram("sums_z", [P, d.NP], F32)[:, :],
        "z": dram("z_rows", [d.NP, F], F32)[:, :],
        "counts": dram("counts_kept", [d.NB * P, d.HI * BN], BF16)[:, :],
    }
    with ExitStack() as ctx:
        sb = lambda name, shape, dt: ctx.enter_context(nc.sbuf_tensor(name, shape, dt))
        keep = {
            "xrows": sb("xrows", [P, d.HI, F], F32),
            "ident": sb("ident", [P, P], F32),
            "flag": sb("flag", [1, 1], I32),
        }
        with ExitStack() as tables:
            tb = lambda name, shape, dt: tables.enter_context(nc.sbuf_tensor(name, shape, dt))
            keep.update({
                "xsplit": tb("xsplit", [P, d.HI, 2, F], F16),
                "total": tb("total", [P, 4], F32), "dl": tb("dl", [P, d.G, WE], BF16),
                "xscale": tb("xscale", [P, 4], F32),
                "iota": tb("iota", [P, 256], BF16), "iota_e": tb("iota_e", [P, EW], F32),
                "key_t": tb("key_t", [P, d.NW * TILES], F32), "lo_t": tb("lo_t", [P, d.NW * TILES], F32),
                "ekey_t": tb("ekey_t", [P, NE, EJ], F32), "startrow": tb("startrow", [1, NE], I32),
            })
            prepare(nc, d, x, src, dst, keep, scratch)
            aggregate_fast(nc, d, ea, keep, scratch)
        aggregate_any(nc, d, "any0", x, ea, src, dst, keep, scratch["sx"], scratch["se"], scratch["deg"])
        keep.update({
            "zsplit": sb("zsplit", [P, d.HI, 2, F], F16),
            "zT": sb("zT", [P, d.NP], F32),
            "y": sb("y", [P, d.NP], F32), "dinv": sb("dinv", [P, d.NP], F32),
            "w1": sb("w1", [P, F], F32), "vec": sb("vec", [P, 3], F32),
            "stats": sb("stats", [P, 6 * d.NB], F32),
        })
        update_first(nc, d, W0, b0, We, be, W1, (b1, gamma, beta), keep, scratch)
        aggregate_any(nc, d, "any1sum", scratch["z"], None, src, dst, keep, scratch["s1"], None, None)
        project(nc, d, True, keep, scratch)
        project(nc, d, False, keep, scratch)
        update_second(nc, d, out, keep, scratch)


_INS = ["x", "src", "dst", "edge_attr_128", "L0_gnn_W", "L0_gnn_b_W", "L0_gnn_W_e", "L0_gnn_b_We",
        "L1_gnn_W", "L1_gnn_b", "L1_gnn_gamma", "L1_gnn_beta"]


def kernel(**inputs):
    import numpy as np
    import concourse.bacc as bacc
    from concourse.bass_utils import run_bass_kernel_spmd

    nc = bacc.Bacc("TRN2", target_bir_lowering=False, num_devices=1)
    arrays, args = {}, []
    for name in _INS:
        a = np.ascontiguousarray(inputs[name])
        arrays[f"in_{name}"] = a
        args.append(nc.dram_tensor(f"in_{name}", a.shape, mybir.dt.from_np(a.dtype), kind="ExternalInput").ap())
    out = nc.dram_tensor("out_rows", inputs["x"].shape, F32, kind="ExternalOutput").ap()
    build(nc, *args, out)
    result = run_bass_kernel_spmd(nc, [arrays], core_ids=[0])
    return result.results[0]["out_rows"]
```
